# Optimizing a Trainium2 kernel written in Bass

```python
import numpy as np
import jax
import jax.numpy as jnp

def _softmax(x, axis=-1):
    return jax.nn.softmax(x, axis=axis)
def _gelu(x):
    return jax.nn.gelu(x, approximate=True)
def _silu(x):
    return jax.nn.silu(x)
def _sigmoid(x):
    return jax.nn.sigmoid(x)
def _layernorm(x, axis=-1, eps=1e-5):
    m = jnp.mean(x, axis=axis, keepdims=True)
    v = jnp.var(x, axis=axis, keepdims=True)
    return (x - m) / jnp.sqrt(v + eps)
def _scatter_add(tgt, idx, src, axis=0):
    return tgt.at[idx].add(src)
def _segment_sum(src, seg, n):
    return jax.ops.segment_sum(src, seg, n)

kernel_name = 'mk_conv_preact_d2_conv_nchw64_a99eca'

def setup_inputs(seed: int = 0):
    np.random.seed(seed)
    _w = jnp.asarray
    def _rec_inputs():
        import jax
        import jax.numpy as jnp
        _gk = jax.random.key(seed)
        x = 7.22e-05 + 1 * jax.random.normal(jax.random.fold_in(_gk, 1), (8, 64, 128, 128), jnp.float32)
        return x
    x = _rec_inputs()
    def _L0_conv_setup():
        import jax, jax.numpy as jnp
        import numpy as np
        ATT = 16
        SK = 3
        LK = 13
        LEVELS = 4
        B, C, H, W = (8, 64, 128, 128)
        OUT = 64

        def _conv(x, w, b=None, pad=0, dil=1):
            y = jax.lax.conv_general_dilated(x, w, (1, 1), [(pad, pad), (pad, pad)], rhs_dilation=(dil, dil), dimension_numbers=('NCHW', 'OIHW', 'NCHW'))
            return y if b is None else y + b[None, :, None, None]

        def _conv1x1(x, w, b):
            return jnp.einsum('oc,bchw->bohw', w, x) + b[None, :, None, None]

        def _conv_att2(x, kg_w1, kg_b1, kg_w2, kg_b2, lk_filter, fus_w, fus_b):
            b = x.shape[0]
            f_att, f_idt = (x[:, :ATT], x[:, ATT:])
            pooled = f_att.mean(axis=(2, 3))
            hdn = jax.nn.gelu(pooled @ kg_w1.T + kg_b1, approximate=False)
            ker = (hdn @ kg_w2.T + kg_b2).reshape(b, ATT, 1, SK, SK)

            def dyn(xi, ki):
                return jax.lax.conv_general_dilated(xi[None], ki, (1, 1), [(SK // 2, SK // 2)] * 2, dimension_numbers=('NCHW', 'OIHW', 'NCHW'), feature_group_count=ATT)[0]
            out_dk = jax.vmap(dyn)(f_att, ker)
            out_lk = _conv(f_att, lk_filter, pad=LK // 2)
            out = jnp.concatenate([out_lk + out_dk, f_idt], axis=1)
            return _conv1x1(out, fus_w, fus_b)

        def _msdam(x, ds_w3, ds_b3, ds_w1, ds_b1, kg_w1, kg_b1, kg_w2, kg_b2, lk_filter, fus_w, fus_b, fin_w, fin_b):
            att = lambda t: _conv_att2(t, kg_w1, kg_b1, kg_w2, kg_b2, lk_filter, fus_w, fus_b)
            feats = []
            for i in range(LEVELS):
                y = x
                if i > 0:
                    k = 2 ** i
                    bb, cc, hh, ww = y.shape
                    y = y.reshape(bb, cc, hh // k, k, ww // k, k).mean(axis=(3, 5))
                    d = 2 * (i + 1) + 1
                else:
                    d = 1
                y = jax.nn.relu(_conv(y, ds_w3[i], ds_b3[i], pad=d, dil=d))
                y = _conv1x1(y, ds_w1[i], ds_b1[i])
                feats.append(y)
            out = att(feats[0])
            for i in range(1, LEVELS):
                k = 2 ** i
                out = out + jnp.repeat(jnp.repeat(att(feats[i]), k, axis=2), k, axis=3)
            return _conv1x1(out, fin_w, fin_b)
        key = jax.random.key(seed)
        ks = jax.random.split(key, 8)

        def rn(k, shape, fan_in):
            return jax.random.normal(k, shape, jnp.float32) / np.float32(np.sqrt(fan_in))
        return {'x': jax.random.normal(ks[0], (B, C, H, W), jnp.float32), 'ds_w3': rn(ks[1], (LEVELS, C, C, 3, 3), C * 9), 'ds_b3': jnp.zeros((LEVELS, C), jnp.float32), 'ds_w1': rn(ks[2], (LEVELS, C, C), C), 'ds_b1': jnp.zeros((LEVELS, C), jnp.float32), 'kg_w1': rn(ks[3], (ATT // 2, ATT), ATT), 'kg_b1': jnp.zeros((ATT // 2,), jnp.float32), 'kg_w2': rn(ks[4], (ATT * SK * SK, ATT // 2), ATT // 2), 'kg_b2': jnp.zeros((ATT * SK * SK,), jnp.float32), 'lk_filter': rn(ks[5], (ATT, ATT, LK, LK), ATT * LK * LK), 'fus_w': rn(ks[6], (C, C), C), 'fus_b': jnp.zeros((C,), jnp.float32), 'fin_w': rn(ks[7], (OUT, C), C), 'fin_b': jnp.zeros((OUT,), jnp.float32)}
    _L0_conv_all = _L0_conv_setup()
    _L0_conv_in = {k: v for k, v in _L0_conv_all.items() if k in ('ds_w3', 'ds_b3', 'ds_w1', 'ds_b1', 'kg_w1', 'kg_b1', 'kg_w2', 'kg_b2', 'lk_filter', 'fus_w', 'fus_b', 'fin_w', 'fin_b', )}
    del _L0_conv_all

    def _L1_conv_setup():
        import jax, jax.numpy as jnp
        import numpy as np
        from jax import lax
        DN = ('NCHW', 'OIHW', 'NCHW')
        key = jax.random.key(seed)
        ks = jax.random.split(key, 7)
        B, IC, OC, H, W = (8, 64, 64, 128, 128)
        return {'x': jax.random.normal(ks[0], (B, IC, H, W), jnp.float32), 'w3': jax.random.normal(ks[1], (OC, IC, 3, 3), jnp.float32) * 0.05, 'b3': jax.random.normal(ks[2], (OC,), jnp.float32) * 0.05, 'w5': jax.random.normal(ks[3], (OC, IC, 5, 5), jnp.float32) * 0.05, 'b5': jax.random.normal(ks[4], (OC,), jnp.float32) * 0.05, 'wr': jax.random.normal(ks[5], (OC, 10, 1, 1), jnp.float32) * 0.1, 'br': jax.random.normal(ks[6], (OC,), jnp.float32) * 0.05}
    _L1_conv_all = _L1_conv_setup()
    _L1_conv_in = {k: v for k, v in _L1_conv_all.items() if k in ('w3', 'b3', 'w5', 'b5', 'wr', 'br', )}
    del _L1_conv_all

    return {
        "x": x,
        "L0_conv_ds_w3": _L0_conv_in["ds_w3"],
        "L0_conv_ds_b3": _L0_conv_in["ds_b3"],
        "L0_conv_ds_w1": _L0_conv_in["ds_w1"],
        "L0_conv_ds_b1": _L0_conv_in["ds_b1"],
        "L0_conv_kg_w1": _L0_conv_in["kg_w1"],
        "L0_conv_kg_b1": _L0_conv_in["kg_b1"],
        "L0_conv_kg_w2": _L0_conv_in["kg_w2"],
        "L0_conv_kg_b2": _L0_conv_in["kg_b2"],
        "L0_conv_lk_filter": _L0_conv_in["lk_filter"],
        "L0_conv_fus_w": _L0_conv_in["fus_w"],
        "L0_conv_fus_b": _L0_conv_in["fus_b"],
        "L0_conv_fin_w": _L0_conv_in["fin_w"],
        "L0_conv_fin_b": _L0_conv_in["fin_b"],
        "L1_conv_w3": _L1_conv_in["w3"],
        "L1_conv_b3": _L1_conv_in["b3"],
        "L1_conv_w5": _L1_conv_in["w5"],
        "L1_conv_b5": _L1_conv_in["b5"],
        "L1_conv_wr": _L1_conv_in["wr"],
        "L1_conv_br": _L1_conv_in["br"],
    }

def reference(x, L0_conv_ds_w3, L0_conv_ds_b3, L0_conv_ds_w1, L0_conv_ds_b1, L0_conv_kg_w1, L0_conv_kg_b1, L0_conv_kg_w2, L0_conv_kg_b2, L0_conv_lk_filter, L0_conv_fus_w, L0_conv_fus_b, L0_conv_fin_w, L0_conv_fin_b, L1_conv_w3, L1_conv_b3, L1_conv_w5, L1_conv_b5, L1_conv_wr, L1_conv_br):
    import jax
    import jax.numpy as jnp
    def _L0_conv_ref(x, ds_w3, ds_b3, ds_w1, ds_b1, kg_w1, kg_b1, kg_w2, kg_b2, lk_filter, fus_w, fus_b, fin_w, fin_b):
        import jax, jax.numpy as jnp
        import numpy as np
        ATT = 16
        SK = 3
        LK = 13
        LEVELS = 4
        B, C, H, W = (8, 64, 128, 128)
        OUT = 64

        def _conv(x, w, b=None, pad=0, dil=1):
            y = jax.lax.conv_general_dilated(x, w, (1, 1), [(pad, pad), (pad, pad)], rhs_dilation=(dil, dil), dimension_numbers=('NCHW', 'OIHW', 'NCHW'))
            return y if b is None else y + b[None, :, None, None]

        def _conv1x1(x, w, b):
            return jnp.einsum('oc,bchw->bohw', w, x) + b[None, :, None, None]

        def _conv_att2(x, kg_w1, kg_b1, kg_w2, kg_b2, lk_filter, fus_w, fus_b):
            b = x.shape[0]
            f_att, f_idt = (x[:, :ATT], x[:, ATT:])
            pooled = f_att.mean(axis=(2, 3))
            hdn = jax.nn.gelu(pooled @ kg_w1.T + kg_b1, approximate=False)
            ker = (hdn @ kg_w2.T + kg_b2).reshape(b, ATT, 1, SK, SK)

            def dyn(xi, ki):
                return jax.lax.conv_general_dilated(xi[None], ki, (1, 1), [(SK // 2, SK // 2)] * 2, dimension_numbers=('NCHW', 'OIHW', 'NCHW'), feature_group_count=ATT)[0]
            out_dk = jax.vmap(dyn)(f_att, ker)
            out_lk = _conv(f_att, lk_filter, pad=LK // 2)
            out = jnp.concatenate([out_lk + out_dk, f_idt], axis=1)
            return _conv1x1(out, fus_w, fus_b)

        def _msdam(x, ds_w3, ds_b3, ds_w1, ds_b1, kg_w1, kg_b1, kg_w2, kg_b2, lk_filter, fus_w, fus_b, fin_w, fin_b):
            att = lambda t: _conv_att2(t, kg_w1, kg_b1, kg_w2, kg_b2, lk_filter, fus_w, fus_b)
            feats = []
            for i in range(LEVELS):
                y = x
                if i > 0:
                    k = 2 ** i
                    bb, cc, hh, ww = y.shape
                    y = y.reshape(bb, cc, hh // k, k, ww // k, k).mean(axis=(3, 5))
                    d = 2 * (i + 1) + 1
                else:
                    d = 1
                y = jax.nn.relu(_conv(y, ds_w3[i], ds_b3[i], pad=d, dil=d))
                y = _conv1x1(y, ds_w1[i], ds_b1[i])
                feats.append(y)
            out = att(feats[0])
            for i in range(1, LEVELS):
                k = 2 ** i
                out = out + jnp.repeat(jnp.repeat(att(feats[i]), k, axis=2), k, axis=3)
            return _conv1x1(out, fin_w, fin_b)
        return _msdam(x, ds_w3, ds_b3, ds_w1, ds_b1, kg_w1, kg_b1, kg_w2, kg_b2, lk_filter, fus_w, fus_b, fin_w, fin_b)

    def _L1_conv_ref(x, w3, b3, w5, b5, wr, br):
        import jax, jax.numpy as jnp
        import numpy as np
        from jax import lax
        DN = ('NCHW', 'OIHW', 'NCHW')
        y3 = lax.conv_general_dilated(x, w3, (1, 1), 'SAME', dimension_numbers=DN) + b3[None, :, None, None]
        y5 = lax.conv_general_dilated(x, w5, (1, 1), 'SAME', dimension_numbers=DN) + b5[None, :, None, None]
        B, C, H, W = y3.shape
        P = jnp.pad(y3, ((0, 0), (0, 0), (1, 1), (1, 1)))
        shifts = [P[:, :, 2 - sw:2 - sw + H, 2 - sh:2 - sh + W] for sh in range(3) for sw in range(3)]
        stacked = jnp.stack([y5] + shifts, axis=2)
        out = jnp.einsum('bcghw,cg->bchw', stacked, wr[:, :, 0, 0]) + br[None, :, None, None]
        return out

    def _gn(v, G=32, eps=1e-5):
        B_, C_, H_, W_ = v.shape
        g = v.reshape(B_, G, C_ // G, H_, W_)
        m = jnp.mean(g, axis=(2, 3, 4), keepdims=True)
        s = jnp.var(g, axis=(2, 3, 4), keepdims=True)
        return ((g - m) / jnp.sqrt(s + eps)).reshape(v.shape)

    def _ln_c(v, eps=1e-6):
        m = jnp.mean(v, axis=1, keepdims=True)
        s = jnp.var(v, axis=1, keepdims=True)
        return (v - m) / jnp.sqrt(s + eps)

    def _ln_t(v, eps=1e-5):
        m = jnp.mean(v, axis=-1, keepdims=True)
        s = jnp.var(v, axis=-1, keepdims=True)
        return (v - m) / jnp.sqrt(s + eps)

    def _to_tokens(v):
        B_, C_, H_, W_ = v.shape
        return v.reshape(B_, C_, H_ * W_).transpose(0, 2, 1)
    def _from_tokens(t, like):
        B_, C_, H_, W_ = like.shape
        return t.transpose(0, 2, 1).reshape(B_, C_, H_, W_)

    x = x + _L0_conv_ref(_gn(x), L0_conv_ds_w3, L0_conv_ds_b3, L0_conv_ds_w1, L0_conv_ds_b1, L0_conv_kg_w1, L0_conv_kg_b1, L0_conv_kg_w2, L0_conv_kg_b2, L0_conv_lk_filter, L0_conv_fus_w, L0_conv_fus_b, L0_conv_fin_w, L0_conv_fin_b)
    x = x + _L1_conv_ref(_gn(x), L1_conv_w3, L1_conv_b3, L1_conv_w5, L1_conv_b5, L1_conv_wr, L1_conv_br)
    return x


_drawn_inputs = setup_inputs


def setup_inputs(seed=0):
    import zlib

    import numpy as np

    out = dict(_drawn_inputs(seed))
    spreads = {'L0_conv_ds_b3': (0.0, 0.1),
     'L0_conv_ds_b1': (0.0, 0.1),
     'L0_conv_kg_b1': (0.0, 0.1),
     'L0_conv_kg_b2': (0.0, 0.1),
     'L0_conv_fus_b': (0.0, 0.1),
     'L0_conv_fin_b': (0.0, 0.1)}
    factors = {'L1_conv_b3': 5.014, 'L1_conv_b5': 8.0}
    for name, (base, spread) in spreads.items():
        noise = np.random.default_rng([zlib.crc32(name.encode()), seed]).standard_normal(out[name].shape)
        drawn = base * np.exp(spread * noise) if base else spread * noise
        out[name] = jnp.asarray(drawn.astype(out[name].dtype))
    for name, factor in factors.items():
        out[name] = (out[name] * factor).astype(out[name].dtype)
    return out
```

```python
from contextlib import ExitStack

import numpy as np
import concourse.bass as bass
from concourse import mybir

F32 = mybir.dt.float32
F32R = mybir.dt.float32r
ALU = mybir.AluOpType
ACT = mybir.ActivationFunctionType
AX = mybir.AxisListType

P = 128
B, C, H, W = 8, 64, 128, 128
ATT = 16
NI = C - ATT
LK = 13
LEVELS = 4
EPS = 1e-5
NPAIR = H // 2
NPB, NCB = 7, 4
DYN = [(pb, cb) for pb in (2, 3, 4) for cb in (1, 2)]
ND = len(DYN)
NSTAT = NPB * NCB - ND
SIDE = {1: 64, 2: 32, 3: 16}
DIL = {1: 5, 2: 7, 3: 9}


def slot(dr, dc):
    return (dc // 2) * 4 + dr * 2 + dc % 2


def par(r):
    return slice((1 - r) * C, (2 - r) * C)


PIX = [(dr, dc) for dr in range(2) for dc in range(4)]


class Steps:

    def __init__(self, sem, per_image):
        self.sem, self.per, self.n = sem, per_image, 0

    def start(self, image):
        self.base, self.n = self.per * image, 0

    def done(self, ins):
        ins.then_inc(self.sem, 1)
        self.n += 1
        assert self.n <= self.per

    def wait(self, eng):
        eng.wait_ge(self.sem, self.base + self.n)

    def at(self, eng, image, n):
        eng.wait_ge(self.sem, self.per * image + n)


def conv_kernel(nc, x, w3t, w1t, w1, b3, b1, kgw1t, kgb1, kgw2, kgb2, lkt, fus, fusb, fint, finb,
                c3t, c5t, c3b, c5b, wr, wrt, br, tapmask, chmask, slotmask, groupavg, out):
    zs = nc.dram_tensor("z_pooled", (B, C, NPAIR, W // 2), F32)

    with ExitStack() as ctx:
        def sb(name, shape, dt=F32, stack=ctx):
            return stack.enter_context(nc.sbuf_tensor(name, shape, dt))

        def sem(name, stack=ctx):
            return stack.enter_context(nc.semaphore(name))

        def psum(name, shape):
            return ctx.enter_context(nc.psum_tensor(name, shape, F32))

        ps_main = psum("ps_main", [P, 2, 512])
        ps_q = psum("ps_q", [P, 2, 512])
        ps_stat = psum("ps_stat", [P, 512])
        ps_chain = psum("ps_chain", [P, 512])
        ps_edge = psum("ps_edge", [P, 512])

        lk_h = sb("lk_h", [P, NPB, NCB, P], F32R)
        lk_l = sb("lk_l", [P, NPB, NCB, P], F32R)
        lk_base = sb("lk_base", [P, ND, P])
        idt_h = sb("idt_h", [P, LEVELS, P], F32R)
        idt_l = sb("idt_l", [P, LEVELS, P], F32R)
        gn0 = sb("gn0", [P, B, 2])
        gar = sb("gar", [P, C])
        w1a = sb("w1a", [P, LEVELS, ATT])
        b1a = sb("b1a", [P, LEVELS])
        b3p = sb("b3p", [P, LEVELS])
        kg1 = sb("kg1", [ATT, ATT // 2])
        kb1 = sb("kb1", [ATT // 2, 1])
        kg2 = sb("kg2", [ATT // 2, 9, P])
        kb2 = sb("kb2", [P, 9])
        tapm = sb("tapm", [P, ND * 8, 9])
        chm = sb("chm", [P, ATT])
        slm = sb("slm", [P, 8])
        gav = sb("gav", [P, P])
        bz = sb("bz", [P, 1])
        small = sb("small", [P, 64])
        dtap = sb("dtap", [P, ND * 8, 9])
        dcoef = sb("dcoef", [P, ND * 8])
        dker = sb("dker", [P, ND * P])
        kerr = sb("kerr", [P, 3, 9])
        stat = sb("stat", [P, 16, 6])

        passed = sem("passed")

        def alone(eng):
            eng.sem_inc(passed, 1)

        with ExitStack() as st:
            s_ld = sem("s_ld", st)
            s_lks = sem("s_lks", st)
            s_zero = sem("s_zero", st)
            s_hi = sem("s_hi", st)
            s_lo = sem("s_lo", st)
            s_mm = sem("s_mm", st)
            s_cp = sem("s_cp", st)
            lks = sb("lks", [P, 14, 16, ATT], stack=st)
            fus_s = sb("fus_s", [C, C], stack=st)
            fus_r = sb("fus_r", [C, 8, ATT], stack=st)
            fin_s = sb("fin_s", [C, 2, C], stack=st)
            fusb_s = sb("fusb_s", [C, 1], stack=st)
            finb_s = sb("finb_s", [P, 1], stack=st)
            w1i = sb("w1i", [NI, LEVELS, 2, C], stack=st)
            b1i = sb("b1i", [NI, LEVELS], stack=st)
            gti = sb("gti", [NI, 2, C], stack=st)
            idt = sb("idt", [P, LEVELS, P], stack=st)
            b1t = b1.rearrange("l c -> c l")
            b3t = b3.rearrange("l c -> c l")
            loads = [(fus_s[:, :], fus), (fusb_s[:, :], fusb.rearrange("(c a) -> c a", a=1)),
                     (kg1[:, :], kgw1t), (kb1[:, :], kgb1.rearrange("(c a) -> c a", a=1)),
                     (tapm[:, :, :], tapmask), (chm[:, :], chmask), (slm[:, :], slotmask), (gav[:, :], groupavg),
                     (b1i[:, :], b1t[ATT:, :])]
            for r in range(2):
                hp = slice(r * C, r * C + C)
                loads += [(fin_s[:, r, :], fint), (w1i[:, :, r, :], w1.rearrange("l o c -> o l c")[ATT:, :, :]),
                          (w1a[hp, :, :], w1t.rearrange("l c o -> c l o")[:, :, 0:ATT]),
                          (finb_s[hp, :], finb.rearrange("(c a) -> c a", a=1)), (b3p[hp, :], b3t)]
            for s in range(8):
                sp16 = slice(s * ATT, s * ATT + ATT)
                loads += [(fus_r[:, s, :], fus[:, 0:ATT]), (b1a[sp16, :], b1t[0:ATT, :]),
                          (kb2[sp16, :], kgb2), (kg2[:, :, sp16], kgw2)]
            NLD = len(loads)
            pieces = [(pb, dr, dc) for pb in range(NPB) for dr, dc in PIX]

            with nc.Block() as block:
                @block.sync
                def _(sp):
                    with nc.allow_non_contiguous_dma(reason="small weight layouts"):
                        for d, s in loads:
                            sp.dma_start(d, s).then_inc(s_ld, 16)
                        sp.wait_ge(s_zero, 1)
                        for dr, dc in PIX:
                            q = slot(dr, dc) * ATT
                            sp.dma_start(lks[q:q + ATT, 1 - dr:14 - dr, 3 - dc:16 - dc, :], lkt).then_inc(s_lks, 16)

                @block.gpsimd
                def _(pool):
                    pool.memset(lks[:, :, :, :], 0.0).then_inc(s_zero, 1)
                    pool.memset(idt[:, :, :], 0.0).then_inc(s_zero, 1)

                @block.scalar
                def _(act):
                    act.wait_ge(s_lks, 16 * 8)
                    for pb, dr, dc in pieces:
                        src = lks[:, 2 * pb - dr + 1, 3 - dc:16 - dc:4, :]
                        q = slot(dr, dc) * ATT
                        act.activation(lk_h[:, pb, :, q:q + ATT], src, ACT.Identity).then_inc(s_hi, 1)

                @block.vector
                def _(dve):
                    dve.wait_ge(s_ld, 16 * NLD)
                    dve.wait_ge(s_lks, 16 * 8)
                    for k, (pb, dr, dc) in enumerate(pieces):
                        src = lks[:, 2 * pb - dr + 1, 3 - dc:16 - dc:4, :]
                        q = slot(dr, dc) * ATT
                        dve.wait_ge(s_hi, k + 1)
                        dve.tensor_tensor(lk_l[:, pb, :, q:q + ATT], src, lk_h[:, pb, :, q:q + ATT].bitcast(F32),
                                          ALU.subtract).then_inc(s_lo, 1)
                        if pb in (2, 3, 4):
                            t = (pb - 2) * 2
                            dve.tensor_copy(lk_base[:, t:t + 2, q:q + ATT], src[:, 1:3, :]).then_inc(s_lo, 1)
                    dve.wait_ge(s_mm, 1)
                    dve.tensor_copy(gti[:, :, :], ps_main[0:NI, 0, 0:P]).then_inc(s_cp, 1)
                    dve.tensor_copy(gar[:, :], ps_main[:, 0, P:P + C]).then_inc(s_cp, 1)
                    dve.wait_ge(s_mm, 2)
                    dve.wait_ge(s_zero, 2)
                    for r in range(2):
                        hp = slice(r * C, r * C + C)
                        dve.tensor_copy(idt[hp, :, r * C:r * C + C],
                                        ps_q[hp, 0, 0:LEVELS * C].rearrange("p (l o) -> p l o", o=C)).then_inc(s_cp, 1)
                    dve.tensor_tensor(bz[:, :], ps_q[:, 1, 0:1], finb_s[:, :], ALU.add).then_inc(s_cp, 1)
                    dve.wait_ge(s_cp, 5)
                    dve.tensor_copy(idt_h[:, :, :], idt[:, :, :]).then_inc(s_cp, 1)
                    dve.wait_ge(s_cp, 6)
                    dve.tensor_tensor(idt_l[:, :, :], idt[:, :, :], idt_h[:, :, :].bitcast(F32),
                                      ALU.subtract).then_inc(s_cp, 1)

                @block.tensor
                def _(pe):
                    pe.wait_ge(s_ld, 16 * NLD)
                    pe.matmul(ps_main[0:NI, 0, 0:P], fus_s[:, ATT:C], fin_s[:, :, :], start=True, stop=True)
                    pe.matmul(ps_main[:, 0, P:P + C], fus_r[:, :, :], fin_s[:, 0, :], start=True,
                              stop=True, skip_group_check=True).then_inc(s_mm, 1)
                    pe.wait_ge(s_cp, 2)
                    for lv in range(LEVELS):
                        pe.matmul(ps_q[:, 0, lv * C:lv * C + C], w1i[:, lv, :, :], gti[:, 0, :],
                                  start=(lv == 0), stop=True, skip_group_check=True)
                    for lv in range(LEVELS):
                        pe.matmul(ps_q[:, 1, 0:1], gti[:, :, :], b1i[:, lv:lv + 1], start=(lv == 0), stop=False)
                    for lv in range(LEVELS):
                        mm = pe.matmul(ps_q[:, 1, 0:1], fin_s[:, :, :], fusb_s[:, :], start=False,
                                       stop=(lv == LEVELS - 1))
                    mm.then_inc(s_mm, 1)

        def product(pe, o, wh, wl, xh, xl, first, last):
            pe.matmul(o, wh, xh, start=first, stop=False, skip_group_check=True)
            pe.matmul(o, wh, xl, start=False, stop=False, skip_group_check=True)
            return pe.matmul(o, wl, xh, start=False, stop=last, skip_group_check=True)

        def large_filter(pe, o, fh, fl, p0, np_, nq, between):
            tiles = [(pb, cb) for pb in range(NPB) for cb in range(NCB) if (pb, cb) not in DYN] + DYN
            for k, (pb, cb) in enumerate(tiles):
                if k in between:
                    between[k]()
                v = (slice(None), slice(p0 + pb, p0 + pb + np_), slice(cb, cb + nq))
                mm = product(pe, o, lk_h[:, pb, cb, :], lk_l[:, pb, cb, :], fh[v], fl[v],
                             k == 0, k == len(tiles) - 1)
            return mm

        def dynamic_tiles(dve, steps, ker):
            steps.done(dve.tensor_tensor(dtap[:, :, :], tapm[:, :, :],
                                         ker.unsqueeze(1).to_broadcast([P, ND * 8, 9]), ALU.mult))
            steps.wait(dve)
            steps.done(dve.tensor_reduce(dcoef[:, :], dtap[:, :, :], AX.X, ALU.add))
            steps.wait(dve)
            steps.done(dve.tensor_tensor(dker[:, :].rearrange("p (m c) -> p m c", c=ATT),
                                         dcoef[:, :].unsqueeze(2).to_broadcast([P, ND * 8, ATT]),
                                         chm[:, :].unsqueeze(1).to_broadcast([P, ND * 8, ATT]), ALU.mult))
            steps.wait(dve)
            steps.done(dve.tensor_tensor(dker[:, :], dker[:, :], lk_base[:, :, :].rearrange("p t m -> p (t m)"),
                                         ALU.add))
            steps.wait(dve)
            dk = dker[:, :].rearrange("p (b m) -> p b m", b=3)
            hi = lk_h[:, 2:5, 1:3, :].rearrange("p b c m -> p b (c m)")
            lo = lk_l[:, 2:5, 1:3, :].rearrange("p b c m -> p b (c m)")
            steps.done(dve.tensor_copy(hi, dk))
            steps.wait(dve)
            steps.done(dve.tensor_tensor(lo, dk, hi.bitcast(F32), ALU.subtract))
        DSTEPS = 6

        def group_stats_dve(dve, steps, averaged, rooted, image, entries, mean, rstd):
            mv, dm, tv, vv, sd = (small[:, 0:2], small[:, 2:3], small[:, 3:4], small[:, 4:5], small[:, 5:6])
            steps.done(dve.bn_aggr(mv, entries))
            averaged(2 * image + 1)
            steps.done(dve.tensor_copy(mean, ps_stat[:, 0:1]))
            steps.wait(dve)
            steps.done(dve.tensor_tensor(dm, mv[:, 0:1], mean, ALU.subtract))
            steps.wait(dve)
            steps.done(dve.scalar_tensor_tensor(tv, dm, dm, mv[:, 1:2], ALU.mult, ALU.add))
            averaged(2 * image + 2)
            steps.done(dve.tensor_scalar(vv, ps_stat[:, 1:2], EPS, None, ALU.add))
            rooted(image + 1)
            steps.done(dve.reciprocal(rstd, sd))
            steps.wait(dve)
        GSTEPS = 6

        def group_stats_pe(pe, steps, image, s_avg):
            steps.at(pe, image, 1)
            pe.matmul(ps_stat[:, 0:1], gav[:, :], small[:, 0:1], start=True, stop=True,
                      skip_group_check=True).then_inc(s_avg, 1)
            steps.at(pe, image, 4)
            pe.matmul(ps_stat[:, 1:2], gav[:, :], small[:, 3:4], start=True, stop=True,
                      skip_group_check=True).then_inc(s_avg, 1)

        def group_stats_act(act, steps, image, s_root):
            steps.at(act, image, 5)
            act.activation(small[:, 5:6], small[:, 4:5], ACT.Sqrt).then_inc(s_root, 1)

        def chain_pooled(pe, image, lvs, s_sum, s_chain):
            s_sum.at(pe, image, s_sum.per)
            for k, lv in enumerate(lvs):
                mm = pe.matmul(ps_chain[0:ATT, k:k + 1], w1a[:, lv, :], rsum[:, k:k + 1], start=(k == 0),
                               stop=True, skip_group_check=True)
            mm.then_inc(s_chain, 1)

        def chain_hidden(pe, image, n, s_pooled, s_chain):
            pe.wait_ge(s_pooled, n * (image + 1))
            alone(pe)
            pe.matmul(ps_chain[0:ATT // 2, 8:8 + n], kg1[:, :], pooled[:, 0:n], start=True, stop=True,
                      skip_group_check=True).then_inc(s_chain, 1)

        def chain_taps(pe, image, n, s_hdn, s_chain):
            pe.wait_ge(s_hdn, image + 1)
            for t in range(9):
                mm = pe.matmul(ps_chain[:, 16 + n * t:16 + n * t + n], kg2[:, t, :], hdn[:, 0:n],
                               start=(t == 0), stop=True, skip_group_check=True)
            mm.then_inc(s_chain, 1)

        def chain_dve(dve, image, lvs, s_pooled, s_chain, s_ker):
            n = len(lvs)
            dve.wait_ge(s_chain, 3 * image + 1)
            for k, lv in enumerate(lvs):
                side = SIDE.get(lv, H)
                dve.tensor_scalar(pooled[:, k:k + 1], ps_chain[0:ATT, k:k + 1], 1.0 / (side * side),
                                  b1a[0:ATT, lv:lv + 1], ALU.mult, ALU.add).then_inc(s_pooled, 1)
            dve.wait_ge(s_chain, 3 * image + 3)
            dve.tensor_tensor(kerr[:, 0:n, :], ps_chain[:, 16:16 + 9 * n].rearrange("p (t k) -> p k t", k=n),
                              kb2[:, :].unsqueeze(1).to_broadcast([P, n, 9]), ALU.add).then_inc(s_ker, 1)

        def chain_act(act, image, n, s_chain, s_hdn):
            act.wait_ge(s_chain, 3 * image + 2)
            act.activation(hdn[:, 0:n], ps_chain[0:ATT // 2, 8:8 + n], ACT.Gelu, bias=kb1[:, 0:1]).then_inc(s_hdn, 1)

        rsum = sb("rsum", [P, 4])
        pooled = sb("pooled", [ATT, 4])
        hdn = sb("hdn", [ATT // 2, 4])

        with ExitStack() as st:
            def s1(name):
                return sem("p1_" + name, st)

            xc = sb("xc", [P, 2, 4, W], stack=st)
            half = {lv: SIDE[lv] // 2 for lv in SIDE}
            prow = {lv: half[lv] + 2 * DIL[lv] for lv in SIDE}
            plen = {lv: SIDE[lv] + DIL[lv] + (SIDE[lv] + DIL[lv]) % 2 for lv in SIDE}
            pl = {lv: sb(f"pl{lv}", [P, prow[lv], SIDE[lv]], stack=st) for lv in SIDE}
            nh = {lv: sb(f"nh{lv}", [P, prow[lv] * plen[lv] + 2 * DIL[lv]], F32R, stack=st) for lv in SIDE}
            nl = {lv: sb(f"nl{lv}", [P, prow[lv] * plen[lv] + 2 * DIL[lv]], F32R, stack=st) for lv in SIDE}
            rf = sb("rf", [P, 2, 512], stack=st)
            rh = {lv: sb(f"rh{lv}", [P, half[lv], SIDE[lv] + 8], F32R, stack=st) for lv in SIDE}
            rl = {lv: sb(f"rl{lv}", [P, half[lv], SIDE[lv] + 8], F32R, stack=st) for lv in SIDE}
            fh = {lv: sb(f"fh{lv}", [P, SIDE[lv] // 2 + 6, SIDE[lv] // 4 + 4], F32R, stack=st) for lv in SIDE}
            fl = {lv: sb(f"fl{lv}", [P, SIDE[lv] // 2 + 6, SIDE[lv] // 4 + 4], F32R, stack=st) for lv in SIDE}
            z = {lv: sb(f"z{lv}", [P, half[lv], SIDE[lv]], stack=st) for lv in SIDE}
            w3h = sb("w3h", [P, 3, 9, P], F32R, stack=st)
            w3l = sb("w3l", [P, 3, 9, P], F32R, stack=st)
            fa_h = sb("fa_h", [P, 3, 240], F32R, stack=st)
            fa_l = sb("fa_l", [P, 3, 240], F32R, stack=st)
            ga_h = sb("ga_h", [P, 8 * P + C], F32R, stack=st)
            ga_l = sb("ga_l", [P, 8 * P + C], F32R, stack=st)
            lh = sb("lh", [P, 512], F32R, stack=st)
            ll = sb("ll", [P, 512], F32R, stack=st)
            rs = sb("rs", [P, 8], stack=st)
            coef = sb("coef", [P, 3, 2], stack=st)
            zeros = sb("zeros", [P, 5 * 64], stack=st)

            order = (3, 2, 1)
            chunks = [(3, 0, 4), (3, 4, 4), (2, 0, 16)] + [(1, 8 * k, 8) for k in range(4)]
            NCH = len(chunks)
            MAIN = NCH + 3
            QF = 6
            Q = QF + 24
            assert MAIN % 2 == 0 and Q % 2 == 0
            fuses = [(lv, hf) for lv in order for hf in range(2)]

            with ExitStack() as se:
                stage = sb("stage", [P, 9, P], stack=se)
                fst = sb("fst", [P, 240], stack=se)
                gst = sb("gst", [P, C], stack=se)
                a_z = sem("a_z", se)
                a_ld = sem("a_ld", se)
                a_s = sem("a_s", se)
                a_p = sem("a_p", se)
                a_b = sem("a_b", se)
                a_g = sem("a_g", se)
                with nc.Block() as block:
                    @block.gpsimd
                    def _(pool):
                        for lv in SIDE:
                            for t in (nh[lv], nl[lv]):
                                pool.memset(t[:, :].bitcast(F32), 0.0).then_inc(a_p, 1)
                            for t in (rh[lv], rl[lv], fh[lv], fl[lv]):
                                pool.memset(t[:, :, :].bitcast(F32), 0.0).then_inc(a_p, 1)
                        pool.memset(zeros[:, :], 0.0).then_inc(a_p, 1)

                    @block.sync
                    def _(sp):
                        sp.wait_ge(a_z, 1)
                        for k in range(3):
                            if k > 0:
                                sp.wait_ge(a_s, 2 * k)
                            for r in range(2):
                                hp = slice(r * C, r * C + C)
                                sp.dma_start(stage[hp, :, hp], w3t[k + 1]).then_inc(a_ld, 16)

                    @block.vector
                    def _(dve):
                        dve.memset(stage[:, :, :], 0.0).then_inc(a_z, 1)
                        dve.memset(fa_h[:, :, :].bitcast(F32), 0.0).then_inc(a_b, 1)
                        dve.memset(fa_l[:, :, :].bitcast(F32), 0.0).then_inc(a_b, 1)
                        dve.memset(ga_h[:, :].bitcast(F32), 0.0).then_inc(a_b, 1)
                        dve.memset(ga_l[:, :].bitcast(F32), 0.0).then_inc(a_b, 1)
                        dve.wait_ge(a_b, 4)
                        n = 0
                        for k in range(3):
                            dve.tensor_copy(fa_h[:, k, 112:128], w1a[:, k + 1, :]).then_inc(a_g, 1)
                            n += 1
                            dve.wait_ge(a_g, n)
                            dve.tensor_tensor(fa_l[:, k, 112:128], w1a[:, k + 1, :],
                                              fa_h[:, k, 112:128].bitcast(F32), ALU.subtract).then_inc(a_b, 1)
                        for s in range(8):
                            o = slice(s * P + C, s * P + P)
                            dve.tensor_scalar(gst[:, :], gar[:, :], slm[:, s:s + 1], None, ALU.mult).then_inc(a_g, 1)
                            dve.wait_ge(a_g, n + 1)
                            dve.tensor_copy(ga_h[:, o], gst[:, :]).then_inc(a_g, 1)
                            dve.wait_ge(a_g, n + 2)
                            dve.tensor_tensor(ga_l[:, o], gst[:, :], ga_h[:, o].bitcast(F32),
                                              ALU.subtract).then_inc(a_g, 1)
                            n += 3
                            dve.wait_ge(a_g, n)
                        for k in range(3):
                            dve.wait_ge(a_ld, 32 * (k + 1))
                            dve.tensor_copy(w3h[:, k, :, :], stage[:, :, :]).then_inc(a_s, 1)
                            dve.wait_ge(a_s, 2 * k + 1)
                            dve.tensor_tensor(w3l[:, k, :, :], stage[:, :, :], w3h[:, k, :, :].bitcast(F32),
                                              ALU.subtract).then_inc(a_s, 1)

            xc_full = [s1("xc_full0"), s1("xc_full1")]
            bn_done = s1("bn_done")
            pl_done = s1("pl_done")
            p_done = s1("p_done")
            p_acc = s1("p_acc")
            p_done2 = s1("p_done2")
            halo = s1("halo")
            stats = Steps(s1("stats"), GSTEPS + 6 + 8)
            avg = s1("avg")
            root = s1("root")
            n_f = s1("n_f")
            n_h = s1("n_h")
            n_l = s1("n_l")
            main = s1("main")
            mfree = s1("mfree")
            qful = s1("qful")
            qfree = s1("qfree")
            r_h = s1("r_h")
            r_l = s1("r_l")
            f_h = s1("f_h")
            f_z = s1("f_z")
            sums = Steps(s1("sums"), 3)
            pooled_s = s1("pooled")
            chain = s1("chain")
            hdn_s = s1("hdn")
            ker_s = s1("ker")
            dyn = Steps(s1("dyn"), 3 * DSTEPS)
            l_h = s1("l_h")
            l_l = s1("l_l")
            zst = s1("zst")

            def nview(a, lv):
                d, n, m = DIL[lv], prow[lv], plen[lv]
                return a[lv][:, d:d + n * m].rearrange("p (r c) -> p r c", c=m)[:, :, 0:SIDE[lv]]

            def prep_at(k, last):
                per = -(-16 // NCH)
                return [] if last else range(per * k, min(per * k + per, 16))

            def edge_fills(lv):
                d, n2, rows = DIL[lv], half[lv], prow[lv]
                fills = [(0, 0, d), (1, n2 + d, rows)]
                if d > n2:
                    fills += [(0, d + 2 * n2, rows), (1, 0, d - n2)]
                return fills
            NFILL = sum(len(edge_fills(lv)) for lv in SIDE)
            assert NFILL == 8

            with nc.Block() as block:
                @block.sync
                def _(sp):
                    sp.sem_inc(bn_done, 2)
                    sp.sem_inc(pl_done, 2)
                    sp.sem_inc(mfree, 2)
                    sp.sem_inc(qfree, 2)
                    sp.sem_inc(r_l, 2)
                    sp.sem_inc(zst, 16)

                    def prep(i):
                        with sp.Fori(0, 8) as t:
                            for h in range(2):
                                sp.wait_ge(bn_done, 16 * i + 2 * t + h + 1)
                                sp.wait_ge(pl_done, 16 * i + 2 * t + h + 1)
                                for r in range(2):
                                    sp.dma_start(xc[r * C:r * C + C, h, :, :],
                                                 x[i, :, bass.ds(t * 8 + (4 * h + r * (H // 2)), 4), :]
                                                 ).then_inc(xc_full[h], 16)
                        sp.wait_ge(p_done, i + 1)
                        alone(sp)
                        sp.wait_ge(stats.sem, stats.per * (i + 1))
                        alone(sp)
                        for lv in order:
                            d, n2 = DIL[lv], half[lv]
                            k = min(d, n2)
                            sp.dma_start(pl[lv][0:C, d + n2:d + n2 + k, :],
                                         pl[lv][C:P, d:d + k, :]).then_inc(halo, 16)
                            sp.dma_start(pl[lv][C:P, d - k:d, :],
                                         pl[lv][0:C, d + n2 - k:d + n2, :]).then_inc(halo, 16)

                    def store(i):
                        sp.wait_ge(qfree, 2 + Q * (i + 1))
                        alone(sp)
                        for r in range(2):
                            sp.dma_start(zs.ap()[i, :, 32 * r:32 * r + 32, :], z[1][r * C:r * C + C, :, :]).then_inc(zst, 16)

                    prep(0)
                    with sp.Fori(0, B - 1) as i:
                        prep(i + 1)
                        store(i)
                    store(B - 1)
                    sp.wait_ge(zst, 16 + 32 * B)

                @block.gpsimd
                def _(pool):
                    def quad_sum(dst, src, k):
                        alone(pool)
                        v = src.rearrange("p (r a) (c b) -> p r a c b", a=2, b=2)
                        pool.tensor_tensor(dst, v[:, :, 0, :, 0], v[:, :, 0, :, 1], ALU.add).then_inc(p_acc, 1)
                        pool.wait_ge(p_acc, k + 1)
                        alone(pool)
                        pool.tensor_tensor(dst, dst, v[:, :, 1, :, 0], ALU.add).then_inc(p_acc, 1)
                        pool.wait_ge(p_acc, k + 2)
                        alone(pool)
                        return pool.tensor_tensor(dst, dst, v[:, :, 1, :, 1], ALU.add)

                    def prep_chunk(i, c):
                        pool.wait_ge(xc_full[c % 2], 32 * (8 * i + c // 2 + 1))
                        r0 = DIL[1] + 2 * c
                        quad_sum(pl[1][:, r0:r0 + 2, :], xc[:, c % 2, :, :], i * 36 + 2 * c).then_inc(pl_done, 1)

                    def prep_rest(i):
                        pool.wait_ge(pl_done, 2 + 16 * (i + 1))
                        quad_sum(pl[2][:, DIL[2]:DIL[2] + 16, :], pl[1][:, DIL[1]:DIL[1] + 32, :],
                                 i * 36 + 32).then_inc(p_done2, 1)
                        pool.wait_ge(p_done2, i + 1)
                        quad_sum(pl[3][:, DIL[3]:DIL[3] + 8, :], pl[2][:, DIL[2]:DIL[2] + 16, :],
                                 i * 36 + 34).then_inc(p_done, 1)

                    def norm(i):
                        for k, lv in enumerate(order):
                            pool.wait_ge(n_h, 3 * i + k + 1)
                            pool.tensor_tensor(nview(nl, lv), pl[lv][:, :, :], nview(nh, lv).bitcast(F32),
                                               ALU.subtract).then_inc(n_l, 1)

                    def body(i, last):
                        pool.wait_ge(n_l, 3 * (i + 1))
                        alone(pool)
                        for k, (lv, r0, nr) in enumerate(chunks):
                            pool.wait_ge(r_h, NCH * i + k + 1)
                            s = SIDE[lv]
                            pool.tensor_tensor(rl[lv][:, r0:r0 + nr, 2:2 + s],
                                               rf[:, k % 2, 0:nr * s].rearrange("p (r c) -> p r c", c=s),
                                               rh[lv][:, r0:r0 + nr, 2:2 + s].bitcast(F32),
                                               ALU.subtract).then_inc(r_l, 1)
                            for c in prep_at(k, last):
                                prep_chunk(i + 1, c)
                        pool.wait_ge(qfree, 2 + Q * i + QF)
                        alone(pool)
                        for lv in order:
                            n, q = SIDE[lv] // 2, SIDE[lv] // 4
                            for t in (fh[lv], fl[lv]):
                                pool.memset(t[0:C, 3:3 + n, 1:2].bitcast(F32), 0.0).then_inc(f_z, 1)
                                pool.memset(t[C:P, 3:3 + n, 1 + q:2 + q].bitcast(F32), 0.0).then_inc(f_z, 1)
                        pool.wait_ge(f_z, 12 * (i + 1))
                        alone(pool)
                        if not last:
                            prep_rest(i + 1)
                            norm(i + 1)

                    for c in range(16):
                        prep_chunk(0, c)
                    prep_rest(0)
                    norm(0)
                    with pool.Fori(0, B - 1) as i:
                        body(i, False)
                    body(B - 1, True)

                @block.scalar
                def _(act):
                    def norm(i):
                        for k, lv in enumerate(order):
                            act.wait_ge(n_f, 3 * i + k + 1)
                            act.activation(nview(nh, lv), pl[lv][:, :, :], ACT.Identity).then_inc(n_h, 1)

                    def body(i, last):
                        for k, (lv, r0, nr) in enumerate(chunks):
                            act.wait_ge(main, MAIN * i + k + 1)
                            act.wait_ge(r_l, NCH * i + k + 1)
                            n = nr * SIDE[lv]
                            act.activation(rf[:, k % 2, 0:n], ps_main[:, k % 2, 0:n], ACT.Relu,
                                           bias=b3p[:, lv:lv + 1], accum_out=rs[:, k:k + 1]).then_inc(mfree, 1)
                        for k, (lv, hf) in enumerate(fuses):
                            act.wait_ge(qful, Q * i + k + 1)
                            n, q = half[lv] // 2, SIDE[lv] // 4
                            p0 = 3 + n * hf
                            ps = ps_q[:, k % 2, 0:n * (q + 2)].rearrange("p (n q) -> p n q", q=q + 2)
                            act.activation(fh[lv][:, p0:p0 + n, 1:q + 2], ps[:, :, 0:q + 1], ACT.Identity,
                                           bias=b1a[:, lv:lv + 1]).then_inc(f_h, 1)
                        chain_act(act, i, 3, chain, hdn_s)
                        for k, lv in enumerate(order):
                            act.wait_ge(main, MAIN * i + NCH + k + 1)
                            act.wait_ge(qfree, 2 + Q * i + QF + 8 * k)
                            n = SIDE[lv] * SIDE[lv] // 8
                            act.activation(lh[:, 0:n], ps_main[:, (NCH + k) % 2, 0:n], ACT.Identity).then_inc(l_h, 1)
                            if k == 0 and not last:
                                group_stats_act(act, stats, i + 1, root)
                            if k == 1 and not last:
                                norm(i + 1)

                    group_stats_act(act, stats, 0, root)
                    norm(0)
                    with act.Fori(0, B - 1) as i:
                        body(i, False)
                    body(B - 1, True)

                @block.vector
                def _(dve):
                    def prep_chunk(i, c):
                        dve.wait_ge(xc_full[c % 2], 32 * (8 * i + c // 2 + 1))
                        dve.bn_stats(stat[:, c, :], xc[:, c % 2, :, :].rearrange("p a b -> p (a b)")).then_inc(bn_done, 1)

                    def prep_rest(i):
                        dve.wait_ge(bn_done, 2 + 16 * (i + 1))
                        alone(dve)
                        stats.start(i)
                        mean, rstd = gn0[:, bass.ds(i, 1), 0], gn0[:, bass.ds(i, 1), 1]
                        group_stats_dve(dve, stats, lambda v: dve.wait_ge(avg, v), lambda v: dve.wait_ge(root, v),
                                        i, stat[:, :, :].rearrange("p a b -> p (a b)"), mean, rstd)
                        for lv in SIDE:
                            k2 = float((H // SIDE[lv]) ** 2)
                            stats.done(dve.tensor_scalar(coef[:, lv - 1, 0:1], mean, k2, None, ALU.mult))
                            stats.done(dve.tensor_scalar(coef[:, lv - 1, 1:2], rstd, 1.0 / k2, None, ALU.mult))
                        stats.wait(dve)
                        for lv in SIDE:
                            for hf, r0, r1 in edge_fills(lv):
                                hp = slice(hf * C, hf * C + C)
                                n = (r1 - r0) * SIDE[lv]
                                stats.done(dve.tensor_scalar(
                                    pl[lv][hp, r0:r1, :].rearrange("p a b -> p (a b)"), zeros[hp, 0:n],
                                    coef[hp, lv - 1, 0:1], None, ALU.add))

                    def y_out(i, k):
                        lv = order[k]
                        for p, (dr, dc) in enumerate(PIX):
                            u = QF + 8 * k + p
                            dve.wait_ge(qful, Q * i + u + 1)
                            n, q = half[lv] // 2, SIDE[lv] // 4
                            dst = z[lv][:, dr::2, dc::4]
                            src = ps_q[:, u % 2, 0:n * q].rearrange("p (n q) -> p n q", q=q)
                            if lv == 3:
                                dve.tensor_copy(dst, src).then_inc(qfree, 1)
                            else:
                                dve.tensor_tensor(dst, src, z[lv + 1][:, :, dc // 2::2], ALU.add).then_inc(qfree, 1)

                    def split_lk(i, k):
                        n = SIDE[order[k]] ** 2 // 8
                        dve.wait_ge(l_h, 3 * i + k + 1)
                        dve.tensor_tensor(ll[:, 0:n], ps_main[:, (NCH + k) % 2, 0:n], lh[:, 0:n].bitcast(F32),
                                          ALU.subtract).then_inc(mfree, 1)

                    def dyn_tiles(i, k):
                        if k > 0:
                            dve.wait_ge(main, MAIN * i + NCH + k)
                        dynamic_tiles(dve, dyn, kerr[:, k, :])

                    def norm(i):
                        dve.wait_ge(halo, 96 * (i + 1))
                        for k, lv in enumerate(order):
                            dve.tensor_scalar(pl[lv][:, :, :], pl[lv][:, :, :], coef[:, lv - 1, 0:1],
                                              coef[:, lv - 1, 1:2], ALU.subtract, ALU.mult).then_inc(n_f, 1)

                    def body(i, last):
                        for k, (lv, r0, nr) in enumerate(chunks):
                            dve.wait_ge(mfree, 2 + MAIN * i + k + 1)
                            s = SIDE[lv]
                            dve.tensor_copy(rh[lv][:, r0:r0 + nr, 2:2 + s],
                                            rf[:, k % 2, 0:nr * s].rearrange("p (r c) -> p r c", c=s)).then_inc(r_h, 1)
                            for c in prep_at(k, last):
                                prep_chunk(i + 1, c)
                        sums.start(i)
                        sums.done(dve.tensor_reduce(rsum[:, 0:1], rs[:, 0:2], AX.X, ALU.add))
                        sums.done(dve.tensor_copy(rsum[:, 1:2], rs[:, 2:3]))
                        sums.done(dve.tensor_reduce(rsum[:, 2:3], rs[:, 3:7], AX.X, ALU.add))
                        for k, (lv, hf) in enumerate(fuses):
                            dve.wait_ge(f_h, QF * i + k + 1)
                            n, q = half[lv] // 2, SIDE[lv] // 4
                            p0 = 3 + n * hf
                            ps = ps_q[:, k % 2, 0:n * (q + 2)].rearrange("p (n q) -> p n q", q=q + 2)
                            dve.scalar_tensor_tensor(fl[lv][:, p0:p0 + n, 1:q + 2], ps[:, :, 0:q + 1],
                                                     b1a[:, lv:lv + 1], fh[lv][:, p0:p0 + n, 1:q + 2].bitcast(F32),
                                                     ALU.add, ALU.subtract).then_inc(qfree, 1)
                        chain_dve(dve, i, order, pooled_s, chain, ker_s)
                        dve.wait_ge(ker_s, i + 1)
                        dyn.start(i)
                        dyn_tiles(i, 0)
                        split_lk(i, 0)
                        dyn_tiles(i, 1)
                        if not last:
                            dve.wait_ge(n_l, 3 * (i + 1))
                            alone(dve)
                            prep_rest(i + 1)
                        y_out(i, 0)
                        split_lk(i, 1)
                        dyn_tiles(i, 2)
                        if not last:
                            norm(i + 1)
                        dve.wait_ge(qfree, 2 + Q * i + QF + 8)
                        y_out(i, 1)
                        split_lk(i, 2)
                        dve.wait_ge(qfree, 2 + Q * i + QF + 16)
                        dve.wait_ge(zst, 16 + 32 * i)
                        y_out(i, 2)

                    for c in range(16):
                        prep_chunk(0, c)
                    prep_rest(0)
                    norm(0)
                    with dve.Fori(0, B - 1) as i:
                        body(i, False)
                    body(B - 1, True)

                @block.tensor
                def _(pe):
                    def y_part(i, k):
                        lv = order[k]
                        pe.wait_ge(mfree, 2 + MAIN * i + NCH + k + 1)
                        n, q = half[lv] // 2, SIDE[lv] // 4
                        for p, (dr, dc) in enumerate(PIX):
                            u = QF + 8 * k + p
                            pe.wait_ge(qfree, Q * i + u + 1)
                            o = ps_q[:, u % 2, 0:n * q].rearrange("p (n q) -> p n q", q=q)
                            v = (slice(None), slice(dr, None, 2), slice(2 + dc, 2 + dc + 4 * q - 3, 4))
                            product(pe, o, idt_h[:, lv, :], idt_l[:, lv, :], rh[lv][v], rl[lv][v], True, False)
                            for hf in range(2):
                                g = slice(slot(dr, dc) * P + C * (1 - hf), slot(dr, dc) * P + C * (1 - hf) + P)
                                m = slice(hf * n * q, (hf + 1) * n * q)
                                mm = product(pe, ps_q[:, u % 2, 0:n * q], ga_h[:, g], ga_l[:, g], lh[:, m], ll[:, m],
                                             False, hf == 1)
                            mm.then_inc(qful, 1)

                    def body(i, last):
                        for k, (lv, r0, nr) in enumerate(chunks):
                            pe.wait_ge(n_l, 3 * i + order.index(lv) + 1)
                            pe.wait_ge(mfree, MAIN * i + k + 1)
                            s, d = SIDE[lv], DIL[lv]
                            for t in range(9):
                                o0 = (r0 + (t // 3) * d) * plen[lv] + (t % 3) * d
                                vh, vl = (a[lv][:, o0:o0 + nr * plen[lv]].rearrange("p (r c) -> p r c", c=plen[lv])
                                          [:, :, 0:s] for a in (nh, nl))
                                mm = product(pe, ps_main[:, k % 2, 0:nr * s].rearrange("p (r c) -> p r c", c=s),
                                             w3h[:, lv - 1, t, :], w3l[:, lv - 1, t, :], vh, vl, t == 0, t == 8)
                            mm.then_inc(main, 1)
                        pe.wait_ge(r_l, 2 + NCH * (i + 1))
                        chain_pooled(pe, i, order, sums, chain)
                        for k, lv in enumerate(order):
                            pe.wait_ge(qfree, Q * i + 2 * k + 2)
                            n, q = half[lv] // 2, SIDE[lv] // 4 + 2
                            for j, (dr, dc) in enumerate(PIX):
                                a = 112 - ATT * slot(dr, dc)
                                for hf in range(2):
                                    v = (slice(hf * C, hf * C + C), slice(dr, None, 2), slice(dc, dc + 4 * q - 3, 4))
                                    w = (v[0], lv - 1, slice(a, a + P))
                                    mm = product(pe, ps_q[:, hf, 0:n * q].rearrange("p (n q) -> p n q", q=q),
                                                 fa_h[w], fa_l[w], rh[lv][v], rl[lv][v], j == 0, j == 7)
                                    if j == 7:
                                        mm.then_inc(qful, 1)
                        chain_hidden(pe, i, 3, pooled_s, chain)
                        pe.wait_ge(f_z, 12 * (i + 1))
                        for k, lv in enumerate(order):
                            pe.wait_ge(mfree, MAIN * i + NCH + k + 1)
                            n, q = SIDE[lv] // 2, SIDE[lv] // 4
                            between = {NSTAT: lambda: dyn.at(pe, i, DSTEPS * (k + 1))}
                            if k == 0:
                                between[10] = lambda: chain_taps(pe, i, 3, hdn_s, chain)
                            large_filter(pe, ps_main[:, (NCH + k) % 2, 0:n * q].rearrange("p (n q) -> p n q", q=q),
                                         fh[lv], fl[lv], 0, n, q, between).then_inc(main, 1)
                            if k == 1 and not last:
                                group_stats_pe(pe, stats, i + 1, avg)
                            if k > 0:
                                y_part(i, k - 1)
                        y_part(i, 2)

                    group_stats_pe(pe, stats, 0, avg)
                    with pe.Fori(0, B - 1) as i:
                        body(i, False)
                    body(B - 1, True)

        NW = NPAIR // 4
        with ExitStack() as st:
            def s2(name):
                return sem("p2_" + name, st)

            t3_h = sb("t3_h", [P, 2, 3, P], F32R, stack=st)
            t3_l = sb("t3_l", [P, 2, 3, P], F32R, stack=st)
            c5_h = sb("c5_h", [P, 3, 5, P], F32R, stack=st)
            c5_l = sb("c5_l", [P, 3, 5, P], F32R, stack=st)
            fa_h = sb("fa0_h", [P, 4, P], F32R, stack=st)
            fa_l = sb("fa0_l", [P, 4, P], F32R, stack=st)
            ga_h = sb("ga0_h", [P, 4, P], F32R, stack=st)
            ga_l = sb("ga0_l", [P, 4, P], F32R, stack=st)
            row_w = sb("row_w", [P, 5, C], stack=st)
            col_w = sb("col_w", [P, 2, 3, P], stack=st)
            cor_w = sb("cor_w", [P, 2, C], stack=st)
            edge_b = sb("edge_b", [P, 256], stack=st)
            out_b = sb("out_b", [P, 1], stack=st)
            zeros = sb("zeros0", [P, 2, W], stack=st)

            x1 = sb("x1", [P, NPAIR + 2, W], stack=st)
            fh = sb("fh0", [P, NPAIR + 6, 36], F32R, stack=st)
            fl = sb("fl0", [P, NPAIR + 6, 36], F32R, stack=st)
            xh = sb("xh", [P, 2, 5, W + 2], F32R, stack=st)
            xl = sb("xl", [P, 2, 5, W + 2], F32R, stack=st)
            rh = sb("rh0", [P, 2, 4, W + 8], F32R, stack=st)
            rl = sb("rl0", [P, 2, 4, W + 8], F32R, stack=st)
            yh = sb("yh", [P, 2, 6, W + 4], F32R, stack=st)
            yl = sb("yl", [P, 2, 6, W + 4], F32R, stack=st)
            rowf = sb("rowf", [P, W + 4], stack=st)
            colf = sb("colf", [P, 2, NPAIR + 2], stack=st)
            xp = x.rearrange("b c (p r) w -> b c p r w", r=2)
            op = out.rearrange("b c (p r) w -> b c p r w", r=2)

            with ExitStack() as se:
                b_p = sem("b_p", se)
                b_z = sem("b_z", se)
                b_ld = sem("b_ld", se)
                b_x = sem("b_x", se)
                steps = Steps(sem("b_s", se), 200)
                s3 = sb("s3", [P, 4, 3, C], stack=se)
                s31 = sb("s31", [P, 4, 3, C], stack=se)
                c5 = sb("c5", [P, 6, 5, C], stack=se)
                wrb = sb("wrb", [P, 10, C], stack=se)
                tmp = sb("tmp", [P, 4, 3, C], stack=se)
                tile_f = sb("tile_f", [P, 3, 5, P], stack=se)
                cls = sb("cls", [P, 2, 6, C], stack=se)
                wrs = sb("wrs", [P, 10], stack=se)
                bb = sb("bb", [P, 8], stack=se)

                def g(sh, sw):
                    return 1 + 3 * sh + sw

                with nc.Block() as block:
                    @block.gpsimd
                    def _(pool):
                        for t in (fh, fl):
                            pool.memset(t[:, :, :].bitcast(F32), 0.0).then_inc(b_p, 1)
                        for t in (xh, xl, rh, rl, yh, yl):
                            pool.memset(t[:, :, :, :].bitcast(F32), 0.0).then_inc(b_p, 1)
                        pool.memset(zeros[:, :, :], 0.0).then_inc(b_p, 1)
                        pool.memset(rowf[:, :], 0.0).then_inc(b_p, 1)

                    @block.sync
                    def _(sp):
                        with nc.allow_non_contiguous_dma(reason="small weight layouts"):
                            sp.dma_start(wrb[:, :, :], wrt.unsqueeze(0).to_broadcast([P, 10, C])).then_inc(b_ld, 16)
                            for r in range(2):
                                hp = slice(r * C, r * C + C)
                                sp.dma_start(wrs[hp, :], wr).then_inc(b_ld, 16)
                                for k, v in enumerate((c3b, c5b, br)):
                                    sp.dma_start(bb[hp, k:k + 1], v.rearrange("(c a) -> c a", a=1)).then_inc(b_ld, 16)
                            for r in range(2):
                                sp.dma_start(x1[par(r), 1:NPAIR + 1, :], xp[0, :, :, r, :]).then_inc(b_x, 16)
                            sp.wait_ge(b_z, 3)
                            for r in range(2):
                                hp = slice(r * C, r * C + C)
                                w0 = w3t[0].rearrange("c (y x) o -> c y x o", x=3)
                                sp.dma_start(s3[hp, 1 - r:4 - r, :, :], w0).then_inc(b_ld, 16)
                                sp.dma_start(s31[par(r), 1 - r:4 - r, :, :], c3t).then_inc(b_ld, 16)
                                sp.dma_start(c5[par(r), 1 - r:6 - r, :, :], c5t).then_inc(b_ld, 16)
                            sp.wait_ge(b_x, 16 * 2)

                    @block.vector
                    def _(dve):
                        steps.start(0)

                        def step(ins):
                            steps.done(ins)
                            steps.wait(dve)

                        def split(hi, lo, src):
                            step(dve.tensor_copy(hi, src))
                            step(dve.tensor_tensor(lo, src, hi.bitcast(F32), ALU.subtract))

                        for t in (s3, s31, c5):
                            dve.memset(t[:, :, :, :], 0.0).then_inc(b_z, 1)
                        step(dve.memset(tile_f[:, :, :, :], 0.0))
                        step(dve.memset(row_w[:, :, :], 0.0))
                        step(dve.memset(cls[:, :, :, :], 0.0))
                        for dr, dc in PIX:
                            hp, q = par(dr), slot(dr, dc) * ATT
                            step(dve.tensor_copy(tile_f[hp, 0, dc, q:q + ATT], w1a[hp, 0, :]))
                        split(fa_h[:, :, :], fa_l[:, :, :], tile_f[:, 0, 0:4, :])
                        for dr, dc in PIX:
                            s = slot(dr, dc)
                            step(dve.tensor_scalar(tile_f[:, 0, dc, par(dr)], gar[:, :], slm[:, s:s + 1],
                                                   None, ALU.mult))
                        split(ga_h[:, :, :], ga_l[:, :, :], tile_f[:, 0, 0:4, :])
                        dve.wait_ge(b_ld, 16 * 15)
                        for blk in range(2):
                            for m in range(2):
                                step(dve.tensor_copy(tile_f[:, blk, 0:3, par(m)], s3[:, 2 * blk - m + 1, :, :]))
                        split(t3_h[:, :, :, :], t3_l[:, :, :, :], tile_f[:, 0:2, 0:3, :])

                        step(dve.tensor_tensor(c5[:, :, :, :].rearrange("p a b c -> p (a b) c"),
                                               c5[:, :, :, :].rearrange("p a b c -> p (a b) c"),
                                               wrb[:, 0, :].unsqueeze(1).to_broadcast([P, 30, C]), ALU.mult))
                        for sh in range(3):
                            for sw in range(3):
                                step(dve.tensor_tensor(tmp[:, :, :, :].rearrange("p a b c -> p (a b) c"),
                                                       s31[:, :, :, :].rearrange("p a b c -> p (a b) c"),
                                                       wrb[:, g(sh, sw), :].unsqueeze(1).to_broadcast([P, 12, C]),
                                                       ALU.mult))
                                d = c5[:, 2 - sw:6 - sw, 2 - sh:5 - sh, :]
                                step(dve.tensor_tensor(d, d, tmp[:, :, :, :], ALU.add))
                                for side, h0, kx in ((0, 2, 2), (1, 0, 0)):
                                    if sh == h0:
                                        d = cls[:, side, 2 - sw:6 - sw, :]
                                        step(dve.tensor_tensor(d, d, tmp[:, :, kx, :], ALU.add))
                                for r, w0, a in ((0, 2, 3), (1, 0, 0)):
                                    hp = par(r)
                                    if sw == w0:
                                        d = row_w[hp, 2 - sh:5 - sh, :]
                                        step(dve.tensor_tensor(d, d, tmp[hp, a, :, :], ALU.add))
                                        for side, h0, kx in ((0, 2, 2), (1, 0, 0)):
                                            if sh == h0:
                                                step(dve.tensor_scalar(cor_w[hp, side, :], tmp[hp, a, kx, :], -1.0,
                                                                       None, ALU.mult))
                        for blk in range(3):
                            for m in range(2):
                                step(dve.tensor_copy(tile_f[:, blk, :, par(m)], c5[:, 2 * blk - m + 1, :, :]))
                                step(dve.tensor_copy(col_w[:, :, blk, par(m)], cls[:, :, 2 * blk - m + 1, :]))
                        split(c5_h[:, :, :, :], c5_l[:, :, :, :], tile_f[:, :, :, :])
                        b_3, b_5, b_r, t = (bb[:, k:k + 1] for k in range(4))
                        step(dve.tensor_reduce(t, wrs[:, 1:10], AX.X, ALU.add))
                        step(dve.scalar_tensor_tensor(out_b[:, :], t, b_3, b_r, ALU.mult, ALU.add))
                        step(dve.scalar_tensor_tensor(out_b[:, :], wrs[:, 0:1], b_5, out_b[:, :], ALU.mult, ALU.add))
                        step(dve.memset(edge_b[:, :], 1.0))
                        for r, w0, pair in ((0, 2, 0), (1, 0, NPAIR - 1)):
                            hp = par(r)
                            step(dve.tensor_reduce(t[hp], wrs[hp, g(0, w0):g(2, w0) + 1:3], AX.X, ALU.add))
                            step(dve.tensor_scalar(edge_b[hp, 0:W], edge_b[hp, 0:W], t[hp], b_3[hp], ALU.mult, ALU.mult))
                        for side, h0 in ((0, 2), (1, 0)):
                            e = edge_b[:, W + side * NPAIR:W + side * NPAIR + NPAIR]
                            step(dve.tensor_reduce(t, wrs[:, g(h0, 0):g(h0, 2) + 1], AX.X, ALU.add))
                            step(dve.tensor_scalar(e, e, t, b_3, ALU.mult, ALU.mult))
                            for r, w0, pair in ((0, 2, 0), (1, 0, NPAIR - 1)):
                                hp, k = par(r), g(h0, w0)
                                step(dve.tensor_scalar(t[hp], wrs[hp, k:k + 1], b_3[hp], None, ALU.mult))
                                step(dve.tensor_tensor(e[hp, pair:pair + 1], e[hp, pair:pair + 1], t[hp], ALU.subtract))

            zall = sb("zall", [P, NPAIR, W // 2], stack=st)
            xnf = sb("xnf", [P, 5, W], stack=st)
            rf = sb("rf0", [P, 512], stack=st)
            lh = sb("lh0", [P, 2, 512], F32R, stack=st)
            ll = sb("ll0", [P, 2, 512], F32R, stack=st)
            xn1 = sb("xn1", [P, 6, W], stack=st)
            ot = sb("ot", [P, 2, 4, W], stack=st)
            edge = sb("edge", [P, 256], stack=st)
            m0 = sb("m0", [P, 2], stack=st)
            m1 = sb("m1", [P, 2], stack=st)
            rs = sb("rs0", [P, NW], stack=st)

            MAIN, Q = 36, 48
            QY = 2 * NW
            MB, MC = NW, NW + 4
            assert MAIN == MC + NW and Q == QY + 16
            m_cp, e_in = s2("m_cp"), s2("e_in")
            m_row = s2("m_row")
            x_full = s2("x_full")
            z_full = s2("z_full")
            NLOAD = 8
            x_n, x_h, x_l = s2("x_n"), s2("x_h"), s2("x_l")
            main, mfree, qful, qfree = s2("main"), s2("mfree"), s2("qful"), s2("qfree")
            r_h, r_l, x_z, f_h, f_z = s2("r_h"), s2("r_l"), s2("x_z"), s2("f_h"), s2("f_z")
            sums = Steps(s2("sums"), 1)
            pooled_s, chain, hdn_s, ker_s = s2("pooled"), s2("chain"), s2("hdn"), s2("ker")
            dyn = Steps(s2("dyn"), DSTEPS)
            l_h, bn = s2("l_h"), s2("bn")
            stats = Steps(s2("stats"), GSTEPS + 3)
            avg, root = s2("avg"), s2("root")
            y_n, y_h, y_l = s2("y_n"), s2("y_h"), s2("y_l")
            e_mm, e_out = s2("e_mm"), s2("e_out")
            o_row, o_done = s2("o_row"), s2("o_done")
            stored = [s2("stored0"), s2("stored1")]

            def windows(eng, first, body, before={}):
                for w in range(first, 2):
                    body(w, w % 2)
                with eng.Fori(1, NW // 2 - 1) as t:
                    for h in range(2):
                        body(2 * t + h, h)
                for w in range(NW - 2, NW):
                    if w in before:
                        before[w]()
                    body(w, w % 2)

            def is_last(w, k):
                return isinstance(w, int) and w + k >= NW

            def is_first(w, k):
                return isinstance(w, int) and w < k

            with nc.Block() as block:
                @block.sync
                def _(sp):
                    sp.sem_inc(mfree, 2)
                    sp.sem_inc(qfree, 2)
                    for sm in (x_n, x_l, r_l, y_l):
                        sp.sem_inc(sm, 1)
                    for sm in (x_full, *stored):
                        sp.sem_inc(sm, 16)

                    def load_z(i):
                        for r in range(2):
                            sp.dma_start(zall[par(r), :, :], zs.ap()[i]).then_inc(z_full, 16)

                    def load(i):
                        sp.wait_ge(x_z, NW * (i + 1))
                        alone(sp)
                        load_z(i + 1)
                        n = NPAIR // NLOAD
                        with sp.Fori(0, NLOAD) as u:
                            sp.wait_ge(o_done, NW * i + 2 * u + 2)
                            alone(sp)
                            sp.wait_ge(x_full, 16 + 32 * (NLOAD * i + u))
                            alone(sp)
                            for r in range(2):
                                sp.dma_start(x1[par(r), bass.ds(n * u + 1, n), :],
                                             xp[i + 1, :, bass.ds(n * u, n), r, :]).then_inc(x_full, 16)

                    load_z(0)
                    with sp.Fori(0, B - 1) as i:
                        load(i)

                @block.gpsimd
                def _(pool):
                    def stage_a(i, w, h):
                        pool.wait_ge(x_n, NW * i + w + (2 if is_last(w, 1) else 3))
                        v = x1[:, bass.ds(4 * w + 1, 4), :].rearrange("p a (b c) -> p (a b) c", c=2)
                        zz = zall[:, bass.ds(4 * w, 4), :].rearrange("p a b -> p (a b)").unsqueeze(2)
                        alone(pool)
                        pool.tensor_tensor(v, v, zz.to_broadcast([P, 256, 2]), ALU.add).then_inc(x_z, 1)
                        pool.wait_ge(r_h, NW * i + w + 1)
                        pool.tensor_tensor(rl[:, h, :, 2:2 + W], rf[:, :].rearrange("p (a b) -> p a b", b=W),
                                           rh[:, h, :, 2:2 + W].bitcast(F32), ALU.subtract).then_inc(r_l, 1)

                    def y_low(i, v, h):
                        pool.wait_ge(y_h, NW * i + v + 1)
                        pool.tensor_tensor(yl[:, h, :, 2:2 + W], xn1[:, :, :], yh[:, h, :, 2:2 + W].bitcast(F32),
                                           ALU.subtract).then_inc(y_l, 1)

                    with pool.Fori(0, B) as i:
                        pool.wait_ge(z_full, 32 * (i + 1))
                        alone(pool)
                        windows(pool, 0, lambda w, h: stage_a(i, w, h))
                        pool.wait_ge(qfree, 2 + Q * i + QY)
                        alone(pool)
                        for t in (fh, fl):
                            pool.memset(t[0:C, 3:3 + NPAIR, 1:2].bitcast(F32), 0.0).then_inc(f_z, 1)
                            pool.memset(t[C:P, 3:3 + NPAIR, 33:34].bitcast(F32), 0.0).then_inc(f_z, 1)
                        pool.wait_ge(f_z, 4 * (i + 1))
                        windows(pool, 0, lambda v, h: y_low(i, v, h))

                @block.scalar
                def _(act):
                    def x_high(i, w, h):
                        act.wait_ge(x_n, NW * i + w + 2)
                        if not is_first(w, 2):
                            act.wait_ge(main, MAIN * i + w - 1)
                        act.activation(xh[:, h, :, 1:1 + W], xnf[:, :, :], ACT.Identity).then_inc(x_h, 1)

                    def f_high(i, w, h):
                        act.wait_ge(qful, Q * i + 2 * w + 1)
                        ps = ps_q[:, 0, 0:136].rearrange("p (n q) -> p n q", q=34)
                        act.activation(fh[:, bass.ds(4 * w + 3, 4), 1:34], ps[:, :, 0:33], ACT.Identity,
                                       bias=b1a[:, 0:1]).then_inc(f_h, 1)

                    def stage_a(i, w, h):
                        act.wait_ge(main, MAIN * i + w + 1)
                        act.wait_ge(r_l, NW * i + w + 1)
                        act.activation(rf[:, :], ps_main[:, h, :], ACT.Relu, bias=b3p[:, 0:1],
                                       accum_out=rs[:, bass.ds(w, 1)]).then_inc(mfree, 1)
                        if not is_first(w, 1):
                            f_high(i, w - 1, 1 - h)
                        if not is_last(w, 2):
                            x_high(i, w + 2, h)

                    def y_high(i, v, h):
                        act.wait_ge(y_n, NW * i + v + 1)
                        if not is_first(v, 2):
                            act.wait_ge(main, MAIN * i + MC + v - 1)
                        act.activation(yh[:, h, :, 2:2 + W], xn1[:, :, :], ACT.Identity).then_inc(y_h, 1)

                    def store(i, v, h):
                        act.wait_ge(o_done, NW * i + v + 1)
                        for r in range(2):
                            act.dma_start(op[i, :, bass.ds(4 * v, 4), r, :],
                                          ot[par(r), h, :, :]).then_inc(stored[h], 16)

                    def stage_c(i, v, h):
                        if not is_last(v, 2):
                            y_high(i, v + 2, h)
                        store(i, v, h)

                    def body(i, last):
                        windows(act, 0, lambda w, h: stage_a(i, w, h))
                        f_high(i, NW - 1, 1)
                        chain_act(act, i, 1, chain, hdn_s)
                        for c in range(4):
                            act.wait_ge(main, MAIN * i + MB + c + 1)
                            if c >= 2:
                                act.wait_ge(qful, Q * i + QY + 4 * (c - 1))
                            act.activation(lh[:, c % 2, :], ps_main[:, c % 2, :], ACT.Identity).then_inc(l_h, 1)
                        group_stats_act(act, stats, i, root)
                        for v in range(2):
                            y_high(i, v, v)
                        windows(act, 0, lambda v, h: stage_c(i, v, h), {} if last else {
                            NW - 2: lambda: x_high(i + 1, 0, 0), NW - 1: lambda: x_high(i + 1, 1, 1)})

                    x_high(0, 0, 0)
                    x_high(0, 1, 1)
                    with act.Fori(0, B - 1) as i:
                        body(i, False)
                    body(B - 1, True)
                    for h in range(2):
                        act.wait_ge(stored[h], 16 + 32 * B * NW // 2)

                @block.vector
                def _(dve):
                    def x_norm(i, w):
                        if is_first(w, 2):
                            dve.wait_ge(m_row, i + 1)
                        dve.wait_ge(x_l, NW * i + w + 1)
                        for hp, k in ((par(1), 0), (par(0), 1)):
                            ins = dve.tensor_scalar(xnf[hp, :, :], x1[hp, bass.ds(4 * w + k, 5), :], m0[hp, 0:1],
                                                    m0[hp, 1:2], ALU.subtract, ALU.mult)
                        ins.then_inc(x_n, 1)

                    def x_low(i, w, h):
                        dve.wait_ge(x_h, NW * i + w + 1)
                        dve.tensor_tensor(xl[:, h, :, 1:1 + W], xnf[:, :, :], xh[:, h, :, 1:1 + W].bitcast(F32),
                                          ALU.subtract).then_inc(x_l, 1)

                    def next_image(i):
                        dve.tensor_copy(m0[:, :], gn0[:, bass.ds(i, 1), :].rearrange("p a b -> p (a b)")).then_inc(m_cp, 1)
                        dve.wait_ge(m_cp, i + 1)
                        dve.tensor_scalar(x1[:, 0:NPAIR + 2:NPAIR + 1, :], zeros[:, :, :], m0[:, 0:1], None,
                                          ALU.add).then_inc(m_row, 1)

                    def first_norm(i):
                        next_image(i)
                        x_norm(i, 0)

                    def second_norm(i):
                        x_low(i, 0, 0)
                        x_norm(i, 1)

                    def a_out(i, w, h):
                        dve.wait_ge(f_h, NW * i + w + 1)
                        ps = ps_q[:, 0, 0:136].rearrange("p (n q) -> p n q", q=34)
                        dve.scalar_tensor_tensor(fl[:, bass.ds(4 * w + 3, 4), 1:34], ps[:, :, 0:33], b1a[:, 0:1],
                                                 fh[:, bass.ds(4 * w + 3, 4), 1:34].bitcast(F32), ALU.add,
                                                 ALU.subtract).then_inc(qfree, 1)
                        dve.wait_ge(qful, Q * i + 2 * w + 2)
                        dve.wait_ge(x_z, NW * i + w + 1)
                        dve.scalar_tensor_tensor(x1[:, bass.ds(4 * w + 1, 4), :].rearrange("p a b -> p (a b)"),
                                                 ps_q[:, 1, :], bz[:, 0:1],
                                                 x1[:, bass.ds(4 * w + 1, 4), :].rearrange("p a b -> p (a b)"), ALU.add,
                                                 ALU.add).then_inc(qfree, 1)

                    def stage_a(i, w, h):
                        if not is_last(w, 1):
                            x_low(i, w + 1, 1 - h)
                        dve.wait_ge(mfree, 2 + MAIN * i + w + 1)
                        if not is_first(w, 2):
                            dve.wait_ge(qful, Q * i + 2 * w - 2)
                        dve.tensor_copy(rh[:, h, :, 2:2 + W],
                                        rf[:, :].rearrange("p (a b) -> p a b", b=W)).then_inc(r_h, 1)
                        if not is_first(w, 1):
                            a_out(i, w - 1, 1 - h)
                        if is_first(w, 1):
                            dve.wait_ge(x_full, 16 + 32 * NLOAD * i)
                        if not is_last(w, 2):
                            x_norm(i, w + 2)

                    def low_lk(i, c):
                        dve.wait_ge(l_h, 4 * i + c + 1)
                        dve.tensor_tensor(ll[:, c % 2, :], ps_main[:, c % 2, :], lh[:, c % 2, :].bitcast(F32),
                                          ALU.subtract).then_inc(mfree, 1)

                    def add_attention(i, c):
                        for dc in range(4):
                            dve.wait_ge(qful, Q * i + QY + 4 * c + dc + 1)
                            v = x1[:, 1 + 16 * c:17 + 16 * c, dc::4]
                            dve.tensor_tensor(v, v, ps_q[:, dc % 2, :].rearrange("p (n q) -> p n q", q=32),
                                              ALU.add).then_inc(qfree, 1)
                        dve.wait_ge(qfree, 2 + Q * i + QY + 4 * c + 4)
                        for k in range(4):
                            dve.bn_stats(stat[:, 4 * c + k, :],
                                         x1[:, 1 + 16 * c + 4 * k:5 + 16 * c + 4 * k, :].rearrange("p a b -> p (a b)")
                                         ).then_inc(bn, 1)

                    def y_norm(i, v):
                        dve.wait_ge(y_l, NW * i + v + 1)
                        dve.tensor_scalar(xn1[:, :, :], x1[:, bass.ds(4 * v, 6), :], m1[:, 0:1], m1[:, 1:2],
                                          ALU.subtract, ALU.mult).then_inc(y_n, 1)

                    def stage_c(i, v, h):
                        dve.wait_ge(main, MAIN * i + MC + v + 1)
                        dve.wait_ge(stored[h], 16 + 32 * (8 * i + v // 2))
                        o = ot[:, h, :, :]
                        dve.scalar_tensor_tensor(o.rearrange("p a b -> p (a b)"), ps_main[:, h, :], out_b[:, 0:1],
                                                 x1[:, bass.ds(4 * v + 1, 4), :].rearrange("p a b -> p (a b)"),
                                                 ALU.add, ALU.add).then_inc(mfree, 1)
                        dve.wait_ge(mfree, 2 + MAIN * i + MC + v + 1)
                        for first, r, pair in ((True, 0, 0), (False, 1, 3)):
                            if (is_first(v, 1) if first else is_last(v, 1)):
                                hp = par(r)
                                dve.tensor_tensor(o[hp, pair, :], o[hp, pair, :], edge[hp, 0:W],
                                                  ALU.subtract).then_inc(o_row, 1)
                                dve.wait_ge(o_row, 2 * i + r + 1)
                        e = edge[:, W:].rearrange("p (s n) -> p n s", s=2)[:, bass.ds(4 * v, 4), :]
                        dve.tensor_tensor(o[:, :, 0:W:W - 1], o[:, :, 0:W:W - 1], e, ALU.subtract).then_inc(o_done, 1)
                        if not is_last(v, 2):
                            y_norm(i, v + 2)

                    def body(i, last):
                        windows(dve, 0, lambda w, h: stage_a(i, w, h))
                        sums.start(i)
                        sums.done(dve.tensor_reduce(rsum[:, 0:1], rs[:, :], AX.X, ALU.add))
                        a_out(i, NW - 1, 1)
                        chain_dve(dve, i, (0,), pooled_s, chain, ker_s)
                        dve.wait_ge(ker_s, i + 1)
                        dyn.start(i)
                        dynamic_tiles(dve, dyn, kerr[:, 0, :])
                        dve.wait_ge(qfree, 2 + Q * i + QY)
                        low_lk(i, 0)
                        low_lk(i, 1)
                        add_attention(i, 0)
                        low_lk(i, 2)
                        add_attention(i, 1)
                        low_lk(i, 3)
                        add_attention(i, 2)
                        add_attention(i, 3)
                        dve.wait_ge(bn, 16 * (i + 1))
                        alone(dve)
                        stats.start(i)
                        group_stats_dve(dve, stats, lambda v: dve.wait_ge(avg, v), lambda v: dve.wait_ge(root, v),
                                        i, stat[:, :, :].rearrange("p a b -> p (a b)"), m1[:, 0:1], m1[:, 1:2])
                        stats.done(dve.tensor_scalar(x1[:, 0:NPAIR + 2:NPAIR + 1, :], zeros[:, :, :], m1[:, 0:1],
                                                     None, ALU.add))
                        stats.wait(dve)
                        y_norm(i, 0)
                        y_norm(i, 1)
                        stats.done(dve.tensor_scalar(colf[:, :, :].rearrange("p s n -> p n s"),
                                                     x1[:, :, 0:W:W - 1], m1[:, 0:1], m1[:, 1:2], ALU.subtract, ALU.mult))
                        for r, pair in ((0, 1), (1, NPAIR)):
                            hp = par(r)
                            ins = dve.tensor_scalar(rowf[hp, 2:2 + W], x1[hp, pair, :], m1[hp, 0:1], m1[hp, 1:2],
                                                    ALU.subtract, ALU.mult)
                            if r == 0:
                                ins.then_inc(e_in, 1)
                            else:
                                stats.done(ins)
                        dve.wait_ge(e_mm, i + 1)
                        dve.tensor_tensor(edge[:, :], ps_edge[:, 0:256], edge_b[:, :], ALU.add).then_inc(e_out, 1)
                        dve.wait_ge(e_out, i + 1)

                        def ahead():
                            dve.wait_ge(x_full, 16 + 32 * (NLOAD * i + 2))
                            first_norm(i + 1)

                        windows(dve, 0, lambda v, h: stage_c(i, v, h), {} if last else {
                            NW - 2: ahead, NW - 1: lambda: second_norm(i + 1)})

                    first_norm(0)
                    second_norm(0)
                    with dve.Fori(0, B - 1) as i:
                        body(i, False)
                    body(B - 1, True)

                @block.tensor
                def _(pe):
                    def conv3(i, w, h):
                        pe.wait_ge(x_l, NW * i + w + 2)
                        pe.wait_ge(mfree, MAIN * i + w + 1)
                        o = ps_main[:, h, :].rearrange("p (a b) -> p a b", b=W)
                        for blk in range(2):
                            for kx in range(3):
                                v = (slice(None), h, slice(blk, blk + 4), slice(kx, kx + W))
                                mm = product(pe, o, t3_h[:, blk, kx, :], t3_l[:, blk, kx, :], xh[v], xl[v],
                                             blk + kx == 0, blk + kx == 3)
                        mm.then_inc(main, 1)

                    def pointwise(i, w, h):
                        pe.wait_ge(r_l, NW * i + w + 2)
                        pe.wait_ge(qfree, Q * i + 2 * w + 1)
                        for dc in range(4):
                            v = (slice(None), h, slice(None), slice(dc, dc + 133, 4))
                            mm = product(pe, ps_q[:, 0, 0:136].rearrange("p (n q) -> p n q", q=34), fa_h[:, dc, :],
                                         fa_l[:, dc, :], rh[v], rl[v], dc == 0, dc == 3)
                        mm.then_inc(qful, 1)
                        pe.wait_ge(qfree, Q * i + 2 * w + 2)
                        v = (slice(None), h, slice(None), slice(2, 2 + W))
                        product(pe, ps_q[:, 1, :].rearrange("p (a b) -> p a b", b=W), idt_h[:, 0, :], idt_l[:, 0, :],
                                rh[v], rl[v], True, True).then_inc(qful, 1)

                    def stage_a(i, w, h):
                        conv3(i, w, h)
                        pointwise(i, w - 1, 1 - h)

                    def attention(i, c):
                        pe.wait_ge(mfree, 2 + MAIN * i + MB + c + 1)
                        for dc in range(4):
                            pe.wait_ge(qfree, Q * i + QY + 4 * c + dc + 1)
                            product(pe, ps_q[:, dc % 2, :], ga_h[:, dc, :], ga_l[:, dc, :], lh[:, c % 2, :],
                                    ll[:, c % 2, :], True, True).then_inc(qful, 1)

                    def conv5(i, v, h):
                        pe.wait_ge(y_l, NW * i + v + 2)
                        pe.wait_ge(mfree, MAIN * i + MC + v + 1)
                        o = ps_main[:, h, :].rearrange("p (a b) -> p a b", b=W)
                        for blk in range(3):
                            for kx in range(5):
                                a = (slice(None), h, slice(blk, blk + 4), slice(kx, kx + W))
                                mm = product(pe, o, c5_h[:, blk, kx, :], c5_l[:, blk, kx, :], yh[a], yl[a],
                                             blk + kx == 0, blk + kx == 6)
                        mm.then_inc(main, 1)

                    def body(i, last):
                        windows(pe, 1, lambda w, h: stage_a(i, w, h))
                        chain_pooled(pe, i, (0,), sums, chain)
                        pointwise(i, NW - 1, 1)
                        pe.wait_ge(f_z, 4 * (i + 1))
                        for c in range(4):
                            between = {}
                            if c == 0:
                                between = {4: lambda: chain_hidden(pe, i, 1, pooled_s, chain),
                                           9: lambda: chain_taps(pe, i, 1, hdn_s, chain),
                                           NSTAT: lambda: dyn.at(pe, i, DSTEPS)}
                            pe.wait_ge(mfree, MAIN * i + MB + c + 1)
                            large_filter(pe, ps_main[:, c % 2, :].rearrange("p (n q) -> p n q", q=32), fh, fl,
                                         16 * c, 16, 32, between).then_inc(main, 1)
                            if c > 0:
                                attention(i, c - 1)
                        attention(i, 3)
                        group_stats_pe(pe, stats, i, avg)
                        stats.at(pe, i, stats.per)
                        pe.wait_ge(e_in, i + 1)
                        alone(pe)
                        for kx in range(5):
                            for r in range(2):
                                hp = slice(r * C, r * C + C)
                                pe.matmul(ps_edge[hp, 0:W], row_w[hp, kx, :], rowf[hp, kx:kx + W], start=(kx == 0),
                                          stop=(kx == 4), skip_group_check=True)
                        for side in range(2):
                            c0 = W + side * NPAIR
                            for blk in range(3):
                                pe.matmul(ps_edge[:, c0:c0 + NPAIR], col_w[:, side, blk, :],
                                          colf[:, side, blk:blk + NPAIR], start=False, stop=False,
                                          skip_group_check=True)
                            for r, pair in ((0, 0), (1, NPAIR - 1)):
                                hp = par(r)
                                mm = pe.matmul(ps_edge[hp, c0 + pair:c0 + pair + 1], cor_w[hp, side, :],
                                               colf[hp, side, pair + 1:pair + 2], start=False, stop=True,
                                               skip_group_check=True)
                        mm.then_inc(e_mm, 1)
                        windows(pe, 0, lambda v, h: conv5(i, v, h))
                        if not last:
                            conv3(i + 1, 0, 0)

                    conv3(0, 0, 0)
                    with pe.Fori(0, B - 1) as i:
                        body(i, False)
                    body(B - 1, True)


def constants():
    tapmask = np.zeros((P, ND * 8, 9), np.float32)
    chmask = np.zeros((P, ATT), np.float32)
    slotmask = np.zeros((P, 8), np.float32)
    for dr, dc in PIX:
        s = slot(dr, dc)
        slotmask[s * ATT:s * ATT + ATT, s] = 1.0
        chmask[s * ATT:s * ATT + ATT] = np.eye(ATT)
        for t, (pb, cb) in enumerate(DYN):
            for er, ec in PIX:
                ky, kx = 2 * pb + dr - er - LK // 2 + 1, 4 * cb + dc - ec - LK // 2 + 1
                if 0 <= ky < 3 and 0 <= kx < 3:
                    tapmask[s * ATT:s * ATT + ATT, t * 8 + slot(er, ec), 3 * ky + kx] = 1.0
    ch = np.arange(P) % C // 2
    groupavg = (ch[:, None] == ch[None, :]).astype(np.float32) / 4
    return {"tapmask": tapmask, "chmask": chmask, "slotmask": slotmask, "groupavg": groupavg}


def kernel(x, L0_conv_ds_w3, L0_conv_ds_b3, L0_conv_ds_w1, L0_conv_ds_b1, L0_conv_kg_w1, L0_conv_kg_b1,
           L0_conv_kg_w2, L0_conv_kg_b2, L0_conv_lk_filter, L0_conv_fus_w, L0_conv_fus_b, L0_conv_fin_w,
           L0_conv_fin_b, L1_conv_w3, L1_conv_b3, L1_conv_w5, L1_conv_b5, L1_conv_wr, L1_conv_br):
    import concourse.bacc as bacc
    from concourse.bass_utils import run_bass_kernel_spmd

    a = np.asarray
    arrays = {
        "x": a(x),
        "w3t": a(L0_conv_ds_w3).transpose(0, 2, 3, 4, 1).reshape(LEVELS, C, 9, C),
        "w1t": a(L0_conv_ds_w1).transpose(0, 2, 1),
        "w1": a(L0_conv_ds_w1),
        "b3": a(L0_conv_ds_b3), "b1": a(L0_conv_ds_b1),
        "kgw1t": a(L0_conv_kg_w1).T, "kgb1": a(L0_conv_kg_b1),
        "kgw2": a(L0_conv_kg_w2).reshape(ATT, 9, ATT // 2).transpose(2, 1, 0),
        "kgb2": a(L0_conv_kg_b2).reshape(ATT, 9),
        "lkt": a(L0_conv_lk_filter).transpose(1, 2, 3, 0),
        "fus": a(L0_conv_fus_w), "fusb": a(L0_conv_fus_b),
        "fint": a(L0_conv_fin_w).T, "finb": a(L0_conv_fin_b),
        "c3t": a(L1_conv_w3).transpose(1, 2, 3, 0), "c5t": a(L1_conv_w5).transpose(1, 2, 3, 0),
        "c3b": a(L1_conv_b3), "c5b": a(L1_conv_b5),
        "wr": a(L1_conv_wr)[:, :, 0, 0], "wrt": a(L1_conv_wr)[:, :, 0, 0].T, "br": a(L1_conv_br),
        **constants(),
    }
    nc = bacc.Bacc("TRN2", target_bir_lowering=False, num_devices=1)
    feeds, aps = {}, {}
    for name, v in arrays.items():
        v = np.ascontiguousarray(v)
        feeds["in_" + name] = v
        aps[name] = nc.dram_tensor("in_" + name, v.shape, mybir.dt.from_np(v.dtype), kind="ExternalInput").ap()
    out = nc.dram_tensor("out_0", (B, C, H, W), F32, kind="ExternalOutput").ap()
    conv_kernel(nc, **aps, out=out)
    r = run_bass_kernel_spmd(nc, [feeds], core_ids=[0])
    return r.results[0]["out_0"]
```

```python
from contextlib import ExitStack

import numpy as np
import concourse.bass as bass
from concourse import mybir

F32 = mybir.dt.float32
F32R = mybir.dt.float32r
ALU = mybir.AluOpType
ACT = mybir.ActivationFunctionType
AX = mybir.AxisListType

P = 128
B, C, H, W = 8, 64, 128, 128
ATT = 16
NI = C - ATT
LK = 13
LEVELS = 4
EPS = 1e-5
NPAIR = H // 2
NPB, NCB = 7, 4
DYN = [(pb, cb) for pb in (2, 3, 4) for cb in (1, 2)]
ND = len(DYN)
NSTAT = NPB * NCB - ND
SIDE = {1: 64, 2: 32, 3: 16}
DIL = {1: 5, 2: 7, 3: 9}


def slot(dr, dc):
    return (dc // 2) * 4 + dr * 2 + dc % 2


def par(r):
    return slice((1 - r) * C, (2 - r) * C)


PIX = [(dr, dc) for dr in range(2) for dc in range(4)]


class Steps:

    def __init__(self, sem, per_image):
        self.sem, self.per, self.n = sem, per_image, 0

    def start(self, image):
        self.base, self.n = self.per * image, 0

    def done(self, ins):
        ins.then_inc(self.sem, 1)
        self.n += 1
        assert self.n <= self.per

    def wait(self, eng):
        eng.wait_ge(self.sem, self.base + self.n)

    def at(self, eng, image, n):
        eng.wait_ge(self.sem, self.per * image + n)


def conv_kernel(nc, x, w3t, w1t, w1, b3, b1, kgw1t, kgb1, kgw2, kgb2, lkt, fus, fusb, fint, finb,
                c3t, c5t, c3b, c5b, wr, wrt, br, tapmask, chmask, slotmask, groupavg, out):
    zs = nc.dram_tensor("z_level1", (B, C, NPAIR, W // 2), F32)
    zs2 = nc.dram_tensor("z_levels23", (B, C, H // 4, W // 4), F32)

    with ExitStack() as ctx:
        def sb(name, shape, dt=F32, stack=ctx):
            return stack.enter_context(nc.sbuf_tensor(name, shape, dt))

        def sem(name, stack=ctx):
            return stack.enter_context(nc.semaphore(name))

        def psum(name, shape):
            return ctx.enter_context(nc.psum_tensor(name, shape, F32))

        ps_main = psum("ps_main", [P, 2, 512])
        ps_q = psum("ps_q", [P, 2, 512])
        ps_stat = psum("ps_stat", [P, 512])
        ps_chain = psum("ps_chain", [P, 512])
        ps_edge = psum("ps_edge", [P, 512])
        ps_more = psum("ps_more", [P, 512])

        lk_h = sb("lk_h", [P, NPB, NCB, P], F32R)
        lk_l = sb("lk_l", [P, NPB, NCB, P], F32R)
        lk_base = sb("lk_base", [P, ND, P])
        idt_h = sb("idt_h", [P, LEVELS, P], F32R)
        idt_l = sb("idt_l", [P, LEVELS, P], F32R)
        gn0 = sb("gn0", [P, B, 2])
        gar = sb("gar", [P, C])
        w1a = sb("w1a", [P, LEVELS, ATT])
        b1a = sb("b1a", [P, LEVELS])
        b3p = sb("b3p", [P, LEVELS])
        kg1 = sb("kg1", [ATT, ATT // 2])
        kb1 = sb("kb1", [ATT // 2, 1])
        kg2 = sb("kg2", [ATT // 2, 9, P])
        kb2 = sb("kb2", [P, 9])
        tapm = sb("tapm", [P, ND * 8, 9])
        chm = sb("chm", [P, ATT])
        slm = sb("slm", [P, 8])
        gav = sb("gav", [P, P])
        bz = sb("bz", [P, 1])
        small = sb("small", [P, 64])
        dcoef = sb("dcoef", [P, ND * 8])
        dker = sb("dker", [P, ND * P])
        dtap = dker[:, 0:ND * 8 * 9].rearrange("p (m t) -> p m t", t=9)
        kerr = sb("kerr", [P, 4, 9])
        stat = sb("stat", [P, 16, 6])

        passed = sem("passed")

        def alone(eng):
            eng.sem_inc(passed, 1)

        with ExitStack() as st:
            s_ld = sem("s_ld", st)
            s_lks = sem("s_lks", st)
            s_zero = sem("s_zero", st)
            s_hi = sem("s_hi", st)
            s_lo = sem("s_lo", st)
            s_mm = sem("s_mm", st)
            s_cp = sem("s_cp", st)
            lks = sb("lks", [P, 14, 16, ATT], stack=st)
            fus_s = sb("fus_s", [C, C], stack=st)
            fus_r = sb("fus_r", [C, 8, ATT], stack=st)
            fin_s = sb("fin_s", [C, 2, C], stack=st)
            fusb_s = sb("fusb_s", [C, 1], stack=st)
            finb_s = sb("finb_s", [P, 1], stack=st)
            w1i = sb("w1i", [NI, LEVELS, 2, C], stack=st)
            b1i = sb("b1i", [NI, LEVELS], stack=st)
            gti = sb("gti", [NI, 2, C], stack=st)
            idt = sb("idt", [P, LEVELS, P], stack=st)
            b1t = b1.rearrange("l c -> c l")
            b3t = b3.rearrange("l c -> c l")
            loads = [(fus_s[:, :], fus), (fusb_s[:, :], fusb.rearrange("(c a) -> c a", a=1)),
                     (kg1[:, :], kgw1t), (kb1[:, :], kgb1.rearrange("(c a) -> c a", a=1)),
                     (tapm[:, :, :], tapmask), (chm[:, :], chmask), (slm[:, :], slotmask), (gav[:, :], groupavg),
                     (b1i[:, :], b1t[ATT:, :])]
            for r in range(2):
                hp = slice(r * C, r * C + C)
                loads += [(fin_s[:, r, :], fint), (w1i[:, :, r, :], w1.rearrange("l o c -> o l c")[ATT:, :, :]),
                          (w1a[hp, :, :], w1t.rearrange("l c o -> c l o")[:, :, 0:ATT]),
                          (finb_s[hp, :], finb.rearrange("(c a) -> c a", a=1)), (b3p[hp, :], b3t)]
            for s in range(8):
                sp16 = slice(s * ATT, s * ATT + ATT)
                loads += [(fus_r[:, s, :], fus[:, 0:ATT]), (b1a[sp16, :], b1t[0:ATT, :]),
                          (kb2[sp16, :], kgb2), (kg2[:, :, sp16], kgw2)]
            NLD = len(loads)
            pieces = [(pb, dr, dc) for pb in range(NPB) for dr, dc in PIX]

            with nc.Block() as block:
                @block.sync
                def _(sp):
                    with nc.allow_non_contiguous_dma(reason="small weight layouts"):
                        for d, s in loads:
                            sp.dma_start(d, s).then_inc(s_ld, 16)
                        sp.wait_ge(s_zero, 1)
                        for dr, dc in PIX:
                            q = slot(dr, dc) * ATT
                            sp.dma_start(lks[q:q + ATT, 1 - dr:14 - dr, 3 - dc:16 - dc, :], lkt).then_inc(s_lks, 16)

                @block.gpsimd
                def _(pool):
                    pool.memset(lks[:, :, :, :], 0.0).then_inc(s_zero, 1)
                    pool.memset(idt[:, :, :], 0.0).then_inc(s_zero, 1)

                @block.scalar
                def _(act):
                    act.wait_ge(s_lks, 16 * 8)
                    for pb, dr, dc in pieces:
                        src = lks[:, 2 * pb - dr + 1, 3 - dc:16 - dc:4, :]
                        q = slot(dr, dc) * ATT
                        act.activation(lk_h[:, pb, :, q:q + ATT], src, ACT.Identity).then_inc(s_hi, 1)

                @block.vector
                def _(dve):
                    dve.wait_ge(s_ld, 16 * NLD)
                    dve.wait_ge(s_lks, 16 * 8)
                    for k, (pb, dr, dc) in enumerate(pieces):
                        src = lks[:, 2 * pb - dr + 1, 3 - dc:16 - dc:4, :]
                        q = slot(dr, dc) * ATT
                        dve.wait_ge(s_hi, k + 1)
                        dve.tensor_tensor(lk_l[:, pb, :, q:q + ATT], src, lk_h[:, pb, :, q:q + ATT].bitcast(F32),
                                          ALU.subtract).then_inc(s_lo, 1)
                        if pb in (2, 3, 4):
                            t = (pb - 2) * 2
                            dve.tensor_copy(lk_base[:, t:t + 2, q:q + ATT], src[:, 1:3, :]).then_inc(s_lo, 1)
                    dve.wait_ge(s_mm, 1)
                    dve.tensor_copy(gti[:, :, :], ps_main[0:NI, 0, 0:P]).then_inc(s_cp, 1)
                    dve.tensor_copy(gar[:, :], ps_main[:, 0, P:P + C]).then_inc(s_cp, 1)
                    dve.wait_ge(s_mm, 2)
                    dve.wait_ge(s_zero, 2)
                    for r in range(2):
                        hp = slice(r * C, r * C + C)
                        dve.tensor_copy(idt[hp, :, r * C:r * C + C],
                                        ps_q[hp, 0, 0:LEVELS * C].rearrange("p (l o) -> p l o", o=C)).then_inc(s_cp, 1)
                    dve.tensor_tensor(bz[:, :], ps_q[:, 1, 0:1], finb_s[:, :], ALU.add).then_inc(s_cp, 1)
                    dve.wait_ge(s_cp, 5)
                    dve.tensor_copy(idt_h[:, :, :], idt[:, :, :]).then_inc(s_cp, 1)
                    dve.wait_ge(s_cp, 6)
                    dve.tensor_tensor(idt_l[:, :, :], idt[:, :, :], idt_h[:, :, :].bitcast(F32),
                                      ALU.subtract).then_inc(s_cp, 1)

                @block.tensor
                def _(pe):
                    pe.wait_ge(s_ld, 16 * NLD)
                    pe.matmul(ps_main[0:NI, 0, 0:P], fus_s[:, ATT:C], fin_s[:, :, :], start=True, stop=True)
                    pe.matmul(ps_main[:, 0, P:P + C], fus_r[:, :, :], fin_s[:, 0, :], start=True,
                              stop=True, skip_group_check=True).then_inc(s_mm, 1)
                    pe.wait_ge(s_cp, 2)
                    for lv in range(LEVELS):
                        pe.matmul(ps_q[:, 0, lv * C:lv * C + C], w1i[:, lv, :, :], gti[:, 0, :],
                                  start=(lv == 0), stop=True, skip_group_check=True)
                    for lv in range(LEVELS):
                        pe.matmul(ps_q[:, 1, 0:1], gti[:, :, :], b1i[:, lv:lv + 1], start=(lv == 0), stop=False)
                    for lv in range(LEVELS):
                        mm = pe.matmul(ps_q[:, 1, 0:1], fin_s[:, :, :], fusb_s[:, :], start=False,
                                       stop=(lv == LEVELS - 1))
                    mm.then_inc(s_mm, 1)

        def product(pe, o, wh, wl, xh, xl, first, last):
            pe.matmul(o, wh, xh, start=first, stop=False, skip_group_check=True)
            pe.matmul(o, wh, xl, start=False, stop=False, skip_group_check=True)
            return pe.matmul(o, wl, xh, start=False, stop=last, skip_group_check=True)

        def large_filter(pe, o, fh, fl, p0, np_, nq, between):
            tiles = [(pb, cb) for pb in range(NPB) for cb in range(NCB) if (pb, cb) not in DYN] + DYN
            for k, (pb, cb) in enumerate(tiles):
                if k in between:
                    between[k]()
                v = (slice(None), slice(p0 + pb, p0 + pb + np_), slice(cb, cb + nq))
                mm = product(pe, o, lk_h[:, pb, cb, :], lk_l[:, pb, cb, :], fh[v], fl[v],
                             k == 0, k == len(tiles) - 1)
            return mm

        def lk_mid(t):
            return t[:, 2:5, 1:3, :].rearrange("p b c m -> p b (c m)")

        def dynamic_tiles(dve, steps, ker, hi, lo):
            steps.done(dve.tensor_tensor(dtap[:, :, :], tapm[:, :, :],
                                         ker.unsqueeze(1).to_broadcast([P, ND * 8, 9]), ALU.mult))
            steps.wait(dve)
            steps.done(dve.tensor_reduce(dcoef[:, :], dtap[:, :, :], AX.X, ALU.add))
            steps.wait(dve)
            steps.done(dve.tensor_tensor(dker[:, :].rearrange("p (m c) -> p m c", c=ATT),
                                         dcoef[:, :].unsqueeze(2).to_broadcast([P, ND * 8, ATT]),
                                         chm[:, :].unsqueeze(1).to_broadcast([P, ND * 8, ATT]), ALU.mult))
            steps.wait(dve)
            steps.done(dve.tensor_tensor(dker[:, :], dker[:, :], lk_base[:, :, :].rearrange("p t m -> p (t m)"),
                                         ALU.add))
            steps.wait(dve)
            dk = dker[:, :].rearrange("p (b m) -> p b m", b=3)
            steps.done(dve.tensor_copy(hi, dk))
            steps.wait(dve)
            steps.done(dve.tensor_tensor(lo, dk, hi.bitcast(F32), ALU.subtract))
        DSTEPS = 6

        def group_stats_dve(dve, steps, averaged, rooted, image, entries, mean, rstd):
            mv, dm, tv, vv, sd = (small[:, 0:2], small[:, 2:3], small[:, 3:4], small[:, 4:5], small[:, 5:6])
            steps.done(dve.bn_aggr(mv, entries))
            averaged(2 * image + 1)
            steps.done(dve.tensor_copy(mean, ps_stat[:, 0:1]))
            steps.wait(dve)
            steps.done(dve.tensor_tensor(dm, mv[:, 0:1], mean, ALU.subtract))
            steps.wait(dve)
            steps.done(dve.scalar_tensor_tensor(tv, dm, dm, mv[:, 1:2], ALU.mult, ALU.add))
            averaged(2 * image + 2)
            steps.done(dve.tensor_scalar(vv, ps_stat[:, 1:2], EPS, None, ALU.add))
            rooted(image + 1)
            steps.done(dve.reciprocal(rstd, sd))
            steps.wait(dve)
        GSTEPS = 6

        def group_mean_pe(pe, steps, image, s_avg):
            steps.at(pe, image, 1)
            pe.matmul(ps_stat[:, 0:1], gav[:, :], small[:, 0:1], start=True, stop=True,
                      skip_group_check=True).then_inc(s_avg, 1)

        def group_var_pe(pe, steps, image, s_avg):
            steps.at(pe, image, 4)
            pe.matmul(ps_stat[:, 1:2], gav[:, :], small[:, 3:4], start=True, stop=True,
                      skip_group_check=True).then_inc(s_avg, 1)

        def group_stats_act(act, steps, image, s_root):
            steps.at(act, image, 5)
            act.activation(small[:, 5:6], small[:, 4:5], ACT.Sqrt).then_inc(s_root, 1)

        def chain_pooled(pe, image, parts, s_sum, s_chain):
            if s_sum is not None:
                s_sum.at(pe, image, s_sum.per)
            k = 0
            for lv, n in parts:
                mm = pe.matmul(ps_chain[0:ATT, k:k + n], w1a[:, lv, :], rsum[:, k:k + n], start=(k == 0),
                               stop=True, skip_group_check=True)
                k += n
            mm.then_inc(s_chain, 1)

        def chain_hidden(pe, image, n, nparts, s_pooled, s_chain):
            pe.wait_ge(s_pooled, nparts * (image + 1))
            alone(pe)
            pe.matmul(ps_chain[0:ATT // 2, 8:8 + n], kg1[:, :], pooled[:, 0:n], start=True, stop=True,
                      skip_group_check=True).then_inc(s_chain, 1)

        def chain_taps(pe, image, n, s_hdn, s_chain):
            pe.wait_ge(s_hdn, image + 1)
            for t in range(9):
                mm = pe.matmul(ps_chain[:, 16 + n * t:16 + n * t + n], kg2[:, t, :], hdn[:, 0:n],
                               start=(t == 0), stop=True, skip_group_check=True)
            mm.then_inc(s_chain, 1)

        def chain_pooled_dve(dve, image, parts, s_pooled, s_chain):
            dve.wait_ge(s_chain, 3 * image + 1)
            k = 0
            for lv, n in parts:
                side = SIDE.get(lv, H)
                dve.tensor_scalar(pooled[:, k:k + n], ps_chain[0:ATT, k:k + n], 1.0 / (side * side),
                                  b1a[0:ATT, lv:lv + 1], ALU.mult, ALU.add).then_inc(s_pooled, 1)
                k += n

        def chain_taps_dve(dve, image, n, s_chain, s_ker):
            dve.wait_ge(s_chain, 3 * image + 3)
            dve.tensor_tensor(kerr[:, 0:n, :], ps_chain[:, 16:16 + 9 * n].rearrange("p (t k) -> p k t", k=n),
                              kb2[:, :].unsqueeze(1).to_broadcast([P, n, 9]), ALU.add).then_inc(s_ker, 1)

        def chain_act(act, image, n, s_chain, s_hdn):
            act.wait_ge(s_chain, 3 * image + 2)
            act.activation(hdn[:, 0:n], ps_chain[0:ATT // 2, 8:8 + n], ACT.Gelu, bias=kb1[:, 0:1]).then_inc(s_hdn, 1)

        rsum = sb("rsum", [P, 4])
        pooled = sb("pooled", [ATT, 4])
        hdn = sb("hdn", [ATT // 2, 4])

        st1 = ctx.enter_context(ExitStack())
        half = {lv: SIDE[lv] // 2 for lv in SIDE}
        prow = {lv: half[lv] + 2 * DIL[lv] for lv in SIDE}
        plen = {lv: SIDE[lv] + DIL[lv] + (SIDE[lv] + DIL[lv]) % 2 for lv in SIDE}
        p2 = sb("p2", [P, B, half[2], SIDE[2]], stack=st1)
        w3h = sb("w3h", [P, 3, 9, P], F32R, stack=st1)
        w3l = sb("w3l", [P, 3, 9, P], F32R, stack=st1)
        fa_h = sb("fa_h", [P, 3, 240], F32R, stack=st1)
        fa_l = sb("fa_l", [P, 3, 240], F32R, stack=st1)
        ga_h = sb("ga_h", [P, 8 * P + C], F32R, stack=st1)
        ga_l = sb("ga_l", [P, 8 * P + C], F32R, stack=st1)

        def quad_sum(pool, dst, v, s_acc, count):
            alone(pool)
            pool.tensor_tensor(dst, v(0, 0), v(0, 1), ALU.add).then_inc(s_acc, 1)
            pool.wait_ge(s_acc, count + 1)
            alone(pool)
            pool.tensor_tensor(dst, dst, v(1, 0), ALU.add).then_inc(s_acc, 1)
            pool.wait_ge(s_acc, count + 2)
            alone(pool)
            return pool.tensor_tensor(dst, dst, v(1, 1), ALU.add)

        with ExitStack() as st:
            def s1(name):
                return sem("p1_" + name, st)

            D1, S1, N1 = DIL[1], SIDE[1], half[1]
            NB1, NQ1 = N1 // 2, S1 // 4
            LEN1 = prow[1] * plen[1] + 2 * D1
            xc = sb("xc", [P, 2, 8, W], stack=st)
            pl1 = sb("pl1", [P, prow[1], S1], stack=st)
            nh = sb("nh1", [P, LEN1], F32R, stack=st)
            nl = sb("nl1", [P, LEN1], F32R, stack=st)
            rf = sb("rf1", [P, 2, 512], stack=st)
            rh = sb("rh1", [P, N1, S1 + 8], F32R, stack=st)
            rl = sb("rl1", [P, N1, S1 + 8], F32R, stack=st)
            fh = sb("fh1", [P, N1 + 6, NQ1 + 4], F32R, stack=st)
            fl = sb("fl1", [P, N1 + 6, NQ1 + 4], F32R, stack=st)
            z1 = sb("z1", [P, N1, S1], stack=st)
            lh = sb("lh1", [P, 512], F32R, stack=st)
            ll = sb("ll1", [P, 512], F32R, stack=st)
            rs = sb("rs1", [P, 4], stack=st)
            coef = sb("coef1", [P, 2], stack=st)
            zeros = sb("zeros1", [P, D1 * S1], stack=st)

            with ExitStack() as se:
                stage = sb("stage", [P, 9, P], stack=se)
                gst = sb("gst", [P, C], stack=se)
                a_z = sem("a_z", se)
                a_ld = sem("a_ld", se)
                a_s = sem("a_s", se)
                a_p = sem("a_p", se)
                a_b = sem("a_b", se)
                a_g = sem("a_g", se)
                with nc.Block() as block:
                    @block.gpsimd
                    def _(pool):
                        for t in (nh, nl):
                            pool.memset(t[:, :].bitcast(F32), 0.0).then_inc(a_p, 1)
                        for t in (rh, rl, fh, fl):
                            pool.memset(t[:, :, :].bitcast(F32), 0.0).then_inc(a_p, 1)
                        pool.memset(zeros[:, :], 0.0).then_inc(a_p, 1)

                    @block.sync
                    def _(sp):
                        sp.wait_ge(a_z, 1)
                        for k in range(3):
                            if k > 0:
                                sp.wait_ge(a_s, 2 * k)
                            for r in range(2):
                                hp = slice(r * C, r * C + C)
                                sp.dma_start(stage[hp, :, hp], w3t[k + 1]).then_inc(a_ld, 16)

                    @block.vector
                    def _(dve):
                        dve.memset(stage[:, :, :], 0.0).then_inc(a_z, 1)
                        dve.memset(fa_h[:, :, :].bitcast(F32), 0.0).then_inc(a_b, 1)
                        dve.memset(fa_l[:, :, :].bitcast(F32), 0.0).then_inc(a_b, 1)
                        dve.memset(ga_h[:, :].bitcast(F32), 0.0).then_inc(a_b, 1)
                        dve.memset(ga_l[:, :].bitcast(F32), 0.0).then_inc(a_b, 1)
                        dve.wait_ge(a_b, 4)
                        n = 0
                        for k in range(3):
                            dve.tensor_copy(fa_h[:, k, 112:128], w1a[:, k + 1, :]).then_inc(a_g, 1)
                            n += 1
                            dve.wait_ge(a_g, n)
                            dve.tensor_tensor(fa_l[:, k, 112:128], w1a[:, k + 1, :],
                                              fa_h[:, k, 112:128].bitcast(F32), ALU.subtract).then_inc(a_b, 1)
                        for s in range(8):
                            o = slice(s * P + C, s * P + P)
                            dve.tensor_scalar(gst[:, :], gar[:, :], slm[:, s:s + 1], None, ALU.mult).then_inc(a_g, 1)
                            dve.wait_ge(a_g, n + 1)
                            dve.tensor_copy(ga_h[:, o], gst[:, :]).then_inc(a_g, 1)
                            dve.wait_ge(a_g, n + 2)
                            dve.tensor_tensor(ga_l[:, o], gst[:, :], ga_h[:, o].bitcast(F32),
                                              ALU.subtract).then_inc(a_g, 1)
                            n += 3
                            dve.wait_ge(a_g, n)
                        for k in range(3):
                            dve.wait_ge(a_ld, 32 * (k + 1))
                            dve.tensor_copy(w3h[:, k, :, :], stage[:, :, :]).then_inc(a_s, 1)
                            dve.wait_ge(a_s, 2 * k + 1)
                            dve.tensor_tensor(w3l[:, k, :, :], stage[:, :, :], w3h[:, k, :, :].bitcast(F32),
                                              ALU.subtract).then_inc(a_s, 1)

            NX = 8
            NCH = S1 // 16
            Q = 2 + 8
            pieces = [(0, 8 + 2 * D1)] + [(8 * k + 2 * D1, 8 * k + 8 + 2 * D1) for k in range(1, NCH)]
            xc_full = [s1("xc_full0"), s1("xc_full1")]
            bn_done = s1("bn_done")
            pl_done = s1("pl_done")
            p_acc = s1("p_acc")
            p2_done = s1("p2_done")
            halo = s1("halo")
            stats = Steps(s1("stats"), GSTEPS + 4)
            avg, root = s1("avg"), s1("root")
            n_f = s1("n_f")
            n_h = s1("n_h")
            n_l = s1("n_l")
            main = s1("main")
            mfree = s1("mfree")
            qful, qfree = s1("qful"), s1("qfree")
            r_h = s1("r_h")
            r_l = s1("r_l")
            f_h = s1("f_h")
            f_z = s1("f_z")
            sums = Steps(s1("sums"), 1)
            pooled_s, chain, hdn_s, ker_s = s1("pooled"), s1("chain"), s1("hdn"), s1("ker")
            dyn = Steps(s1("dyn"), DSTEPS)
            lk_f = s1("lk_f")
            l_h = s1("l_h")
            l_l = s1("l_l")
            zst = s1("zst")
            ps_lk = ps_edge

            def nview(a, r0, r1):
                return a[:, D1:D1 + prow[1] * plen[1]].rearrange("p (r c) -> p r c", c=plen[1])[:, r0:r1, 0:S1]

            def prep_at(k, last):
                return [] if last else [(0, 1), (2, 3), (4, 5), ()][k]

            with nc.Block() as block:
                @block.sync
                def _(sp):
                    sp.sem_inc(bn_done, 4)
                    sp.sem_inc(pl_done, 2)
                    sp.sem_inc(mfree, 2)
                    sp.sem_inc(qfree, 2)
                    sp.sem_inc(r_l, 2)
                    sp.sem_inc(l_l, 1)
                    sp.sem_inc(zst, 16)

                    def prep(i):
                        with sp.Fori(0, NX // 2) as t:
                            for h in range(2):
                                sp.wait_ge(bn_done, 2 * (NX * i + 2 * t + h + 1))
                                sp.wait_ge(pl_done, NX * i + 2 * t + h + 1)
                                for r in range(2):
                                    sp.dma_start(xc[r * C:r * C + C, h, :, :],
                                                 x[i, :, bass.ds(t * 16 + (8 * h + r * (H // 2)), 8), :]
                                                 ).then_inc(xc_full[h], 16)
                        sp.wait_ge(pl_done, 2 + NX * (i + 1))
                        alone(sp)
                        sp.dma_start(pl1[0:C, D1 + N1:N1 + 2 * D1, :], pl1[C:P, D1:2 * D1, :]).then_inc(halo, 16)
                        sp.dma_start(pl1[C:P, 0:D1, :], pl1[0:C, N1:D1 + N1, :]).then_inc(halo, 16)

                    def store(i):
                        sp.wait_ge(qfree, 2 + Q * (i + 1))
                        alone(sp)
                        for r in range(2):
                            sp.dma_start(zs.ap()[i, :, N1 * r:N1 * r + N1, :],
                                         z1[r * C:r * C + C, :, :]).then_inc(zst, 16)

                    prep(0)
                    with sp.Fori(0, B - 1) as i:
                        prep(i + 1)
                        store(i)
                    store(B - 1)
                    sp.wait_ge(zst, 16 + 32 * B)

                @block.gpsimd
                def _(pool):
                    def prep_chunk(i, c):
                        pool.wait_ge(xc_full[c % 2], 32 * (NX // 2 * i + c // 2 + 1))
                        v = xc[:, c % 2, :, :].rearrange("p (r a) (c b) -> p r a c b", a=2, b=2)
                        quad_sum(pool, pl1[:, D1 + 4 * c:D1 + 4 * c + 4, :], lambda a, b: v[:, :, a, :, b], p_acc,
                                 i * (2 * NX + 2) + 2 * c).then_inc(pl_done, 1)

                    def prep_rest(i):
                        pool.wait_ge(pl_done, 2 + NX * (i + 1))
                        v = pl1[:, D1:D1 + N1, :].rearrange("p (r a) (c b) -> p r a c b", a=2, b=2)
                        quad_sum(pool, p2[:, bass.ds(i, 1), :, :].rearrange("p i r c -> p (i r) c"),
                                 lambda a, b: v[:, :, a, :, b], p_acc, i * (2 * NX + 2) + 2 * NX).then_inc(p2_done, 1)

                    def norm(i):
                        for k, (r0, r1) in enumerate(pieces):
                            pool.wait_ge(n_h, NCH * i + k + 1)
                            pool.tensor_tensor(nview(nl, r0, r1), pl1[:, r0:r1, :], nview(nh, r0, r1).bitcast(F32),
                                               ALU.subtract).then_inc(n_l, 1)

                    def body(i, last):
                        pool.wait_ge(n_l, NCH * (i + 1))
                        alone(pool)
                        for k in range(NCH):
                            pool.wait_ge(r_h, NCH * i + k + 1)
                            r = slice(8 * k, 8 * k + 8)
                            pool.tensor_tensor(rl[:, r, 2:2 + S1],
                                               rf[:, k % 2, :].rearrange("p (r c) -> p r c", c=S1),
                                               rh[:, r, 2:2 + S1].bitcast(F32), ALU.subtract).then_inc(r_l, 1)
                            for c in prep_at(k, last):
                                prep_chunk(i + 1, c)
                        pool.wait_ge(qfree, 2 + Q * i + 2)
                        alone(pool)
                        for t in (fh, fl):
                            pool.memset(t[0:C, 3:3 + N1, 1:2].bitcast(F32), 0.0).then_inc(f_z, 1)
                            pool.memset(t[C:P, 3:3 + N1, 1 + NQ1:2 + NQ1].bitcast(F32), 0.0).then_inc(f_z, 1)
                        pool.wait_ge(f_z, 4 * (i + 1))
                        alone(pool)
                        if not last:
                            for c in (NX - 2, NX - 1):
                                prep_chunk(i + 1, c)
                            prep_rest(i + 1)
                            norm(i + 1)

                    for c in range(NX):
                        prep_chunk(0, c)
                    prep_rest(0)
                    norm(0)
                    with pool.Fori(0, B - 1) as i:
                        body(i, False)
                    body(B - 1, True)

                @block.scalar
                def _(act):
                    def norm(i, k):
                        r0, r1 = pieces[k]
                        act.wait_ge(n_f, NCH * i + k + 1)
                        act.activation(nview(nh, r0, r1), pl1[:, r0:r1, :], ACT.Identity).then_inc(n_h, 1)

                    def body(i, last):
                        for k in range(NCH):
                            act.wait_ge(main, NCH * i + k + 1)
                            act.wait_ge(r_l, NCH * i + k + 1)
                            act.activation(rf[:, k % 2, :], ps_main[:, k % 2, :], ACT.Relu,
                                           bias=b3p[:, 1:2], accum_out=rs[:, k:k + 1]).then_inc(mfree, 1)
                        for hf in range(2):
                            act.wait_ge(qful, Q * i + hf + 1)
                            p0 = 3 + NB1 * hf
                            ps = ps_q[:, hf, 0:NB1 * (NQ1 + 2)].rearrange("p (n q) -> p n q", q=NQ1 + 2)
                            act.activation(fh[:, p0:p0 + NB1, 1:NQ1 + 2], ps[:, :, 0:NQ1 + 1], ACT.Identity,
                                           bias=b1a[:, 1:2]).then_inc(f_h, 1)
                        chain_act(act, i, 1, chain, hdn_s)
                        if not last:
                            group_stats_act(act, stats, i + 1, root)
                            norm(i + 1, 0)
                            norm(i + 1, 1)
                        act.wait_ge(lk_f, i + 1)
                        act.activation(lh[:, :], ps_lk[:, :], ACT.Identity).then_inc(l_h, 1)
                        if not last:
                            norm(i + 1, 2)
                            norm(i + 1, 3)

                    group_stats_act(act, stats, 0, root)
                    for k in range(NCH):
                        norm(0, k)
                    with act.Fori(0, B - 1) as i:
                        body(i, False)
                    body(B - 1, True)

                @block.vector
                def _(dve):
                    def prep_chunk(i, c):
                        dve.wait_ge(xc_full[c % 2], 32 * (NX // 2 * i + c // 2 + 1))
                        for e in range(2):
                            dve.bn_stats(stat[:, 2 * c + e, :],
                                         xc[:, c % 2, 4 * e:4 * e + 4, :].rearrange("p a b -> p (a b)")).then_inc(bn_done, 1)

                    def prep_rest(i):
                        dve.wait_ge(bn_done, 4 + 2 * NX * (i + 1))
                        alone(dve)
                        stats.start(i)
                        mean, rstd = gn0[:, bass.ds(i, 1), 0], gn0[:, bass.ds(i, 1), 1]
                        group_stats_dve(dve, stats, lambda v: dve.wait_ge(avg, v), lambda v: dve.wait_ge(root, v),
                                        i, stat[:, :, :].rearrange("p a b -> p (a b)"), mean, rstd)
                        k2 = float((H // S1) ** 2)
                        stats.done(dve.tensor_scalar(coef[:, 0:1], mean, k2, None, ALU.mult))
                        stats.done(dve.tensor_scalar(coef[:, 1:2], rstd, 1.0 / k2, None, ALU.mult))
                        stats.wait(dve)
                        for hf, r0 in ((0, 0), (1, D1 + N1)):
                            hp = slice(hf * C, hf * C + C)
                            stats.done(dve.tensor_scalar(pl1[hp, r0:r0 + D1, :].rearrange("p a b -> p (a b)"),
                                                         zeros[hp, :], coef[hp, 0:1], None, ALU.add))
                        stats.wait(dve)
                        dve.wait_ge(halo, 32 * (i + 1))
                        dve.wait_ge(p2_done, i + 1)

                    def norm(i, k):
                        r0, r1 = pieces[k]
                        dve.tensor_scalar(pl1[:, r0:r1, :], pl1[:, r0:r1, :], coef[:, 0:1], coef[:, 1:2],
                                          ALU.subtract, ALU.mult).then_inc(n_f, 1)

                    def body(i, last):
                        for k in range(NCH):
                            dve.wait_ge(mfree, 2 + NCH * i + k + 1)
                            dve.tensor_copy(rh[:, 8 * k:8 * k + 8, 2:2 + S1],
                                            rf[:, k % 2, :].rearrange("p (r c) -> p r c", c=S1)).then_inc(r_h, 1)
                            for c in prep_at(k, last):
                                prep_chunk(i + 1, c)
                        sums.start(i)
                        sums.done(dve.tensor_reduce(rsum[:, 0:1], rs[:, :], AX.X, ALU.add))
                        for hf in range(2):
                            dve.wait_ge(f_h, 2 * i + hf + 1)
                            p0 = 3 + NB1 * hf
                            ps = ps_q[:, hf, 0:NB1 * (NQ1 + 2)].rearrange("p (n q) -> p n q", q=NQ1 + 2)
                            dve.scalar_tensor_tensor(fl[:, p0:p0 + NB1, 1:NQ1 + 2], ps[:, :, 0:NQ1 + 1],
                                                     b1a[:, 1:2], fh[:, p0:p0 + NB1, 1:NQ1 + 2].bitcast(F32),
                                                     ALU.add, ALU.subtract).then_inc(qfree, 1)
                        chain_pooled_dve(dve, i, ((1, 1),), pooled_s, chain)
                        if not last:
                            for c in (NX - 2, NX - 1):
                                prep_chunk(i + 1, c)
                        chain_taps_dve(dve, i, 1, chain, ker_s)
                        dve.wait_ge(ker_s, i + 1)
                        dyn.start(i)
                        dynamic_tiles(dve, dyn, kerr[:, 0, :], lk_mid(lk_h), lk_mid(lk_l))
                        if not last:
                            dve.wait_ge(n_l, NCH * (i + 1))
                            alone(dve)
                            prep_rest(i + 1)
                            norm(i + 1, 0)
                            norm(i + 1, 1)
                        dve.wait_ge(l_h, i + 1)
                        dve.tensor_tensor(ll[:, :], ps_lk[:, :], lh[:, :].bitcast(F32), ALU.subtract).then_inc(l_l, 1)
                        if not last:
                            norm(i + 1, 2)
                            norm(i + 1, 3)
                        dve.wait_ge(zst, 16 + 32 * i)
                        for p, (dr, dc) in enumerate(PIX):
                            dve.wait_ge(qful, Q * i + 2 + p + 1)
                            dve.tensor_copy(z1[:, dr::2, dc::4],
                                            ps_q[:, p % 2, 0:NB1 * NQ1].rearrange("p (n q) -> p n q", q=NQ1)
                                            ).then_inc(qfree, 1)

                    for c in range(NX):
                        prep_chunk(0, c)
                    prep_rest(0)
                    for k in range(NCH):
                        norm(0, k)
                    with dve.Fori(0, B - 1) as i:
                        body(i, False)
                    body(B - 1, True)

                @block.tensor
                def _(pe):
                    def body(i, last):
                        for k in range(NCH):
                            pe.wait_ge(n_l, NCH * i + k + 1)
                            pe.wait_ge(mfree, NCH * i + k + 1)
                            for t in range(9):
                                o0 = (8 * k + (t // 3) * D1) * plen[1] + (t % 3) * D1
                                vh, vl = (a[:, o0:o0 + 8 * plen[1]].rearrange("p (r c) -> p r c", c=plen[1])
                                          [:, :, 0:S1] for a in (nh, nl))
                                mm = product(pe, ps_main[:, k % 2, :].rearrange("p (r c) -> p r c", c=S1),
                                             w3h[:, 0, t, :], w3l[:, 0, t, :], vh, vl, t == 0, t == 8)
                            mm.then_inc(main, 1)
                        pe.wait_ge(r_l, 2 + NCH * (i + 1))
                        chain_pooled(pe, i, ((1, 1),), sums, chain)
                        pe.wait_ge(qfree, Q * i + 2)
                        for j, (dr, dc) in enumerate(PIX):
                            a = 112 - ATT * slot(dr, dc)
                            for hf in range(2):
                                v = (slice(hf * C, hf * C + C), slice(dr, None, 2), slice(dc, dc + 4 * NQ1 + 5, 4))
                                w = (v[0], 0, slice(a, a + P))
                                mm = product(pe, ps_q[:, hf, 0:NB1 * (NQ1 + 2)].rearrange("p (n q) -> p n q", q=NQ1 + 2),
                                             fa_h[w], fa_l[w], rh[v], rl[v], j == 0, j == 7)
                                if j == 7:
                                    mm.then_inc(qful, 1)
                        pe.wait_ge(f_z, 4 * (i + 1))
                        pe.wait_ge(l_l, i + 1)
                        between = {4: lambda: chain_hidden(pe, i, 1, 1, pooled_s, chain),
                                   10: lambda: chain_taps(pe, i, 1, hdn_s, chain),
                                   NSTAT: lambda: dyn.at(pe, i, DSTEPS)}
                        if not last:
                            between[NSTAT + 1] = lambda: group_mean_pe(pe, stats, i + 1, avg)
                            between[NSTAT + 4] = lambda: group_var_pe(pe, stats, i + 1, avg)
                        large_filter(pe, ps_lk[:, :].rearrange("p (n q) -> p n q", q=NQ1), fh, fl, 0, N1, NQ1,
                                     between).then_inc(lk_f, 1)
                        pe.wait_ge(l_l, i + 2)
                        for p, (dr, dc) in enumerate(PIX):
                            pe.wait_ge(qfree, Q * i + 2 + p + 1)
                            o = ps_q[:, p % 2, 0:NB1 * NQ1]
                            v = (slice(None), slice(dr, None, 2), slice(2 + dc, 2 + dc + 4 * NQ1 - 3, 4))
                            product(pe, o.rearrange("p (n q) -> p n q", q=NQ1), idt_h[:, 1, :], idt_l[:, 1, :],
                                    rh[v], rl[v], True, False)
                            for hf in range(2):
                                g = slice(slot(dr, dc) * P + C * (1 - hf), slot(dr, dc) * P + C * (1 - hf) + P)
                                m = slice(hf * NB1 * NQ1, (hf + 1) * NB1 * NQ1)
                                mm = product(pe, o, ga_h[:, g], ga_l[:, g], lh[:, m], ll[:, m], False, hf == 1)
                            mm.then_inc(qful, 1)

                    group_mean_pe(pe, stats, 0, avg)
                    group_var_pe(pe, stats, 0, avg)
                    with pe.Fori(0, B - 1) as i:
                        body(i, False)
                    body(B - 1, True)

        G = 2
        NG = B // G
        with ExitStack() as st:
            def s1(name):
                return sem("pb_" + name, st)

            order = (3, 2)
            NB = {lv: half[lv] // 2 for lv in order}
            NQ = {lv: SIDE[lv] // 4 for lv in order}
            NBQ = {lv: 2 * NB[lv] * NQ[lv] for lv in order}
            LEN = {lv: prow[lv] * plen[lv] + 2 * DIL[lv] for lv in order}
            pl = {lv: sb(f"pl{lv}", [P, G, prow[lv], SIDE[lv]], stack=st) for lv in order}
            nh = {lv: sb(f"nh{lv}", [P, G, LEN[lv]], F32R, stack=st) for lv in order}
            nl = {lv: sb(f"nl{lv}", [P, G, LEN[lv]], F32R, stack=st) for lv in order}
            rh = {lv: sb(f"rh{lv}", [P, G, half[lv], SIDE[lv] + 8], F32R, stack=st) for lv in order}
            rl = {lv: sb(f"rl{lv}", [P, G, half[lv], SIDE[lv] + 8], F32R, stack=st) for lv in order}
            fh = {lv: sb(f"fh{lv}", [P, G, half[lv] + 6, NQ[lv] + 4], F32R, stack=st) for lv in order}
            fl = {lv: sb(f"fl{lv}", [P, G, half[lv] + 6, NQ[lv] + 4], F32R, stack=st) for lv in order}
            z = {lv: sb(f"z{lv}", [P, G, half[lv], SIDE[lv]], stack=st) for lv in order}
            lh = {lv: sb(f"lh{lv}", [P, G, NBQ[lv]], F32R, stack=st) for lv in order}
            ll = {lv: sb(f"ll{lv}", [P, G, NBQ[lv]], F32R, stack=st) for lv in order}
            dt_h = sb("dt_h", [P, 2 * G - 1, ND, P], F32R, stack=st)
            dt_l = sb("dt_l", [P, 2 * G - 1, ND, P], F32R, stack=st)
            rf = sb("rfb", [P, 3, 512], stack=st)
            coefs = sb("coefs", [P, 2, 2, B], stack=st)
            cg = sb("cg", [P, 2, 2, G], stack=st)

            items = [(lv, j) for lv in order for j in range(G)]
            NI1 = len(items)
            convs = [(3, None, ps_stat[:, 0:G * half[3] * SIDE[3]])] + [(2, j, ps_main[:, j, :]) for j in range(G)]
            relus = [(0, slice(j * 128, j * 128 + 128)) for j in range(G)] + [(1 + j, slice(0, 512)) for j in range(G)]
            Q = 4 + 16
            ps_lk = {3: ps_edge, 2: ps_more}

            cf_s = s1("cf")
            p_acc = s1("p_acc")
            zero = s1("zero")
            cg_s = s1("cg_s")
            s3 = s1("s3")
            n_i = s1("n_i")
            halo = {lv: s1(f"halo{lv}") for lv in order}
            n_h, n_l = s1("n_h"), s1("n_l")
            main = s1("main")
            mfree = s1("mfree")
            r_h = s1("r_h")
            r_l = s1("r_l")
            qful, qfree = s1("qful"), s1("qfree")
            f_h, f_z = s1("f_h"), s1("f_z")
            pooled_s, chain, hdn_s, ker_s = s1("pooled"), s1("chain"), s1("hdn"), s1("ker")
            dyn = Steps(s1("dyn"), NI1 * DSTEPS)
            lk_f = s1("lk_f")
            l_h = s1("l_h")
            l_l = s1("l_l")
            zst = s1("zst")

            def nview(a, lv):
                d, n, m = DIL[lv], prow[lv], plen[lv]
                return a[lv][:, :, d:d + n * m].rearrange("p g (r c) -> p g r c", c=m)[:, :, :, 0:SIDE[lv]]

            def tiles_of(k):
                if k == NI1 - 1:
                    return lk_mid(lk_h), lk_mid(lk_l)
                return (t[:, k, :, :].rearrange("p (b c) m -> p b (c m)", b=3) for t in (dt_h, dt_l))

            with nc.Block() as block:
                @block.sync
                def _(sp):
                    sp.sem_inc(mfree, 2 * G)
                    sp.sem_inc(r_l, 2 * G)
                    sp.sem_inc(qfree, 2)
                    sp.sem_inc(l_l, 2)
                    sp.sem_inc(zst, 16)

                    def halos(g):
                        for k, lv in enumerate(order):
                            sp.wait_ge(n_i, NI1 * g + G * (k + 1))
                            alone(sp)
                            d, n2 = DIL[lv], half[lv]
                            m = min(d, n2)
                            for j in range(G):
                                sp.dma_start(pl[lv][0:C, j, d + n2:d + n2 + m, :],
                                             pl[lv][C:P, j, d:d + m, :]).then_inc(halo[lv], 16)
                                sp.dma_start(pl[lv][C:P, j, d - m:d, :],
                                             pl[lv][0:C, j, d + n2 - m:d + n2, :]).then_inc(halo[lv], 16)

                    def store(g):
                        sp.wait_ge(qfree, 2 + Q * (g + 1))
                        alone(sp)
                        for j in range(G):
                            for r in range(2):
                                sp.dma_start(zs2.ap()[G * g + j, :, half[2] * r:half[2] * r + half[2], :],
                                             z[2][r * C:r * C + C, j, :, :]).then_inc(zst, 16)

                    sp.wait_ge(zero, 2)
                    halos(0)
                    with sp.Fori(0, NG - 1) as g:
                        halos(g + 1)
                        store(g)
                    store(NG - 1)
                    sp.wait_ge(zst, 16 + 32 * G * NG)

                @block.gpsimd
                def _(pool):
                    def sums3(g):
                        v = p2[:, bass.ds(G * g, G), :, :].rearrange("p g (r a) (c b) -> p g r a c b", a=2, b=2)
                        quad_sum(pool, pl[3][:, :, DIL[3]:DIL[3] + half[3], :], lambda a, b: v[:, :, :, a, :, b],
                                 p_acc, 2 * g).then_inc(s3, 1)

                    def norm(g):
                        for k, lv in enumerate(order):
                            pool.wait_ge(n_h, 2 * g + k + 1)
                            for j in range(G):
                                pool.tensor_tensor(nview(nl, lv)[:, j], pl[lv][:, j, :, :],
                                                   nview(nh, lv)[:, j].bitcast(F32), ALU.subtract).then_inc(n_l, 1)

                    def body(g, last):
                        for k, (lv, j) in enumerate(items):
                            pool.wait_ge(r_h, NI1 * g + k + 1)
                            s, (b, c) = SIDE[lv], relus[k]
                            pool.tensor_tensor(rl[lv][:, j, :, 2:2 + s],
                                               rf[:, b, c].rearrange("p (r c) -> p r c", c=s),
                                               rh[lv][:, j, :, 2:2 + s].bitcast(F32), ALU.subtract).then_inc(r_l, 1)
                        if not last:
                            pool.wait_ge(n_l, NI1 * (g + 1))
                            alone(pool)
                            sums3(g + 1)
                        pool.wait_ge(qfree, 2 + Q * g + 4)
                        alone(pool)
                        for lv in order:
                            n, q = half[lv], NQ[lv]
                            for t in (fh[lv], fl[lv]):
                                for j in range(G):
                                    pool.memset(t[0:C, j, 3:3 + n, 1:2].bitcast(F32), 0.0).then_inc(f_z, 1)
                                    pool.memset(t[C:P, j, 3:3 + n, 1 + q:2 + q].bitcast(F32), 0.0).then_inc(f_z, 1)
                        pool.wait_ge(f_z, 8 * G * (g + 1))
                        alone(pool)
                        if not last:
                            norm(g + 1)

                    for lv in order:
                        pool.memset(pl[lv][:, :, :, :], 0.0).then_inc(zero, 1)
                    pool.wait_ge(zero, 2)
                    sums3(0)
                    for lv in order:
                        for t in (nh[lv], nl[lv]):
                            pool.memset(t[:, :, :].bitcast(F32), 0.0).then_inc(zero, 1)
                    for lv in order:
                        for t in (rh[lv], rl[lv], fh[lv], fl[lv]):
                            pool.memset(t[:, :, :, :].bitcast(F32), 0.0).then_inc(zero, 1)
                    pool.wait_ge(zero, 14)
                    norm(0)
                    with pool.Fori(0, NG - 1) as g:
                        body(g, False)
                    body(NG - 1, True)

                @block.scalar
                def _(act):
                    def norm(g):
                        for k, lv in enumerate(order):
                            act.wait_ge(halo[lv], 32 * G * (g + 1))
                            for j in range(G):
                                ins = act.activation(nview(nh, lv)[:, j], pl[lv][:, j, :, :], ACT.Identity)
                            ins.then_inc(n_h, 1)

                    def body(g, last):
                        for k, (lv, j) in enumerate(items):
                            act.wait_ge(main, 3 * g + (1 if lv == 3 else 2 + j))
                            act.wait_ge(r_l, NI1 * g + k + 1)
                            b, c = relus[k]
                            src = ps_stat[:, c] if lv == 3 else ps_main[:, j, :]
                            act.activation(rf[:, b, c], src, ACT.Relu, bias=b3p[:, lv:lv + 1],
                                           accum_out=rsum[:, k:k + 1]).then_inc(mfree, 1)
                        for k, lv in enumerate(order):
                            n, q = NB[lv], NQ[lv]
                            for hf in range(2):
                                act.wait_ge(qful, Q * g + 2 * k + hf + 1)
                                p0 = 3 + n * hf
                                ps = ps_q[:, hf, 0:G * n * (q + 2)].rearrange("p (g n q) -> p g n q", g=G, q=q + 2)
                                act.activation(fh[lv][:, :, p0:p0 + n, 1:q + 2], ps[:, :, :, 0:q + 1], ACT.Identity,
                                               bias=b1a[:, lv:lv + 1]).then_inc(f_h, 1)
                            if k == 0:
                                chain_act(act, g, NI1, chain, hdn_s)
                        if not last:
                            norm(g + 1)
                        for k, lv in enumerate(order):
                            act.wait_ge(lk_f, 2 * g + k + 1)
                            act.activation(lh[lv][:, :, :].rearrange("p g n -> p (g n)"),
                                           ps_lk[lv][:, 0:G * NBQ[lv]], ACT.Identity).then_inc(l_h, 1)

                    act.wait_ge(zero, 14)
                    norm(0)
                    with act.Fori(0, NG - 1) as g:
                        body(g, False)
                    body(NG - 1, True)

                @block.vector
                def _(dve):
                    def norm(g):
                        dve.tensor_copy(cg[:, :, :, :].rearrange("p l k b -> p (l k) b"),
                                        coefs[:, :, :, :].rearrange("p l k b -> p (l k) b")[:, :, bass.ds(G * g, G)]
                                        ).then_inc(cg_s, 1)
                        dve.wait_ge(cg_s, g + 1)
                        dve.wait_ge(s3, g + 1)
                        for k, lv in enumerate(order):
                            for j in range(G):
                                dst = pl[lv][:, j, DIL[lv]:DIL[lv] + half[lv], :]
                                src = dst if lv == 3 else p2[:, bass.ds(G * g + j, 1), :, :].rearrange(
                                    "p g r c -> p (g r) c")
                                dve.tensor_scalar(dst, src, cg[:, k, 0, j:j + 1], cg[:, k, 1, j:j + 1], ALU.subtract,
                                                  ALU.mult).then_inc(n_i, 1)

                    def body(g, last):
                        for k, (lv, j) in enumerate(items):
                            dve.wait_ge(mfree, 2 * G + NI1 * g + k + 1)
                            s, (b, c) = SIDE[lv], relus[k]
                            dve.tensor_copy(rh[lv][:, j, :, 2:2 + s],
                                            rf[:, b, c].rearrange("p (r c) -> p r c", c=s)).then_inc(r_h, 1)
                        chain_pooled_dve(dve, g, ((3, G), (2, G)), pooled_s, chain)
                        for k, lv in enumerate(order):
                            n, q = NB[lv], NQ[lv]
                            for hf in range(2):
                                dve.wait_ge(f_h, 4 * g + 2 * k + hf + 1)
                                p0 = 3 + n * hf
                                ps = ps_q[:, hf, 0:G * n * (q + 2)].rearrange("p (g n q) -> p g n q", g=G, q=q + 2)
                                v = fh[lv][:, :, p0:p0 + n, 1:q + 2].bitcast(F32)
                                for j in range(G):
                                    ins = dve.scalar_tensor_tensor(fl[lv][:, j, p0:p0 + n, 1:q + 2],
                                                                   ps[:, j, :, 0:q + 1], b1a[:, lv:lv + 1],
                                                                   v[:, j], ALU.add, ALU.subtract)
                                ins.then_inc(qfree, 1)
                            if k == 0 and not last:
                                dve.wait_ge(n_l, NI1 * (g + 1))
                                norm(g + 1)
                        chain_taps_dve(dve, g, NI1, chain, ker_s)
                        dve.wait_ge(ker_s, g + 1)
                        dyn.start(g)
                        for k, (lv, j) in enumerate(items):
                            dynamic_tiles(dve, dyn, kerr[:, k, :], *tiles_of(k))
                            dyn.wait(dve)
                        for k, lv in enumerate(order):
                            dve.wait_ge(l_h, 2 * g + k + 1)
                            o = ll[lv][:, :, :].rearrange("p g n -> p (g n)")
                            dve.tensor_tensor(o, ps_lk[lv][:, 0:G * NBQ[lv]],
                                              lh[lv][:, :, :].rearrange("p g n -> p (g n)").bitcast(F32),
                                              ALU.subtract).then_inc(l_l, 1)
                        dve.wait_ge(zst, 16 + 32 * G * g)
                        for k, lv in enumerate(order):
                            n, q = NB[lv], NQ[lv]
                            for p, (dr, dc) in enumerate(PIX):
                                u = 8 * k + p
                                dve.wait_ge(qful, Q * g + 4 + u + 1)
                                src = ps_q[:, p % 2, 0:G * n * q].rearrange("p (g n q) -> p g n q", g=G, q=q)
                                for j in range(G):
                                    dst = z[lv][:, j, dr::2, dc::4]
                                    if lv == 3:
                                        ins = dve.tensor_copy(dst, src[:, j])
                                    else:
                                        ins = dve.tensor_tensor(dst, src[:, j], z[3][:, j, :, dc // 2::2], ALU.add)
                                ins.then_inc(qfree, 1)
                            dve.wait_ge(qfree, 2 + Q * g + 4 + 8 * (k + 1))

                    for k, lv in enumerate(order):
                        k2 = float((H // SIDE[lv]) ** 2)
                        dve.tensor_scalar(coefs[:, k, 0, :], gn0[:, :, 0], k2, None, ALU.mult).then_inc(cf_s, 1)
                        dve.tensor_scalar(coefs[:, k, 1, :], gn0[:, :, 1], 1.0 / k2, None, ALU.mult).then_inc(cf_s, 1)
                    dve.wait_ge(cf_s, 4)
                    norm(0)
                    with dve.Fori(0, NG - 1) as g:
                        body(g, False)
                    body(NG - 1, True)

                @block.tensor
                def _(pe):
                    def large(g, k):
                        lv = order[k]
                        n, q = half[lv], NQ[lv]
                        pe.wait_ge(l_l, 2 * g + k + 1)
                        o = ps_lk[lv][:, 0:G * n * q]
                        still = [(pb, cb) for pb in range(NPB) for cb in range(NCB) if (pb, cb) not in DYN]
                        for m, (pb, cb) in enumerate(still):
                            v = (slice(None), slice(None), slice(pb, pb + n), slice(cb, cb + q))
                            product(pe, o.rearrange("p (g n q) -> p g n q", g=G, q=q), lk_h[:, pb, cb, :],
                                    lk_l[:, pb, cb, :], fh[lv][v], fl[lv][v], m == 0, False)
                        for j in range(G):
                            item = G * k + j
                            dyn.at(pe, g, DSTEPS * (item + 1))
                            for m, (pb, cb) in enumerate(DYN):
                                v = (slice(None), j, slice(pb, pb + n), slice(cb, cb + q))
                                if item == NI1 - 1:
                                    wh, wl = lk_h[:, pb, cb, :], lk_l[:, pb, cb, :]
                                else:
                                    wh, wl = dt_h[:, item, m, :], dt_l[:, item, m, :]
                                mm = product(pe, o[:, j * n * q:(j + 1) * n * q].rearrange("p (n q) -> p n q", q=q),
                                             wh, wl, fh[lv][v], fl[lv][v], False, m == ND - 1)
                        mm.then_inc(lk_f, 1)

                    def body(g, last):
                        for k, (lv, j, o) in enumerate(convs):
                            s, d, n = SIDE[lv], DIL[lv], half[lv]
                            pe.wait_ge(n_l, NI1 * g + (G if lv == 3 else NI1))
                            pe.wait_ge(mfree, NI1 * g + (G if lv == 3 else G + 1 + j))
                            o = o.rearrange("p (g r c) -> p g r c", g=G, c=s) if lv == 3 else \
                                o.rearrange("p (r c) -> p r c", c=s)
                            sel = slice(None) if lv == 3 else j
                            for t in range(9):
                                o0 = (t // 3) * d * plen[lv] + (t % 3) * d
                                vh, vl = (a[lv][:, :, o0:o0 + n * plen[lv]].rearrange(
                                    "p g (r c) -> p g r c", c=plen[lv])[:, sel, :, 0:s] for a in (nh, nl))
                                mm = product(pe, o, w3h[:, lv - 1, t, :], w3l[:, lv - 1, t, :], vh, vl, t == 0, t == 8)
                            mm.then_inc(main, 1)
                        pe.wait_ge(r_l, 2 * G + NI1 * (g + 1))
                        pe.wait_ge(mfree, 2 * G + NI1 * (g + 1))
                        chain_pooled(pe, g, ((3, G), (2, G)), None, chain)
                        for k, lv in enumerate(order):
                            pe.wait_ge(qfree, Q * g + 2 * k + 2)
                            n, q = NB[lv], NQ[lv] + 2
                            for m, (dr, dc) in enumerate(PIX):
                                a = 112 - ATT * slot(dr, dc)
                                for hf in range(2):
                                    v = (slice(hf * C, hf * C + C), slice(None), slice(dr, None, 2),
                                         slice(dc, dc + 4 * q - 3, 4))
                                    w = (v[0], lv - 1, slice(a, a + P))
                                    mm = product(pe, ps_q[:, hf, 0:G * n * q].rearrange("p (g n q) -> p g n q", g=G, q=q),
                                                 fa_h[w], fa_l[w], rh[lv][v], rl[lv][v], m == 0, m == 7)
                                    if m == 7:
                                        mm.then_inc(qful, 1)
                                if k == 0 and m == 3:
                                    chain_hidden(pe, g, NI1, 2, pooled_s, chain)
                            if k == 0:
                                chain_taps(pe, g, NI1, hdn_s, chain)
                        pe.wait_ge(f_z, 8 * G * (g + 1))
                        large(g, 0)
                        large(g, 1)
                        for k, lv in enumerate(order):
                            pe.wait_ge(l_l, 2 + 2 * g + k + 1)
                            n, q = NB[lv], NQ[lv]
                            for p, (dr, dc) in enumerate(PIX):
                                pe.wait_ge(qfree, Q * g + 4 + 8 * k + p + 1)
                                o = ps_q[:, p % 2, 0:G * n * q]
                                v = (slice(None), slice(None), slice(dr, None, 2), slice(2 + dc, 2 + dc + 4 * q - 3, 4))
                                product(pe, o.rearrange("p (g n q) -> p g n q", g=G, q=q), idt_h[:, lv, :],
                                        idt_l[:, lv, :], rh[lv][v], rl[lv][v], True, False)
                                for hf in range(2):
                                    w = slice(slot(dr, dc) * P + C * (1 - hf), slot(dr, dc) * P + C * (1 - hf) + P)
                                    m = (slice(None), slice(None), slice(hf * n * q, (hf + 1) * n * q))
                                    mm = product(pe, o.rearrange("p (g n) -> p g n", g=G), ga_h[:, w], ga_l[:, w],
                                                 lh[lv][m], ll[lv][m], False, hf == 1)
                                mm.then_inc(qful, 1)

                    with pe.Fori(0, NG - 1) as g:
                        body(g, False)
                    body(NG - 1, True)
        st1.close()

        NW = NPAIR // 4
        with ExitStack() as st:
            def s2(name):
                return sem("p2_" + name, st)

            t3_h = sb("t3_h", [P, 2, 3, P], F32R, stack=st)
            t3_l = sb("t3_l", [P, 2, 3, P], F32R, stack=st)
            c5_h = sb("c5_h", [P, 3, 5, P], F32R, stack=st)
            c5_l = sb("c5_l", [P, 3, 5, P], F32R, stack=st)
            fa_h = sb("fa0_h", [P, 4, P], F32R, stack=st)
            fa_l = sb("fa0_l", [P, 4, P], F32R, stack=st)
            ga_h = sb("ga0_h", [P, 4, P], F32R, stack=st)
            ga_l = sb("ga0_l", [P, 4, P], F32R, stack=st)
            row_w = sb("row_w", [P, 5, C], stack=st)
            col_w = sb("col_w", [P, 2, 3, P], stack=st)
            cor_w = sb("cor_w", [P, 2, C], stack=st)
            edge_b = sb("edge_b", [P, 256], stack=st)
            out_b = sb("out_b", [P, 1], stack=st)
            zeros = sb("zeros0", [P, 2, W], stack=st)

            x1 = sb("x1", [P, NPAIR + 2, W], stack=st)
            fh = sb("fh0", [P, NPAIR + 6, 36], F32R, stack=st)
            fl = sb("fl0", [P, NPAIR + 6, 36], F32R, stack=st)
            xh = sb("xh", [P, 2, 5, W + 2], F32R, stack=st)
            xl = sb("xl", [P, 2, 5, W + 2], F32R, stack=st)
            rh = sb("rh0", [P, 2, 4, W + 8], F32R, stack=st)
            rl = sb("rl0", [P, 2, 4, W + 8], F32R, stack=st)
            yh = sb("yh", [P, 2, 6, W + 4], F32R, stack=st)
            yl = sb("yl", [P, 2, 6, W + 4], F32R, stack=st)
            rowf = sb("rowf", [P, W + 4], stack=st)
            colf = sb("colf", [P, 2, NPAIR + 2], stack=st)
            xp = x.rearrange("b c (p r) w -> b c p r w", r=2)
            op = out.rearrange("b c (p r) w -> b c p r w", r=2)

            with ExitStack() as se:
                b_p = sem("b_p", se)
                b_z = sem("b_z", se)
                b_ld = sem("b_ld", se)
                b_x = sem("b_x", se)
                steps = Steps(sem("b_s", se), 200)
                s3 = sb("s3", [P, 4, 3, C], stack=se)
                s31 = sb("s31", [P, 4, 3, C], stack=se)
                c5 = sb("c5", [P, 6, 5, C], stack=se)
                wrb = sb("wrb", [P, 10, C], stack=se)
                tmp = sb("tmp", [P, 4, 3, C], stack=se)
                tile_f = sb("tile_f", [P, 3, 5, P], stack=se)
                cls = sb("cls", [P, 2, 6, C], stack=se)
                wrs = sb("wrs", [P, 10], stack=se)
                bb = sb("bb", [P, 8], stack=se)

                def g(sh, sw):
                    return 1 + 3 * sh + sw

                with nc.Block() as block:
                    @block.gpsimd
                    def _(pool):
                        for t in (fh, fl):
                            pool.memset(t[:, :, :].bitcast(F32), 0.0).then_inc(b_p, 1)
                        for t in (xh, xl, rh, rl, yh, yl):
                            pool.memset(t[:, :, :, :].bitcast(F32), 0.0).then_inc(b_p, 1)
                        pool.memset(zeros[:, :, :], 0.0).then_inc(b_p, 1)
                        pool.memset(rowf[:, :], 0.0).then_inc(b_p, 1)

                    @block.sync
                    def _(sp):
                        with nc.allow_non_contiguous_dma(reason="small weight layouts"):
                            sp.dma_start(wrb[:, :, :], wrt.unsqueeze(0).to_broadcast([P, 10, C])).then_inc(b_ld, 16)
                            for r in range(2):
                                hp = slice(r * C, r * C + C)
                                sp.dma_start(wrs[hp, :], wr).then_inc(b_ld, 16)
                                for k, v in enumerate((c3b, c5b, br)):
                                    sp.dma_start(bb[hp, k:k + 1], v.rearrange("(c a) -> c a", a=1)).then_inc(b_ld, 16)
                            for r in range(2):
                                sp.dma_start(x1[par(r), 1:NPAIR + 1, :], xp[0, :, :, r, :]).then_inc(b_x, 16)
                            sp.wait_ge(b_z, 3)
                            for r in range(2):
                                hp = slice(r * C, r * C + C)
                                w0 = w3t[0].rearrange("c (y x) o -> c y x o", x=3)
                                sp.dma_start(s3[hp, 1 - r:4 - r, :, :], w0).then_inc(b_ld, 16)
                                sp.dma_start(s31[par(r), 1 - r:4 - r, :, :], c3t).then_inc(b_ld, 16)
                                sp.dma_start(c5[par(r), 1 - r:6 - r, :, :], c5t).then_inc(b_ld, 16)
                            sp.wait_ge(b_x, 16 * 2)

                    @block.vector
                    def _(dve):
                        steps.start(0)

                        def step(ins):
                            steps.done(ins)
                            steps.wait(dve)

                        def split(hi, lo, src):
                            step(dve.tensor_copy(hi, src))
                            step(dve.tensor_tensor(lo, src, hi.bitcast(F32), ALU.subtract))

                        for t in (s3, s31, c5):
                            dve.memset(t[:, :, :, :], 0.0).then_inc(b_z, 1)
                        step(dve.memset(tile_f[:, :, :, :], 0.0))
                        step(dve.memset(row_w[:, :, :], 0.0))
                        step(dve.memset(cls[:, :, :, :], 0.0))
                        for dr, dc in PIX:
                            hp, q = par(dr), slot(dr, dc) * ATT
                            step(dve.tensor_copy(tile_f[hp, 0, dc, q:q + ATT], w1a[hp, 0, :]))
                        split(fa_h[:, :, :], fa_l[:, :, :], tile_f[:, 0, 0:4, :])
                        for dr, dc in PIX:
                            s = slot(dr, dc)
                            step(dve.tensor_scalar(tile_f[:, 0, dc, par(dr)], gar[:, :], slm[:, s:s + 1],
                                                   None, ALU.mult))
                        split(ga_h[:, :, :], ga_l[:, :, :], tile_f[:, 0, 0:4, :])
                        dve.wait_ge(b_ld, 16 * 15)
                        for blk in range(2):
                            for m in range(2):
                                step(dve.tensor_copy(tile_f[:, blk, 0:3, par(m)], s3[:, 2 * blk - m + 1, :, :]))
                        split(t3_h[:, :, :, :], t3_l[:, :, :, :], tile_f[:, 0:2, 0:3, :])

                        step(dve.tensor_tensor(c5[:, :, :, :].rearrange("p a b c -> p (a b) c"),
                                               c5[:, :, :, :].rearrange("p a b c -> p (a b) c"),
                                               wrb[:, 0, :].unsqueeze(1).to_broadcast([P, 30, C]), ALU.mult))
                        for sh in range(3):
                            for sw in range(3):
                                step(dve.tensor_tensor(tmp[:, :, :, :].rearrange("p a b c -> p (a b) c"),
                                                       s31[:, :, :, :].rearrange("p a b c -> p (a b) c"),
                                                       wrb[:, g(sh, sw), :].unsqueeze(1).to_broadcast([P, 12, C]),
                                                       ALU.mult))
                                d = c5[:, 2 - sw:6 - sw, 2 - sh:5 - sh, :]
                                step(dve.tensor_tensor(d, d, tmp[:, :, :, :], ALU.add))
                                for side, h0, kx in ((0, 2, 2), (1, 0, 0)):
                                    if sh == h0:
                                        d = cls[:, side, 2 - sw:6 - sw, :]
                                        step(dve.tensor_tensor(d, d, tmp[:, :, kx, :], ALU.add))
                                for r, w0, a in ((0, 2, 3), (1, 0, 0)):
                                    hp = par(r)
                                    if sw == w0:
                                        d = row_w[hp, 2 - sh:5 - sh, :]
                                        step(dve.tensor_tensor(d, d, tmp[hp, a, :, :], ALU.add))
                                        for side, h0, kx in ((0, 2, 2), (1, 0, 0)):
                                            if sh == h0:
                                                step(dve.tensor_scalar(cor_w[hp, side, :], tmp[hp, a, kx, :], -1.0,
                                                                       None, ALU.mult))
                        for blk in range(3):
                            for m in range(2):
                                step(dve.tensor_copy(tile_f[:, blk, :, par(m)], c5[:, 2 * blk - m + 1, :, :]))
                                step(dve.tensor_copy(col_w[:, :, blk, par(m)], cls[:, :, 2 * blk - m + 1, :]))
                        split(c5_h[:, :, :, :], c5_l[:, :, :, :], tile_f[:, :, :, :])
                        b_3, b_5, b_r, t = (bb[:, k:k + 1] for k in range(4))
                        step(dve.tensor_reduce(t, wrs[:, 1:10], AX.X, ALU.add))
                        step(dve.scalar_tensor_tensor(out_b[:, :], t, b_3, b_r, ALU.mult, ALU.add))
                        step(dve.scalar_tensor_tensor(out_b[:, :], wrs[:, 0:1], b_5, out_b[:, :], ALU.mult, ALU.add))
                        step(dve.memset(edge_b[:, :], 1.0))
                        for r, w0, pair in ((0, 2, 0), (1, 0, NPAIR - 1)):
                            hp = par(r)
                            step(dve.tensor_reduce(t[hp], wrs[hp, g(0, w0):g(2, w0) + 1:3], AX.X, ALU.add))
                            step(dve.tensor_scalar(edge_b[hp, 0:W], edge_b[hp, 0:W], t[hp], b_3[hp], ALU.mult, ALU.mult))
                        for side, h0 in ((0, 2), (1, 0)):
                            e = edge_b[:, W + side * NPAIR:W + side * NPAIR + NPAIR]
                            step(dve.tensor_reduce(t, wrs[:, g(h0, 0):g(h0, 2) + 1], AX.X, ALU.add))
                            step(dve.tensor_scalar(e, e, t, b_3, ALU.mult, ALU.mult))
                            for r, w0, pair in ((0, 2, 0), (1, 0, NPAIR - 1)):
                                hp, k = par(r), g(h0, w0)
                                step(dve.tensor_scalar(t[hp], wrs[hp, k:k + 1], b_3[hp], None, ALU.mult))
                                step(dve.tensor_tensor(e[hp, pair:pair + 1], e[hp, pair:pair + 1], t[hp], ALU.subtract))

            zall = sb("zall", [P, NPAIR, W // 2], stack=st)
            z23 = sb("z23", [P, H // 4, W // 4], stack=st)
            xnf = sb("xnf", [P, 5, W], stack=st)
            rf = sb("rf0", [P, 512], stack=st)
            lh = sb("lh0", [P, 2, 512], F32R, stack=st)
            ll = sb("ll0", [P, 2, 512], F32R, stack=st)
            xn1 = sb("xn1", [P, 6, W], stack=st)
            ot = sb("ot", [P, 2, 4, W], stack=st)
            edge = sb("edge", [P, 256], stack=st)
            m0 = sb("m0", [P, 2], stack=st)
            m1 = sb("m1", [P, 2], stack=st)
            rs = sb("rs0", [P, NW], stack=st)

            MAIN, Q = 36, 48
            QY = 2 * NW
            MB, MC = NW, NW + 4
            assert MAIN == MC + NW and Q == QY + 16
            m_cp, e_in = s2("m_cp"), s2("e_in")
            m_row = s2("m_row")
            x_full = s2("x_full")
            z_done = s2("z_done")
            z_full = s2("z_full")
            NLOAD = 8
            x_n, x_h, x_l = s2("x_n"), s2("x_h"), s2("x_l")
            main, mfree, qful, qfree = s2("main"), s2("mfree"), s2("qful"), s2("qfree")
            r_h, r_l, x_z, f_h, f_z = s2("r_h"), s2("r_l"), s2("x_z"), s2("f_h"), s2("f_z")
            sums = Steps(s2("sums"), 1)
            pooled_s, chain, hdn_s, ker_s = s2("pooled"), s2("chain"), s2("hdn"), s2("ker")
            dyn = Steps(s2("dyn"), DSTEPS)
            l_h, bn = s2("l_h"), s2("bn")
            stats = Steps(s2("stats"), GSTEPS + 3)
            avg, root = s2("avg"), s2("root")
            y_n, y_h, y_l = s2("y_n"), s2("y_h"), s2("y_l")
            e_mm, e_out = s2("e_mm"), s2("e_out")
            o_row, o_done = s2("o_row"), s2("o_done")
            stored = [s2("stored0"), s2("stored1")]

            def windows(eng, first, body, before={}):
                for w in range(first, 2):
                    body(w, w % 2)
                with eng.Fori(1, NW // 2 - 1) as t:
                    for h in range(2):
                        body(2 * t + h, h)
                for w in range(NW - 2, NW):
                    if w in before:
                        before[w]()
                    body(w, w % 2)

            def is_last(w, k):
                return isinstance(w, int) and w + k >= NW

            def is_first(w, k):
                return isinstance(w, int) and w < k

            with nc.Block() as block:
                @block.sync
                def _(sp):
                    sp.sem_inc(mfree, 2)
                    sp.sem_inc(qfree, 2)
                    for sm in (x_n, x_l, r_l, y_l):
                        sp.sem_inc(sm, 1)
                    for sm in (x_full, *stored):
                        sp.sem_inc(sm, 16)

                    def load_z(i):
                        for r in range(2):
                            sp.dma_start(zall[par(r), :, :], zs.ap()[i]).then_inc(z_full, 16)
                            sp.dma_start(z23[par(r), :, :], zs2.ap()[i]).then_inc(z_full, 16)

                    def load(i):
                        sp.wait_ge(x_z, NW * (i + 1))
                        alone(sp)
                        load_z(i + 1)
                        n = NPAIR // NLOAD
                        with sp.Fori(0, NLOAD) as u:
                            sp.wait_ge(o_done, NW * i + 2 * u + 2)
                            alone(sp)
                            sp.wait_ge(x_full, 16 + 32 * (NLOAD * i + u))
                            alone(sp)
                            for r in range(2):
                                sp.dma_start(x1[par(r), bass.ds(n * u + 1, n), :],
                                             xp[i + 1, :, bass.ds(n * u, n), r, :]).then_inc(x_full, 16)

                    load_z(0)
                    with sp.Fori(0, B - 1) as i:
                        load(i)

                @block.gpsimd
                def _(pool):
                    def stage_a(i, w, h):
                        pool.wait_ge(x_n, NW * i + w + (2 if is_last(w, 1) else 3))
                        v = x1[:, bass.ds(4 * w + 1, 4), :].rearrange("p a (b c) -> p (a b) c", c=2)
                        zz = zall[:, bass.ds(4 * w, 4), :].rearrange("p a b -> p (a b)").unsqueeze(2)
                        alone(pool)
                        pool.tensor_tensor(v, v, zz.to_broadcast([P, 256, 2]), ALU.add).then_inc(x_z, 1)
                        pool.wait_ge(r_h, NW * i + w + 1)
                        pool.tensor_tensor(rl[:, h, :, 2:2 + W], rf[:, :].rearrange("p (a b) -> p a b", b=W),
                                           rh[:, h, :, 2:2 + W].bitcast(F32), ALU.subtract).then_inc(r_l, 1)

                    def y_low(i, v, h):
                        pool.wait_ge(y_h, NW * i + v + 1)
                        pool.tensor_tensor(yl[:, h, :, 2:2 + W], xn1[:, :, :], yh[:, h, :, 2:2 + W].bitcast(F32),
                                           ALU.subtract).then_inc(y_l, 1)

                    def z_sum(i):
                        pool.wait_ge(z_full, 64 * (i + 1))
                        zz = z23[:, :, :].unsqueeze(3).to_broadcast([P, H // 4, W // 4, 2])
                        for r in range(2):
                            v = zall[:, r::2, :].rearrange("p a (b c) -> p a b c", c=2)
                            alone(pool)
                            pool.tensor_tensor(v, v, zz, ALU.add).then_inc(z_done, 1)

                    def body(i, last):
                        pool.wait_ge(z_done, 2 * (i + 1))
                        alone(pool)
                        windows(pool, 0, lambda w, h: stage_a(i, w, h))
                        pool.wait_ge(qfree, 2 + Q * i + QY)
                        alone(pool)
                        for t in (fh, fl):
                            pool.memset(t[0:C, 3:3 + NPAIR, 1:2].bitcast(F32), 0.0).then_inc(f_z, 1)
                            pool.memset(t[C:P, 3:3 + NPAIR, 33:34].bitcast(F32), 0.0).then_inc(f_z, 1)
                        pool.wait_ge(f_z, 4 * (i + 1))
                        if not last:
                            z_sum(i + 1)
                        windows(pool, 0, lambda v, h: y_low(i, v, h))

                    z_sum(0)
                    with pool.Fori(0, B - 1) as i:
                        body(i, False)
                    body(B - 1, True)

                @block.scalar
                def _(act):
                    def x_high(i, w, h):
                        act.wait_ge(x_n, NW * i + w + 2)
                        if not is_first(w, 2):
                            act.wait_ge(main, MAIN * i + w - 1)
                        act.activation(xh[:, h, :, 1:1 + W], xnf[:, :, :], ACT.Identity).then_inc(x_h, 1)

                    def f_high(i, w, h):
                        act.wait_ge(qful, Q * i + 2 * w + 1)
                        ps = ps_q[:, 0, 0:136].rearrange("p (n q) -> p n q", q=34)
                        act.activation(fh[:, bass.ds(4 * w + 3, 4), 1:34], ps[:, :, 0:33], ACT.Identity,
                                       bias=b1a[:, 0:1]).then_inc(f_h, 1)

                    def stage_a(i, w, h):
                        act.wait_ge(main, MAIN * i + w + 1)
                        act.wait_ge(r_l, NW * i + w + 1)
                        act.activation(rf[:, :], ps_main[:, h, :], ACT.Relu, bias=b3p[:, 0:1],
                                       accum_out=rs[:, bass.ds(w, 1)]).then_inc(mfree, 1)
                        if not is_first(w, 1):
                            f_high(i, w - 1, 1 - h)
                        if not is_last(w, 2):
                            x_high(i, w + 2, h)

                    def y_high(i, v, h):
                        act.wait_ge(y_n, NW * i + v + 1)
                        if not is_first(v, 2):
                            act.wait_ge(main, MAIN * i + MC + v - 1)
                        act.activation(yh[:, h, :, 2:2 + W], xn1[:, :, :], ACT.Identity).then_inc(y_h, 1)

                    def store(i, v, h):
                        act.wait_ge(o_done, NW * i + v + 1)
                        for r in range(2):
                            act.dma_start(op[i, :, bass.ds(4 * v, 4), r, :],
                                          ot[par(r), h, :, :]).then_inc(stored[h], 16)

                    def stage_c(i, v, h):
                        if not is_last(v, 2):
                            y_high(i, v + 2, h)
                        store(i, v, h)

                    def body(i, last):
                        windows(act, 0, lambda w, h: stage_a(i, w, h))
                        f_high(i, NW - 1, 1)
                        chain_act(act, i, 1, chain, hdn_s)
                        for c in range(4):
                            act.wait_ge(main, MAIN * i + MB + c + 1)
                            if c >= 2:
                                act.wait_ge(qful, Q * i + QY + 4 * (c - 1))
                            act.activation(lh[:, c % 2, :], ps_main[:, c % 2, :], ACT.Identity).then_inc(l_h, 1)
                        group_stats_act(act, stats, i, root)
                        for v in range(2):
                            y_high(i, v, v)
                        windows(act, 0, lambda v, h: stage_c(i, v, h), {} if last else {
                            NW - 2: lambda: x_high(i + 1, 0, 0), NW - 1: lambda: x_high(i + 1, 1, 1)})

                    x_high(0, 0, 0)
                    x_high(0, 1, 1)
                    with act.Fori(0, B - 1) as i:
                        body(i, False)
                    body(B - 1, True)
                    for h in range(2):
                        act.wait_ge(stored[h], 16 + 32 * B * NW // 2)

                @block.vector
                def _(dve):
                    def x_norm(i, w):
                        if is_first(w, 2):
                            dve.wait_ge(m_row, i + 1)
                        dve.wait_ge(x_l, NW * i + w + 1)
                        for hp, k in ((par(1), 0), (par(0), 1)):
                            ins = dve.tensor_scalar(xnf[hp, :, :], x1[hp, bass.ds(4 * w + k, 5), :], m0[hp, 0:1],
                                                    m0[hp, 1:2], ALU.subtract, ALU.mult)
                        ins.then_inc(x_n, 1)

                    def x_low(i, w, h):
                        dve.wait_ge(x_h, NW * i + w + 1)
                        dve.tensor_tensor(xl[:, h, :, 1:1 + W], xnf[:, :, :], xh[:, h, :, 1:1 + W].bitcast(F32),
                                          ALU.subtract).then_inc(x_l, 1)

                    def next_image(i):
                        dve.tensor_copy(m0[:, :], gn0[:, bass.ds(i, 1), :].rearrange("p a b -> p (a b)")).then_inc(m_cp, 1)
                        dve.wait_ge(m_cp, i + 1)
                        dve.tensor_scalar(x1[:, 0:NPAIR + 2:NPAIR + 1, :], zeros[:, :, :], m0[:, 0:1], None,
                                          ALU.add).then_inc(m_row, 1)

                    def first_norm(i):
                        next_image(i)
                        x_norm(i, 0)

                    def second_norm(i):
                        x_low(i, 0, 0)
                        x_norm(i, 1)

                    def a_out(i, w, h):
                        dve.wait_ge(f_h, NW * i + w + 1)
                        ps = ps_q[:, 0, 0:136].rearrange("p (n q) -> p n q", q=34)
                        dve.scalar_tensor_tensor(fl[:, bass.ds(4 * w + 3, 4), 1:34], ps[:, :, 0:33], b1a[:, 0:1],
                                                 fh[:, bass.ds(4 * w + 3, 4), 1:34].bitcast(F32), ALU.add,
                                                 ALU.subtract).then_inc(qfree, 1)
                        dve.wait_ge(qful, Q * i + 2 * w + 2)
                        dve.wait_ge(x_z, NW * i + w + 1)
                        dve.scalar_tensor_tensor(x1[:, bass.ds(4 * w + 1, 4), :].rearrange("p a b -> p (a b)"),
                                                 ps_q[:, 1, :], bz[:, 0:1],
                                                 x1[:, bass.ds(4 * w + 1, 4), :].rearrange("p a b -> p (a b)"), ALU.add,
                                                 ALU.add).then_inc(qfree, 1)

                    def stage_a(i, w, h):
                        if not is_last(w, 1):
                            x_low(i, w + 1, 1 - h)
                        dve.wait_ge(mfree, 2 + MAIN * i + w + 1)
                        if not is_first(w, 2):
                            dve.wait_ge(qful, Q * i + 2 * w - 2)
                        dve.tensor_copy(rh[:, h, :, 2:2 + W],
                                        rf[:, :].rearrange("p (a b) -> p a b", b=W)).then_inc(r_h, 1)
                        if not is_first(w, 1):
                            a_out(i, w - 1, 1 - h)
                        if is_first(w, 1):
                            dve.wait_ge(x_full, 16 + 32 * NLOAD * i)
                        if not is_last(w, 2):
                            x_norm(i, w + 2)

                    def low_lk(i, c):
                        dve.wait_ge(l_h, 4 * i + c + 1)
                        dve.tensor_tensor(ll[:, c % 2, :], ps_main[:, c % 2, :], lh[:, c % 2, :].bitcast(F32),
                                          ALU.subtract).then_inc(mfree, 1)

                    def add_attention(i, c):
                        for dc in range(4):
                            dve.wait_ge(qful, Q * i + QY + 4 * c + dc + 1)
                            v = x1[:, 1 + 16 * c:17 + 16 * c, dc::4]
                            dve.tensor_tensor(v, v, ps_q[:, dc % 2, :].rearrange("p (n q) -> p n q", q=32),
                                              ALU.add).then_inc(qfree, 1)
                        dve.wait_ge(qfree, 2 + Q * i + QY + 4 * c + 4)
                        for k in range(4):
                            dve.bn_stats(stat[:, 4 * c + k, :],
                                         x1[:, 1 + 16 * c + 4 * k:5 + 16 * c + 4 * k, :].rearrange("p a b -> p (a b)")
                                         ).then_inc(bn, 1)

                    def y_norm(i, v):
                        dve.wait_ge(y_l, NW * i + v + 1)
                        dve.tensor_scalar(xn1[:, :, :], x1[:, bass.ds(4 * v, 6), :], m1[:, 0:1], m1[:, 1:2],
                                          ALU.subtract, ALU.mult).then_inc(y_n, 1)

                    def stage_c(i, v, h):
                        dve.wait_ge(main, MAIN * i + MC + v + 1)
                        dve.wait_ge(stored[h], 16 + 32 * (8 * i + v // 2))
                        o = ot[:, h, :, :]
                        dve.scalar_tensor_tensor(o.rearrange("p a b -> p (a b)"), ps_main[:, h, :], out_b[:, 0:1],
                                                 x1[:, bass.ds(4 * v + 1, 4), :].rearrange("p a b -> p (a b)"),
                                                 ALU.add, ALU.add).then_inc(mfree, 1)
                        dve.wait_ge(mfree, 2 + MAIN * i + MC + v + 1)
                        for first, r, pair in ((True, 0, 0), (False, 1, 3)):
                            if (is_first(v, 1) if first else is_last(v, 1)):
                                hp = par(r)
                                dve.tensor_tensor(o[hp, pair, :], o[hp, pair, :], edge[hp, 0:W],
                                                  ALU.subtract).then_inc(o_row, 1)
                                dve.wait_ge(o_row, 2 * i + r + 1)
                        e = edge[:, W:].rearrange("p (s n) -> p n s", s=2)[:, bass.ds(4 * v, 4), :]
                        dve.tensor_tensor(o[:, :, 0:W:W - 1], o[:, :, 0:W:W - 1], e, ALU.subtract).then_inc(o_done, 1)
                        if not is_last(v, 2):
                            y_norm(i, v + 2)

                    def body(i, last):
                        windows(dve, 0, lambda w, h: stage_a(i, w, h))
                        sums.start(i)
                        sums.done(dve.tensor_reduce(rsum[:, 0:1], rs[:, :], AX.X, ALU.add))
                        a_out(i, NW - 1, 1)
                        chain_pooled_dve(dve, i, ((0, 1),), pooled_s, chain)
                        chain_taps_dve(dve, i, 1, chain, ker_s)
                        dve.wait_ge(ker_s, i + 1)
                        dyn.start(i)
                        dynamic_tiles(dve, dyn, kerr[:, 0, :], lk_mid(lk_h), lk_mid(lk_l))
                        dve.wait_ge(qfree, 2 + Q * i + QY)
                        low_lk(i, 0)
                        low_lk(i, 1)
                        add_attention(i, 0)
                        low_lk(i, 2)
                        add_attention(i, 1)
                        low_lk(i, 3)
                        add_attention(i, 2)
                        add_attention(i, 3)
                        dve.wait_ge(bn, 16 * (i + 1))
                        alone(dve)
                        stats.start(i)
                        group_stats_dve(dve, stats, lambda v: dve.wait_ge(avg, v), lambda v: dve.wait_ge(root, v),
                                        i, stat[:, :, :].rearrange("p a b -> p (a b)"), m1[:, 0:1], m1[:, 1:2])
                        stats.done(dve.tensor_scalar(x1[:, 0:NPAIR + 2:NPAIR + 1, :], zeros[:, :, :], m1[:, 0:1],
                                                     None, ALU.add))
                        stats.wait(dve)
                        y_norm(i, 0)
                        y_norm(i, 1)
                        stats.done(dve.tensor_scalar(colf[:, :, :].rearrange("p s n -> p n s"),
                                                     x1[:, :, 0:W:W - 1], m1[:, 0:1], m1[:, 1:2], ALU.subtract, ALU.mult))
                        for r, pair in ((0, 1), (1, NPAIR)):
                            hp = par(r)
                            ins = dve.tensor_scalar(rowf[hp, 2:2 + W], x1[hp, pair, :], m1[hp, 0:1], m1[hp, 1:2],
                                                    ALU.subtract, ALU.mult)
                            if r == 0:
                                ins.then_inc(e_in, 1)
                            else:
                                stats.done(ins)
                        dve.wait_ge(e_mm, i + 1)
                        dve.tensor_tensor(edge[:, :], ps_edge[:, 0:256], edge_b[:, :], ALU.add).then_inc(e_out, 1)
                        dve.wait_ge(e_out, i + 1)

                        def ahead():
                            dve.wait_ge(x_full, 16 + 32 * (NLOAD * i + 2))
                            first_norm(i + 1)

                        windows(dve, 0, lambda v, h: stage_c(i, v, h), {} if last else {
                            NW - 2: ahead, NW - 1: lambda: second_norm(i + 1)})

                    first_norm(0)
                    second_norm(0)
                    with dve.Fori(0, B - 1) as i:
                        body(i, False)
                    body(B - 1, True)

                @block.tensor
                def _(pe):
                    def conv3(i, w, h):
                        pe.wait_ge(x_l, NW * i + w + 2)
                        pe.wait_ge(mfree, MAIN * i + w + 1)
                        o = ps_main[:, h, :].rearrange("p (a b) -> p a b", b=W)
                        for blk in range(2):
                            for kx in range(3):
                                v = (slice(None), h, slice(blk, blk + 4), slice(kx, kx + W))
                                mm = product(pe, o, t3_h[:, blk, kx, :], t3_l[:, blk, kx, :], xh[v], xl[v],
                                             blk + kx == 0, blk + kx == 3)
                        mm.then_inc(main, 1)

                    def pointwise(i, w, h):
                        pe.wait_ge(r_l, NW * i + w + 2)
                        pe.wait_ge(qfree, Q * i + 2 * w + 1)
                        for dc in range(4):
                            v = (slice(None), h, slice(None), slice(dc, dc + 133, 4))
                            mm = product(pe, ps_q[:, 0, 0:136].rearrange("p (n q) -> p n q", q=34), fa_h[:, dc, :],
                                         fa_l[:, dc, :], rh[v], rl[v], dc == 0, dc == 3)
                        mm.then_inc(qful, 1)
                        pe.wait_ge(qfree, Q * i + 2 * w + 2)
                        v = (slice(None), h, slice(None), slice(2, 2 + W))
                        product(pe, ps_q[:, 1, :].rearrange("p (a b) -> p a b", b=W), idt_h[:, 0, :], idt_l[:, 0, :],
                                rh[v], rl[v], True, True).then_inc(qful, 1)

                    def stage_a(i, w, h):
                        conv3(i, w, h)
                        pointwise(i, w - 1, 1 - h)

                    def attention(i, c):
                        pe.wait_ge(mfree, 2 + MAIN * i + MB + c + 1)
                        for dc in range(4):
                            pe.wait_ge(qfree, Q * i + QY + 4 * c + dc + 1)
                            product(pe, ps_q[:, dc % 2, :], ga_h[:, dc, :], ga_l[:, dc, :], lh[:, c % 2, :],
                                    ll[:, c % 2, :], True, True).then_inc(qful, 1)

                    def conv5(i, v, h):
                        pe.wait_ge(y_l, NW * i + v + 2)
                        pe.wait_ge(mfree, MAIN * i + MC + v + 1)
                        o = ps_main[:, h, :].rearrange("p (a b) -> p a b", b=W)
                        for blk in range(3):
                            for kx in range(5):
                                a = (slice(None), h, slice(blk, blk + 4), slice(kx, kx + W))
                                mm = product(pe, o, c5_h[:, blk, kx, :], c5_l[:, blk, kx, :], yh[a], yl[a],
                                             blk + kx == 0, blk + kx == 6)
                        mm.then_inc(main, 1)

                    def body(i, last):
                        windows(pe, 1, lambda w, h: stage_a(i, w, h))
                        chain_pooled(pe, i, ((0, 1),), sums, chain)
                        pointwise(i, NW - 1, 1)
                        pe.wait_ge(f_z, 4 * (i + 1))
                        for c in range(4):
                            between = {}
                            if c == 0:
                                between = {4: lambda: chain_hidden(pe, i, 1, 1, pooled_s, chain),
                                           9: lambda: chain_taps(pe, i, 1, hdn_s, chain),
                                           NSTAT: lambda: dyn.at(pe, i, DSTEPS)}
                            pe.wait_ge(mfree, MAIN * i + MB + c + 1)
                            large_filter(pe, ps_main[:, c % 2, :].rearrange("p (n q) -> p n q", q=32), fh, fl,
                                         16 * c, 16, 32, between).then_inc(main, 1)
                            if c > 0:
                                attention(i, c - 1)
                        attention(i, 3)
                        group_mean_pe(pe, stats, i, avg)
                        group_var_pe(pe, stats, i, avg)
                        stats.at(pe, i, stats.per)
                        pe.wait_ge(e_in, i + 1)
                        alone(pe)
                        for kx in range(5):
                            for r in range(2):
                                hp = slice(r * C, r * C + C)
                                pe.matmul(ps_edge[hp, 0:W], row_w[hp, kx, :], rowf[hp, kx:kx + W], start=(kx == 0),
                                          stop=(kx == 4), skip_group_check=True)
                        for side in range(2):
                            c0 = W + side * NPAIR
                            for blk in range(3):
                                pe.matmul(ps_edge[:, c0:c0 + NPAIR], col_w[:, side, blk, :],
                                          colf[:, side, blk:blk + NPAIR], start=False, stop=False,
                                          skip_group_check=True)
                            for r, pair in ((0, 0), (1, NPAIR - 1)):
                                hp = par(r)
                                mm = pe.matmul(ps_edge[hp, c0 + pair:c0 + pair + 1], cor_w[hp, side, :],
                                               colf[hp, side, pair + 1:pair + 2], start=False, stop=True,
                                               skip_group_check=True)
                        mm.then_inc(e_mm, 1)
                        windows(pe, 0, lambda v, h: conv5(i, v, h))
                        if not last:
                            conv3(i + 1, 0, 0)

                    conv3(0, 0, 0)
                    with pe.Fori(0, B - 1) as i:
                        body(i, False)
                    body(B - 1, True)


def constants():
    tapmask = np.zeros((P, ND * 8, 9), np.float32)
    chmask = np.zeros((P, ATT), np.float32)
    slotmask = np.zeros((P, 8), np.float32)
    for dr, dc in PIX:
        s = slot(dr, dc)
        slotmask[s * ATT:s * ATT + ATT, s] = 1.0
        chmask[s * ATT:s * ATT + ATT] = np.eye(ATT)
        for t, (pb, cb) in enumerate(DYN):
            for er, ec in PIX:
                ky, kx = 2 * pb + dr - er - LK // 2 + 1, 4 * cb + dc - ec - LK // 2 + 1
                if 0 <= ky < 3 and 0 <= kx < 3:
                    tapmask[s * ATT:s * ATT + ATT, t * 8 + slot(er, ec), 3 * ky + kx] = 1.0
    ch = np.arange(P) % C // 2
    groupavg = (ch[:, None] == ch[None, :]).astype(np.float32) / 4
    return {"tapmask": tapmask, "chmask": chmask, "slotmask": slotmask, "groupavg": groupavg}


def kernel(x, L0_conv_ds_w3, L0_conv_ds_b3, L0_conv_ds_w1, L0_conv_ds_b1, L0_conv_kg_w1, L0_conv_kg_b1,
           L0_conv_kg_w2, L0_conv_kg_b2, L0_conv_lk_filter, L0_conv_fus_w, L0_conv_fus_b, L0_conv_fin_w,
           L0_conv_fin_b, L1_conv_w3, L1_conv_b3, L1_conv_w5, L1_conv_b5, L1_conv_wr, L1_conv_br):
    import concourse.bacc as bacc
    from concourse.bass_utils import run_bass_kernel_spmd

    a = np.asarray
    arrays = {
        "x": a(x),
        "w3t": a(L0_conv_ds_w3).transpose(0, 2, 3, 4, 1).reshape(LEVELS, C, 9, C),
        "w1t": a(L0_conv_ds_w1).transpose(0, 2, 1),
        "w1": a(L0_conv_ds_w1),
        "b3": a(L0_conv_ds_b3), "b1": a(L0_conv_ds_b1),
        "kgw1t": a(L0_conv_kg_w1).T, "kgb1": a(L0_conv_kg_b1),
        "kgw2": a(L0_conv_kg_w2).reshape(ATT, 9, ATT // 2).transpose(2, 1, 0),
        "kgb2": a(L0_conv_kg_b2).reshape(ATT, 9),
        "lkt": a(L0_conv_lk_filter).transpose(1, 2, 3, 0),
        "fus": a(L0_conv_fus_w), "fusb": a(L0_conv_fus_b),
        "fint": a(L0_conv_fin_w).T, "finb": a(L0_conv_fin_b),
        "c3t": a(L1_conv_w3).transpose(1, 2, 3, 0), "c5t": a(L1_conv_w5).transpose(1, 2, 3, 0),
        "c3b": a(L1_conv_b3), "c5b": a(L1_conv_b5),
        "wr": a(L1_conv_wr)[:, :, 0, 0], "wrt": a(L1_conv_wr)[:, :, 0, 0].T, "br": a(L1_conv_br),
        **constants(),
    }
    nc = bacc.Bacc("TRN2", target_bir_lowering=False, num_devices=1)
    feeds, aps = {}, {}
    for name, v in arrays.items():
        v = np.ascontiguousarray(v)
        feeds["in_" + name] = v
        aps[name] = nc.dram_tensor("in_" + name, v.shape, mybir.dt.from_np(v.dtype), kind="ExternalInput").ap()
    out = nc.dram_tensor("out_0", (B, C, H, W), F32, kind="ExternalOutput").ap()
    conv_kernel(nc, **aps, out=out)
    r = run_bass_kernel_spmd(nc, [feeds], core_ids=[0])
    return r.results[0]["out_0"]
```

```python
from contextlib import ExitStack

import numpy as np
import concourse.bass as bass
from concourse import mybir

F32 = mybir.dt.float32
F32R = mybir.dt.float32r
ALU = mybir.AluOpType
ACT = mybir.ActivationFunctionType
AX = mybir.AxisListType

P = 128
B, C, H, W = 8, 64, 128, 128
ATT = 16
NI = C - ATT
LK = 13
LEVELS = 4
EPS = 1e-5
NPAIR = H // 2
NPB, NCB = 7, 4
DYN = [(pb, cb) for pb in (2, 3, 4) for cb in (1, 2)]
ND = len(DYN)
NSTAT = NPB * NCB - ND
SIDE = {1: 64, 2: 32, 3: 16}
DIL = {1: 5, 2: 7, 3: 9}


def slot(dr, dc):
    return (dc // 2) * 4 + dr * 2 + dc % 2


def par(r):
    return slice((1 - r) * C, (2 - r) * C)


PIX = [(dr, dc) for dr in range(2) for dc in range(4)]


class Steps:

    def __init__(self, sem, per_image):
        self.sem, self.per, self.n = sem, per_image, 0

    def start(self, image):
        self.base, self.n = self.per * image, 0

    def done(self, ins):
        ins.then_inc(self.sem, 1)
        self.n += 1
        assert self.n <= self.per

    def wait(self, eng):
        eng.wait_ge(self.sem, self.base + self.n)

    def at(self, eng, image, n):
        eng.wait_ge(self.sem, self.per * image + n)


def conv_kernel(nc, x, w3t, w1t, w1, b3, b1, kgw1t, kgb1, kgw2, kgb2, lkt, fus, fusb, fint, finb,
                c3t, c5t, c3b, c5b, wr, wrt, br, tapmask, chmask, slotmask, groupavg, out):
    zs = nc.dram_tensor("z_level1", (B, C, NPAIR, W // 2), F32)
    zs2 = nc.dram_tensor("z_levels23", (B, C, H // 4, W // 4), F32)

    with ExitStack() as ctx:
        def sb(name, shape, dt=F32, stack=ctx):
            return stack.enter_context(nc.sbuf_tensor(name, shape, dt))

        def sem(name, stack=ctx):
            return stack.enter_context(nc.semaphore(name))

        def psum(name, shape):
            return ctx.enter_context(nc.psum_tensor(name, shape, F32))

        ps_main = psum("ps_main", [P, 2, 512])
        ps_q = psum("ps_q", [P, 2, 512])
        ps_stat = psum("ps_stat", [P, 512])
        ps_chain = psum("ps_chain", [P, 512])
        ps_edge = psum("ps_edge", [P, 512])
        ps_more = psum("ps_more", [P, 512])

        lk_h = sb("lk_h", [P, NPB, NCB, P], F32R)
        lk_l = sb("lk_l", [P, NPB, NCB, P], F32R)
        lk_base = sb("lk_base", [P, ND, P])
        idt_h = sb("idt_h", [P, LEVELS, P], F32R)
        idt_l = sb("idt_l", [P, LEVELS, P], F32R)
        gn0 = sb("gn0", [P, B, 2])
        gar = sb("gar", [P, C])
        w1a = sb("w1a", [P, LEVELS, ATT])
        b1a = sb("b1a", [P, LEVELS])
        b3p = sb("b3p", [P, LEVELS])
        kg1 = sb("kg1", [ATT, ATT // 2])
        kb1 = sb("kb1", [ATT // 2, 1])
        kg2 = sb("kg2", [ATT // 2, 9, P])
        kb2 = sb("kb2", [P, 9])
        c5_h = sb("c5_h", [P, 3, 5, P], F32R)
        c5_l = sb("c5_l", [P, 3, 5, P], F32R)
        row_w = sb("row_w", [P, 5, C])
        col_w = sb("col_w", [P, 2, 3, P])
        cor_w = sb("cor_w", [P, 2, C])
        edge_b = sb("edge_b", [P, 256])
        out_b = sb("out_b", [P, 1])
        tapm = sb("tapm", [P, ND * 8, 9])
        chm = sb("chm", [P, ATT])
        slm = sb("slm", [P, 8])
        gav = sb("gav", [P, P])
        bz = sb("bz", [P, 1])
        small = sb("small", [P, 64])
        dcoef = sb("dcoef", [P, ND * 8])
        dker = sb("dker", [P, ND * P])
        dtap = dker[:, 0:ND * 8 * 9].rearrange("p (m t) -> p m t", t=9)
        kerr = sb("kerr", [P, 4, 9])
        stat = sb("stat", [P, 16, 6])

        passed = sem("passed")

        def alone(eng):
            eng.sem_inc(passed, 1)

        with ExitStack() as st:
            s_ld = sem("s_ld", st)
            s_lks = sem("s_lks", st)
            s_zero = sem("s_zero", st)
            s_hi = sem("s_hi", st)
            s_lo = sem("s_lo", st)
            s_mm = sem("s_mm", st)
            s_cp = sem("s_cp", st)
            lks = sb("lks", [P, 14, 16, ATT], stack=st)
            fus_s = sb("fus_s", [C, C], stack=st)
            fus_r = sb("fus_r", [C, 8, ATT], stack=st)
            fin_s = sb("fin_s", [C, 2, C], stack=st)
            fusb_s = sb("fusb_s", [C, 1], stack=st)
            finb_s = sb("finb_s", [P, 1], stack=st)
            w1i = sb("w1i", [NI, LEVELS, 2, C], stack=st)
            b1i = sb("b1i", [NI, LEVELS], stack=st)
            gti = sb("gti", [NI, 2, C], stack=st)
            idt = sb("idt", [P, LEVELS, P], stack=st)
            s31 = sb("s31", [P, 4, 3, C], stack=st)
            c5 = sb("c5", [P, 6, 5, C], stack=st)
            wrb = sb("wrb", [P, 10, C], stack=st)
            tmp = sb("tmp", [P, 4, 3, C], stack=st)
            cls = sb("cls", [P, 2, 6, C], stack=st)
            wrs = sb("wrs", [P, 10], stack=st)
            bb = sb("bb", [P, 8], stack=st)
            tile5 = sb("tile5", [P, 3, 5, P], stack=st)
            l1_z = sem("l1_z", st)
            l1_ld = sem("l1_ld", st)
            steps = Steps(sem("l1_s", st), 200)

            def g(sh, sw):
                return 1 + 3 * sh + sw

            b1t = b1.rearrange("l c -> c l")
            b3t = b3.rearrange("l c -> c l")
            loads = [(fus_s[:, :], fus), (fusb_s[:, :], fusb.rearrange("(c a) -> c a", a=1)),
                     (kg1[:, :], kgw1t), (kb1[:, :], kgb1.rearrange("(c a) -> c a", a=1)),
                     (tapm[:, :, :], tapmask), (chm[:, :], chmask), (slm[:, :], slotmask), (gav[:, :], groupavg),
                     (b1i[:, :], b1t[ATT:, :])]
            for r in range(2):
                hp = slice(r * C, r * C + C)
                loads += [(fin_s[:, r, :], fint), (w1i[:, :, r, :], w1.rearrange("l o c -> o l c")[ATT:, :, :]),
                          (w1a[hp, :, :], w1t.rearrange("l c o -> c l o")[:, :, 0:ATT]),
                          (finb_s[hp, :], finb.rearrange("(c a) -> c a", a=1)), (b3p[hp, :], b3t)]
            for s in range(8):
                sp16 = slice(s * ATT, s * ATT + ATT)
                loads += [(fus_r[:, s, :], fus[:, 0:ATT]), (b1a[sp16, :], b1t[0:ATT, :]),
                          (kb2[sp16, :], kgb2), (kg2[:, :, sp16], kgw2)]
            NLD = len(loads)
            pieces = [(pb, dr, dc) for pb in range(NPB) for dr, dc in PIX]

            with nc.Block() as block:
                @block.sync
                def _(sp):
                    with nc.allow_non_contiguous_dma(reason="small weight layouts"):
                        sp.wait_ge(l1_z, 2)
                        for r in range(2):
                            sp.dma_start(s31[par(r), 1 - r:4 - r, :, :], c3t).then_inc(l1_ld, 16)
                            sp.dma_start(c5[par(r), 1 - r:6 - r, :, :], c5t).then_inc(l1_ld, 16)
                        sp.dma_start(wrb[:, :, :], wrt.unsqueeze(0).to_broadcast([P, 10, C])).then_inc(l1_ld, 16)
                        for r in range(2):
                            hp = slice(r * C, r * C + C)
                            sp.dma_start(wrs[hp, :], wr).then_inc(l1_ld, 16)
                            for k, v in enumerate((c3b, c5b, br)):
                                sp.dma_start(bb[hp, k:k + 1], v.rearrange("(c a) -> c a", a=1)).then_inc(l1_ld, 16)
                        sp.wait_ge(s_zero, 1)
                        for dr, dc in PIX:
                            q = slot(dr, dc) * ATT
                            sp.dma_start(lks[q:q + ATT, 1 - dr:14 - dr, 3 - dc:16 - dc, :], lkt).then_inc(s_lks, 16)
                        for d, s in loads:
                            sp.dma_start(d, s).then_inc(s_ld, 16)

                @block.gpsimd
                def _(pool):
                    pool.memset(lks[:, :, :, :], 0.0).then_inc(s_zero, 1)
                    pool.memset(idt[:, :, :], 0.0).then_inc(s_zero, 1)
                    pool.wait_ge(s_lks, 16 * 8)
                    for k, (pb, dr, dc) in enumerate(pieces):
                        src = lks[:, 2 * pb - dr + 1, 3 - dc:16 - dc:4, :]
                        q = slot(dr, dc) * ATT
                        pool.wait_ge(s_hi, k + 1)
                        pool.tensor_tensor(lk_l[:, pb, :, q:q + ATT], src, lk_h[:, pb, :, q:q + ATT].bitcast(F32),
                                           ALU.subtract).then_inc(s_lo, 1)

                @block.scalar
                def _(act):
                    act.wait_ge(s_lks, 16 * 8)
                    for pb, dr, dc in pieces:
                        src = lks[:, 2 * pb - dr + 1, 3 - dc:16 - dc:4, :]
                        q = slot(dr, dc) * ATT
                        act.activation(lk_h[:, pb, :, q:q + ATT], src, ACT.Identity).then_inc(s_hi, 1)
                    for pb, dr, dc in pieces:
                        if pb in (2, 3, 4):
                            q, t = slot(dr, dc) * ATT, (pb - 2) * 2
                            act.activation(lk_base[:, t:t + 2, q:q + ATT], lks[:, 2 * pb - dr + 1, 3 - dc:16 - dc:4, :]
                                           [:, 1:3, :], ACT.Identity).then_inc(s_lo, 1)

                @block.vector
                def _(dve):
                    steps.start(0)

                    def step(ins):
                        steps.done(ins)
                        steps.wait(dve)

                    for t in (s31, c5):
                        dve.memset(t[:, :, :, :], 0.0).then_inc(l1_z, 1)
                    step(dve.memset(row_w[:, :, :], 0.0))
                    step(dve.memset(cls[:, :, :, :], 0.0))
                    dve.wait_ge(l1_ld, 16 * 13)
                    step(dve.tensor_tensor(c5[:, :, :, :].rearrange("p a b c -> p (a b) c"),
                                           c5[:, :, :, :].rearrange("p a b c -> p (a b) c"),
                                           wrb[:, 0, :].unsqueeze(1).to_broadcast([P, 30, C]), ALU.mult))
                    for sh in range(3):
                        for sw in range(3):
                            step(dve.tensor_tensor(tmp[:, :, :, :].rearrange("p a b c -> p (a b) c"),
                                                   s31[:, :, :, :].rearrange("p a b c -> p (a b) c"),
                                                   wrb[:, g(sh, sw), :].unsqueeze(1).to_broadcast([P, 12, C]),
                                                   ALU.mult))
                            d = c5[:, 2 - sw:6 - sw, 2 - sh:5 - sh, :]
                            step(dve.tensor_tensor(d, d, tmp[:, :, :, :], ALU.add))
                            for side, h0, kx in ((0, 2, 2), (1, 0, 0)):
                                if sh == h0:
                                    d = cls[:, side, 2 - sw:6 - sw, :]
                                    step(dve.tensor_tensor(d, d, tmp[:, :, kx, :], ALU.add))
                            for r, w0, a in ((0, 2, 3), (1, 0, 0)):
                                hp = par(r)
                                if sw == w0:
                                    d = row_w[hp, 2 - sh:5 - sh, :]
                                    step(dve.tensor_tensor(d, d, tmp[hp, a, :, :], ALU.add))
                                    for side, h0, kx in ((0, 2, 2), (1, 0, 0)):
                                        if sh == h0:
                                            step(dve.tensor_scalar(cor_w[hp, side, :], tmp[hp, a, kx, :], -1.0,
                                                                   None, ALU.mult))
                    for blk in range(3):
                        for m in range(2):
                            step(dve.tensor_copy(tile5[:, blk, :, par(m)], c5[:, 2 * blk - m + 1, :, :]))
                            step(dve.tensor_copy(col_w[:, :, blk, par(m)], cls[:, :, 2 * blk - m + 1, :]))
                    step(dve.tensor_copy(c5_h[:, :, :, :], tile5[:, :, :, :]))
                    step(dve.tensor_tensor(c5_l[:, :, :, :], tile5[:, :, :, :], c5_h[:, :, :, :].bitcast(F32),
                                           ALU.subtract))
                    dve.wait_ge(s_ld, 16 * NLD)
                    dve.wait_ge(s_mm, 1)
                    dve.tensor_copy(gti[:, :, :], ps_main[0:NI, 0, 0:P]).then_inc(s_cp, 1)
                    dve.tensor_copy(gar[:, :], ps_main[:, 0, P:P + C]).then_inc(s_cp, 1)
                    b_3, b_5, b_r, t = (bb[:, k:k + 1] for k in range(4))
                    step(dve.tensor_reduce(t, wrs[:, 1:10], AX.X, ALU.add))
                    step(dve.scalar_tensor_tensor(out_b[:, :], t, b_3, b_r, ALU.mult, ALU.add))
                    step(dve.scalar_tensor_tensor(out_b[:, :], wrs[:, 0:1], b_5, out_b[:, :], ALU.mult, ALU.add))
                    step(dve.memset(edge_b[:, :], 1.0))
                    for r, w0, pair in ((0, 2, 0), (1, 0, NPAIR - 1)):
                        hp = par(r)
                        step(dve.tensor_reduce(t[hp], wrs[hp, g(0, w0):g(2, w0) + 1:3], AX.X, ALU.add))
                        step(dve.tensor_scalar(edge_b[hp, 0:W], edge_b[hp, 0:W], t[hp], b_3[hp], ALU.mult, ALU.mult))
                    for side, h0 in ((0, 2), (1, 0)):
                        e = edge_b[:, W + side * NPAIR:W + side * NPAIR + NPAIR]
                        step(dve.tensor_reduce(t, wrs[:, g(h0, 0):g(h0, 2) + 1], AX.X, ALU.add))
                        step(dve.tensor_scalar(e, e, t, b_3, ALU.mult, ALU.mult))
                        for r, w0, pair in ((0, 2, 0), (1, 0, NPAIR - 1)):
                            hp, k = par(r), g(h0, w0)
                            step(dve.tensor_scalar(t[hp], wrs[hp, k:k + 1], b_3[hp], None, ALU.mult))
                            step(dve.tensor_tensor(e[hp, pair:pair + 1], e[hp, pair:pair + 1], t[hp], ALU.subtract))

                    dve.wait_ge(s_mm, 2)
                    dve.wait_ge(s_zero, 2)
                    for r in range(2):
                        hp = slice(r * C, r * C + C)
                        dve.tensor_copy(idt[hp, :, r * C:r * C + C],
                                        ps_q[hp, 0, 0:LEVELS * C].rearrange("p (l o) -> p l o", o=C)).then_inc(s_cp, 1)
                    dve.tensor_tensor(bz[:, :], ps_q[:, 1, 0:1], finb_s[:, :], ALU.add).then_inc(s_cp, 1)
                    dve.wait_ge(s_cp, 5)
                    dve.tensor_copy(idt_h[:, :, :], idt[:, :, :]).then_inc(s_cp, 1)
                    dve.wait_ge(s_cp, 6)
                    dve.tensor_tensor(idt_l[:, :, :], idt[:, :, :], idt_h[:, :, :].bitcast(F32),
                                      ALU.subtract).then_inc(s_cp, 1)

                @block.tensor
                def _(pe):
                    pe.wait_ge(s_ld, 16 * NLD)
                    pe.matmul(ps_main[0:NI, 0, 0:P], fus_s[:, ATT:C], fin_s[:, :, :], start=True, stop=True)
                    pe.matmul(ps_main[:, 0, P:P + C], fus_r[:, :, :], fin_s[:, 0, :], start=True,
                              stop=True, skip_group_check=True).then_inc(s_mm, 1)
                    pe.wait_ge(s_cp, 2)
                    for lv in range(LEVELS):
                        pe.matmul(ps_q[:, 0, lv * C:lv * C + C], w1i[:, lv, :, :], gti[:, 0, :],
                                  start=(lv == 0), stop=True, skip_group_check=True)
                    for lv in range(LEVELS):
                        pe.matmul(ps_q[:, 1, 0:1], gti[:, :, :], b1i[:, lv:lv + 1], start=(lv == 0), stop=False)
                    for lv in range(LEVELS):
                        mm = pe.matmul(ps_q[:, 1, 0:1], fin_s[:, :, :], fusb_s[:, :], start=False,
                                       stop=(lv == LEVELS - 1))
                    mm.then_inc(s_mm, 1)

        def product(pe, o, wh, wl, xh, xl, first, last):
            pe.matmul(o, wh, xh, start=first, stop=False, skip_group_check=True)
            pe.matmul(o, wh, xl, start=False, stop=False, skip_group_check=True)
            return pe.matmul(o, wl, xh, start=False, stop=last, skip_group_check=True)

        def large_filter(pe, o, fh, fl, p0, np_, nq, between):
            tiles = [(pb, cb) for pb in range(NPB) for cb in range(NCB) if (pb, cb) not in DYN] + DYN
            for k, (pb, cb) in enumerate(tiles):
                if k in between:
                    between[k]()
                v = (slice(None), slice(p0 + pb, p0 + pb + np_), slice(cb, cb + nq))
                mm = product(pe, o, lk_h[:, pb, cb, :], lk_l[:, pb, cb, :], fh[v], fl[v],
                             k == 0, k == len(tiles) - 1)
            return mm

        def lk_mid(t):
            return t[:, 2:5, 1:3, :].rearrange("p b c m -> p b (c m)")

        def dynamic_tiles(dve, steps, ker, hi, lo):
            steps.done(dve.tensor_tensor(dtap[:, :, :], tapm[:, :, :],
                                         ker.unsqueeze(1).to_broadcast([P, ND * 8, 9]), ALU.mult))
            steps.wait(dve)
            steps.done(dve.tensor_reduce(dcoef[:, :], dtap[:, :, :], AX.X, ALU.add))
            steps.wait(dve)
            steps.done(dve.tensor_tensor(dker[:, :].rearrange("p (m c) -> p m c", c=ATT),
                                         dcoef[:, :].unsqueeze(2).to_broadcast([P, ND * 8, ATT]),
                                         chm[:, :].unsqueeze(1).to_broadcast([P, ND * 8, ATT]), ALU.mult))
            steps.wait(dve)
            steps.done(dve.tensor_tensor(dker[:, :], dker[:, :], lk_base[:, :, :].rearrange("p t m -> p (t m)"),
                                         ALU.add))
            steps.wait(dve)
            dk = dker[:, :].rearrange("p (b m) -> p b m", b=3)
            steps.done(dve.tensor_copy(hi, dk))
            steps.wait(dve)
            steps.done(dve.tensor_tensor(lo, dk, hi.bitcast(F32), ALU.subtract))
        DSTEPS = 6

        def group_stats_dve(dve, steps, averaged, rooted, image, entries, mean, rstd):
            mv, dm, tv, vv, sd = (small[:, 0:2], small[:, 2:3], small[:, 3:4], small[:, 4:5], small[:, 5:6])
            steps.done(dve.bn_aggr(mv, entries))
            averaged(2 * image + 1)
            steps.done(dve.tensor_copy(mean, ps_stat[:, 0:1]))
            steps.wait(dve)
            steps.done(dve.tensor_tensor(dm, mv[:, 0:1], mean, ALU.subtract))
            steps.wait(dve)
            steps.done(dve.scalar_tensor_tensor(tv, dm, dm, mv[:, 1:2], ALU.mult, ALU.add))
            averaged(2 * image + 2)
            steps.done(dve.tensor_scalar(vv, ps_stat[:, 1:2], EPS, None, ALU.add))
            rooted(image + 1)
            steps.done(dve.reciprocal(rstd, sd))
            steps.wait(dve)
        GSTEPS = 6

        def group_mean_pe(pe, steps, image, s_avg):
            steps.at(pe, image, 1)
            pe.matmul(ps_stat[:, 0:1], gav[:, :], small[:, 0:1], start=True, stop=True,
                      skip_group_check=True).then_inc(s_avg, 1)

        def group_var_pe(pe, steps, image, s_avg):
            steps.at(pe, image, 4)
            pe.matmul(ps_stat[:, 1:2], gav[:, :], small[:, 3:4], start=True, stop=True,
                      skip_group_check=True).then_inc(s_avg, 1)

        def group_stats_act(act, steps, image, s_root):
            steps.at(act, image, 5)
            act.activation(small[:, 5:6], small[:, 4:5], ACT.Sqrt).then_inc(s_root, 1)

        def chain_pooled(pe, image, parts, s_sum, s_chain):
            if s_sum is not None:
                s_sum.at(pe, image, s_sum.per)
            k = 0
            for lv, n in parts:
                mm = pe.matmul(ps_chain[0:ATT, k:k + n], w1a[:, lv, :], rsum[:, k:k + n], start=(k == 0),
                               stop=True, skip_group_check=True)
                k += n
            mm.then_inc(s_chain, 1)

        def chain_hidden(pe, image, n, nparts, s_pooled, s_chain):
            pe.wait_ge(s_pooled, nparts * (image + 1))
            alone(pe)
            pe.matmul(ps_chain[0:ATT // 2, 8:8 + n], kg1[:, :], pooled[:, 0:n], start=True, stop=True,
                      skip_group_check=True).then_inc(s_chain, 1)

        def chain_taps(pe, image, n, s_hdn, s_chain):
            pe.wait_ge(s_hdn, image + 1)
            for t in range(9):
                mm = pe.matmul(ps_chain[:, 16 + n * t:16 + n * t + n], kg2[:, t, :], hdn[:, 0:n],
                               start=(t == 0), stop=True, skip_group_check=True)
            mm.then_inc(s_chain, 1)

        def chain_pooled_dve(dve, image, parts, s_pooled, s_chain):
            dve.wait_ge(s_chain, 3 * image + 1)
            k = 0
            for lv, n in parts:
                side = SIDE.get(lv, H)
                dve.tensor_scalar(pooled[:, k:k + n], ps_chain[0:ATT, k:k + n], 1.0 / (side * side),
                                  b1a[0:ATT, lv:lv + 1], ALU.mult, ALU.add).then_inc(s_pooled, 1)
                k += n

        def chain_taps_dve(dve, image, n, s_chain, s_ker):
            dve.wait_ge(s_chain, 3 * image + 3)
            dve.tensor_tensor(kerr[:, 0:n, :], ps_chain[:, 16:16 + 9 * n].rearrange("p (t k) -> p k t", k=n),
                              kb2[:, :].unsqueeze(1).to_broadcast([P, n, 9]), ALU.add).then_inc(s_ker, 1)

        def chain_act(act, image, n, s_chain, s_hdn):
            act.wait_ge(s_chain, 3 * image + 2)
            act.activation(hdn[:, 0:n], ps_chain[0:ATT // 2, 8:8 + n], ACT.Gelu, bias=kb1[:, 0:1]).then_inc(s_hdn, 1)

        rsum = sb("rsum", [P, 4])
        pooled = sb("pooled", [ATT, 4])
        hdn = sb("hdn", [ATT // 2, 4])

        st1 = ctx.enter_context(ExitStack())
        half = {lv: SIDE[lv] // 2 for lv in SIDE}
        prow = {lv: half[lv] + 2 * DIL[lv] for lv in SIDE}
        plen = {lv: SIDE[lv] + DIL[lv] + (SIDE[lv] + DIL[lv]) % 2 for lv in SIDE}
        p2 = sb("p2", [P, B, half[2], SIDE[2]], stack=st1)
        w3h = sb("w3h", [P, 3, 9, P], F32R, stack=st1)
        w3l = sb("w3l", [P, 3, 9, P], F32R, stack=st1)
        fa_h = sb("fa_h", [P, 3, 240], F32R, stack=st1)
        fa_l = sb("fa_l", [P, 3, 240], F32R, stack=st1)
        ga_h = sb("ga_h", [P, 8 * P + C], F32R, stack=st1)
        ga_l = sb("ga_l", [P, 8 * P + C], F32R, stack=st1)

        def quad_sum(pool, dst, v, s_acc, count):
            alone(pool)
            pool.tensor_tensor(dst, v(0, 0), v(0, 1), ALU.add).then_inc(s_acc, 1)
            pool.wait_ge(s_acc, count + 1)
            alone(pool)
            pool.tensor_tensor(dst, dst, v(1, 0), ALU.add).then_inc(s_acc, 1)
            pool.wait_ge(s_acc, count + 2)
            alone(pool)
            return pool.tensor_tensor(dst, dst, v(1, 1), ALU.add)

        with ExitStack() as st:
            def s1(name):
                return sem("p1_" + name, st)

            D1, S1, N1 = DIL[1], SIDE[1], half[1]
            NB1, NQ1 = N1 // 2, S1 // 4
            LEN1 = prow[1] * plen[1] + 2 * D1
            xc = sb("xc", [P, 2, 8, W], stack=st)
            pl1 = sb("pl1", [P, prow[1], S1], stack=st)
            nh = sb("nh1", [P, LEN1], F32R, stack=st)
            nl = sb("nl1", [P, LEN1], F32R, stack=st)
            rf = sb("rf1", [P, 2, 512], stack=st)
            rh = sb("rh1", [P, N1, S1 + 8], F32R, stack=st)
            rl = sb("rl1", [P, N1, S1 + 8], F32R, stack=st)
            fh = sb("fh1", [P, N1 + 6, NQ1 + 4], F32R, stack=st)
            fl = sb("fl1", [P, N1 + 6, NQ1 + 4], F32R, stack=st)
            z1 = sb("z1", [P, N1, S1], stack=st)
            lh = sb("lh1", [P, 512], F32R, stack=st)
            ll = sb("ll1", [P, 512], F32R, stack=st)
            rs = sb("rs1", [P, 4], stack=st)
            coef = sb("coef1", [P, 2], stack=st)
            zeros = sb("zeros1", [P, D1 * S1], stack=st)
            gst = sb("gst", [P, C], stack=st)
            stage = z1[:, :, :].rearrange("p a b -> p (a b)")[:, 0:9 * P].rearrange("p (t m) -> p t m", m=P)
            a_z = s1("a_z")
            a_ld = s1("a_ld")
            a_s = s1("a_s")
            a_p = s1("a_p")
            a_b = s1("a_b")
            a_g = s1("a_g")

            NA_G = 3 + 3 * 8
            NX = 8
            NCH = S1 // 16
            QF, QL, QY = 3, 5, 6
            Q = QY + 8
            pieces = [(0, 8 + 2 * D1)] + [(8 * k + 2 * D1, 8 * k + 8 + 2 * D1) for k in range(1, NCH)]
            xc_full = [s1("xc_full0"), s1("xc_full1")]
            bn_done = s1("bn_done")
            pl_done = s1("pl_done")
            p_acc = s1("p_acc")
            p2_done = s1("p2_done")
            halo = s1("halo")
            stats = Steps(s1("stats"), GSTEPS + 4)
            avg, root = s1("avg"), s1("root")
            n_f = s1("n_f")
            n_h = s1("n_h")
            n_l = s1("n_l")
            main = s1("main")
            mfree = s1("mfree")
            qful, qfree = s1("qful"), s1("qfree")
            r_h = s1("r_h")
            r_l = s1("r_l")
            f_h = s1("f_h")
            f_z = s1("f_z")
            sums = Steps(s1("sums"), 1)
            pooled_s, chain, hdn_s, ker_s = s1("pooled"), s1("chain"), s1("hdn"), s1("ker")
            dyn = Steps(s1("dyn"), DSTEPS)
            lk_f = s1("lk_f")
            l_h = s1("l_h")
            l_l = s1("l_l")
            zst = s1("zst")
            ps_lk = ps_edge

            def nview(a, r0, r1):
                return a[:, D1:D1 + prow[1] * plen[1]].rearrange("p (r c) -> p r c", c=plen[1])[:, r0:r1, 0:S1]

            def prep_at(k, last):
                return [] if last else [(0, 1), (2, 3), (4,), ()][k]

            with nc.Block() as block:
                @block.sync
                def _(sp):
                    sp.sem_inc(bn_done, 4)
                    sp.sem_inc(pl_done, 2)
                    sp.sem_inc(mfree, 2)
                    sp.sem_inc(qfree, 2)
                    sp.sem_inc(r_l, 2)
                    sp.sem_inc(l_l, 1)
                    sp.sem_inc(zst, 16)

                    def prep(i):
                        with sp.Fori(0, NX // 2) as t:
                            for h in range(2):
                                sp.wait_ge(bn_done, 2 * (NX * i + 2 * t + h + 1))
                                sp.wait_ge(pl_done, NX * i + 2 * t + h + 1)
                                for r in range(2):
                                    sp.dma_start(xc[r * C:r * C + C, h, :, :],
                                                 x[i, :, bass.ds(t * 16 + (8 * h + r * (H // 2)), 8), :]
                                                 ).then_inc(xc_full[h], 16)
                        sp.wait_ge(pl_done, 2 + NX * (i + 1))
                        alone(sp)
                        sp.dma_start(pl1[0:C, D1 + N1:N1 + 2 * D1, :], pl1[C:P, D1:2 * D1, :]).then_inc(halo, 16)
                        sp.dma_start(pl1[C:P, 0:D1, :], pl1[0:C, N1:D1 + N1, :]).then_inc(halo, 16)

                    def store(i):
                        sp.wait_ge(qfree, 2 + Q * (i + 1))
                        alone(sp)
                        for r in range(2):
                            sp.dma_start(zs.ap()[i, :, N1 * r:N1 * r + N1, :],
                                         z1[r * C:r * C + C, :, :]).then_inc(zst, 16)

                    prep(0)
                    with sp.Fori(0, B - 1) as i:
                        prep(i + 1)
                        store(i)
                    store(B - 1)
                    sp.wait_ge(zst, 16 + 32 * B)

                @block.gpsimd
                def _(pool):
                    def prep_chunk(i, c):
                        pool.wait_ge(xc_full[c % 2], 32 * (NX // 2 * i + c // 2 + 1))
                        v = xc[:, c % 2, :, :].rearrange("p (r a) (c b) -> p r a c b", a=2, b=2)
                        quad_sum(pool, pl1[:, D1 + 4 * c:D1 + 4 * c + 4, :], lambda a, b: v[:, :, a, :, b], p_acc,
                                 i * (2 * NX + 2) + 2 * c).then_inc(pl_done, 1)

                    def prep_rest(i):
                        pool.wait_ge(pl_done, 2 + NX * (i + 1))
                        v = pl1[:, D1:D1 + N1, :].rearrange("p (r a) (c b) -> p r a c b", a=2, b=2)
                        quad_sum(pool, p2[:, bass.ds(i, 1), :, :].rearrange("p i r c -> p (i r) c"),
                                 lambda a, b: v[:, :, a, :, b], p_acc, i * (2 * NX + 2) + 2 * NX).then_inc(p2_done, 1)

                    def norm(i):
                        for k, (r0, r1) in enumerate(pieces):
                            pool.wait_ge(n_h, NCH * i + k + 1)
                            pool.tensor_tensor(nview(nl, r0, r1), pl1[:, r0:r1, :], nview(nh, r0, r1).bitcast(F32),
                                               ALU.subtract).then_inc(n_l, 1)

                    def body(i, last):
                        pool.wait_ge(n_l, NCH * (i + 1))
                        alone(pool)
                        for k in range(NCH):
                            pool.wait_ge(r_h, NCH * i + k + 1)
                            r = slice(8 * k, 8 * k + 8)
                            pool.tensor_tensor(rl[:, r, 2:2 + S1],
                                               rf[:, k % 2, :].rearrange("p (r c) -> p r c", c=S1),
                                               rh[:, r, 2:2 + S1].bitcast(F32), ALU.subtract).then_inc(r_l, 1)
                            for c in prep_at(k, last):
                                prep_chunk(i + 1, c)
                        pool.wait_ge(qfree, 2 + Q * i + QL)
                        alone(pool)
                        for t in (fh, fl):
                            pool.memset(t[0:C, 3:3 + N1, 1:2].bitcast(F32), 0.0).then_inc(f_z, 1)
                            pool.memset(t[C:P, 3:3 + N1, 1 + NQ1:2 + NQ1].bitcast(F32), 0.0).then_inc(f_z, 1)
                        pool.wait_ge(f_z, 4 * (i + 1))
                        alone(pool)
                        if not last:
                            for c in range(NX - 3, NX):
                                prep_chunk(i + 1, c)
                            prep_rest(i + 1)
                            norm(i + 1)

                    for t in (nh, nl):
                        pool.memset(t[:, :].bitcast(F32), 0.0).then_inc(a_p, 1)
                    for t in (rh, rl, fh, fl):
                        pool.memset(t[:, :, :].bitcast(F32), 0.0).then_inc(a_p, 1)
                    pool.memset(zeros[:, :], 0.0).then_inc(a_p, 1)
                    pool.wait_ge(a_p, 7)
                    for c in range(NX):
                        prep_chunk(0, c)
                    prep_rest(0)
                    norm(0)
                    with pool.Fori(0, B - 1) as i:
                        body(i, False)
                    body(B - 1, True)

                @block.scalar
                def _(act):
                    def norm(i, k):
                        r0, r1 = pieces[k]
                        act.wait_ge(n_f, NCH * i + k + 1)
                        act.activation(nview(nh, r0, r1), pl1[:, r0:r1, :], ACT.Identity).then_inc(n_h, 1)

                    def body(i, last):
                        for k in range(NCH):
                            act.wait_ge(main, NCH * i + k + 1)
                            act.wait_ge(r_l, NCH * i + k + 1)
                            act.activation(rf[:, k % 2, :], ps_main[:, k % 2, :], ACT.Relu,
                                           bias=b3p[:, 1:2], accum_out=rs[:, k:k + 1]).then_inc(mfree, 1)
                        for hf in range(2):
                            act.wait_ge(qful, Q * i + QF + hf + 1)
                            p0 = 3 + NB1 * hf
                            ps = ps_q[:, 1 - hf, 0:NB1 * (NQ1 + 2)].rearrange("p (n q) -> p n q", q=NQ1 + 2)
                            act.activation(fh[:, p0:p0 + NB1, 1:NQ1 + 2], ps[:, :, 0:NQ1 + 1], ACT.Identity,
                                           bias=b1a[:, 1:2]).then_inc(f_h, 1)
                        chain_act(act, i, 1, chain, hdn_s)
                        if not last:
                            group_stats_act(act, stats, i + 1, root)
                        act.wait_ge(lk_f, i + 1)
                        act.activation(lh[:, :], ps_lk[:, :], ACT.Identity).then_inc(l_h, 1)
                        if not last:
                            for k in range(NCH):
                                norm(i + 1, k)

                    for k in range(3):
                        if k == 0:
                            act.wait_ge(a_z, 1)
                        else:
                            act.wait_ge(a_s, 2 * k)
                        for r in range(2):
                            hp = slice(r * C, r * C + C)
                            act.dma_start(stage[hp, :, hp], w3t[k + 1]).then_inc(a_ld, 16)
                    act.wait_ge(a_p, 7)
                    group_stats_act(act, stats, 0, root)
                    for k in range(NCH):
                        norm(0, k)
                    with act.Fori(0, B - 1) as i:
                        body(i, False)
                    body(B - 1, True)

                @block.vector
                def _(dve):
                    def prep_chunk(i, c):
                        dve.wait_ge(xc_full[c % 2], 32 * (NX // 2 * i + c // 2 + 1))
                        for e in range(2):
                            dve.bn_stats(stat[:, 2 * c + e, :],
                                         xc[:, c % 2, 4 * e:4 * e + 4, :].rearrange("p a b -> p (a b)")).then_inc(bn_done, 1)

                    def prep_rest(i):
                        dve.wait_ge(bn_done, 4 + 2 * NX * (i + 1))
                        alone(dve)
                        stats.start(i)
                        mean, rstd = gn0[:, bass.ds(i, 1), 0], gn0[:, bass.ds(i, 1), 1]
                        group_stats_dve(dve, stats, lambda v: dve.wait_ge(avg, v), lambda v: dve.wait_ge(root, v),
                                        i, stat[:, :, :].rearrange("p a b -> p (a b)"), mean, rstd)
                        k2 = float((H // S1) ** 2)
                        stats.done(dve.tensor_scalar(coef[:, 0:1], mean, k2, None, ALU.mult))
                        stats.done(dve.tensor_scalar(coef[:, 1:2], rstd, 1.0 / k2, None, ALU.mult))
                        stats.wait(dve)
                        for hf, r0 in ((0, 0), (1, D1 + N1)):
                            hp = slice(hf * C, hf * C + C)
                            stats.done(dve.tensor_scalar(pl1[hp, r0:r0 + D1, :].rearrange("p a b -> p (a b)"),
                                                         zeros[hp, :], coef[hp, 0:1], None, ALU.add))
                        stats.wait(dve)
                        dve.wait_ge(halo, 32 * (i + 1))
                        dve.wait_ge(p2_done, i + 1)

                    def norm(i, k):
                        r0, r1 = pieces[k]
                        dve.tensor_scalar(pl1[:, r0:r1, :], pl1[:, r0:r1, :], coef[:, 0:1], coef[:, 1:2],
                                          ALU.subtract, ALU.mult).then_inc(n_f, 1)

                    def plain(i, k):
                        u = k if k < 3 else QL
                        dve.wait_ge(qful, Q * i + u + 1)
                        dve.tensor_copy(z1[:, 8 * k:8 * k + 8, :].rearrange("p a b -> p (a b)"),
                                        ps_q[:, u % 2, :]).then_inc(qfree, 1)

                    def body(i, last):
                        for k in range(NCH):
                            dve.wait_ge(mfree, 2 + NCH * i + k + 1)
                            dve.tensor_copy(rh[:, 8 * k:8 * k + 8, 2:2 + S1],
                                            rf[:, k % 2, :].rearrange("p (r c) -> p r c", c=S1)).then_inc(r_h, 1)
                            for c in prep_at(k, last):
                                prep_chunk(i + 1, c)
                        sums.start(i)
                        sums.done(dve.tensor_reduce(rsum[:, 0:1], rs[:, :], AX.X, ALU.add))
                        dve.wait_ge(zst, 16 + 32 * i)
                        for k in range(3):
                            plain(i, k)
                        for hf in range(2):
                            dve.wait_ge(f_h, 2 * i + hf + 1)
                            p0 = 3 + NB1 * hf
                            ps = ps_q[:, 1 - hf, 0:NB1 * (NQ1 + 2)].rearrange("p (n q) -> p n q", q=NQ1 + 2)
                            dve.scalar_tensor_tensor(fl[:, p0:p0 + NB1, 1:NQ1 + 2], ps[:, :, 0:NQ1 + 1],
                                                     b1a[:, 1:2], fh[:, p0:p0 + NB1, 1:NQ1 + 2].bitcast(F32),
                                                     ALU.add, ALU.subtract).then_inc(qfree, 1)
                        chain_pooled_dve(dve, i, ((1, 1),), pooled_s, chain)
                        if not last:
                            for c in range(NX - 3, NX):
                                prep_chunk(i + 1, c)
                        chain_taps_dve(dve, i, 1, chain, ker_s)
                        dve.wait_ge(ker_s, i + 1)
                        dyn.start(i)
                        dynamic_tiles(dve, dyn, kerr[:, 0, :], lk_mid(lk_h), lk_mid(lk_l))
                        if not last:
                            dve.wait_ge(n_l, NCH * (i + 1))
                            alone(dve)
                            prep_rest(i + 1)
                        dve.wait_ge(l_h, i + 1)
                        dve.tensor_tensor(ll[:, :], ps_lk[:, :], lh[:, :].bitcast(F32), ALU.subtract).then_inc(l_l, 1)
                        plain(i, 3)
                        if not last:
                            norm(i + 1, 0)
                            norm(i + 1, 1)
                        for p, (dr, dc) in enumerate(PIX):
                            dve.wait_ge(qful, Q * i + QY + p + 1)
                            if p == 0:
                                dve.wait_ge(qfree, 2 + Q * i + QY)
                            v = z1[:, dr::2, dc::4]
                            dve.tensor_tensor(v, v, ps_q[:, p % 2, 0:NB1 * NQ1].rearrange("p (n q) -> p n q", q=NQ1),
                                              ALU.add).then_inc(qfree, 1)
                            if p < 2 and not last:
                                norm(i + 1, 2 + p)

                    dve.memset(stage, 0.0).then_inc(a_z, 1)
                    dve.memset(fa_h[:, :, :].bitcast(F32), 0.0).then_inc(a_b, 1)
                    dve.memset(fa_l[:, :, :].bitcast(F32), 0.0).then_inc(a_b, 1)
                    dve.memset(ga_h[:, :].bitcast(F32), 0.0).then_inc(a_b, 1)
                    dve.memset(ga_l[:, :].bitcast(F32), 0.0).then_inc(a_b, 1)
                    dve.wait_ge(a_b, 4)
                    n = 0
                    for k in range(3):
                        dve.tensor_copy(fa_h[:, k, 112:128], w1a[:, k + 1, :]).then_inc(a_g, 1)
                        n += 1
                        dve.wait_ge(a_g, n)
                        dve.tensor_tensor(fa_l[:, k, 112:128], w1a[:, k + 1, :],
                                          fa_h[:, k, 112:128].bitcast(F32), ALU.subtract).then_inc(a_b, 1)
                    for m in range(8):
                        o = slice(m * P + C, m * P + P)
                        dve.tensor_scalar(gst[:, :], gar[:, :], slm[:, m:m + 1], None, ALU.mult).then_inc(a_g, 1)
                        dve.wait_ge(a_g, n + 1)
                        dve.tensor_copy(ga_h[:, o], gst[:, :]).then_inc(a_g, 1)
                        dve.wait_ge(a_g, n + 2)
                        dve.tensor_tensor(ga_l[:, o], gst[:, :], ga_h[:, o].bitcast(F32),
                                          ALU.subtract).then_inc(a_g, 1)
                        n += 3
                        dve.wait_ge(a_g, n)
                    assert n == NA_G
                    for k in range(3):
                        dve.wait_ge(a_ld, 32 * (k + 1))
                        dve.tensor_copy(w3h[:, k, :, :], stage).then_inc(a_s, 1)
                        dve.wait_ge(a_s, 2 * k + 1)
                        dve.tensor_tensor(w3l[:, k, :, :], stage, w3h[:, k, :, :].bitcast(F32),
                                          ALU.subtract).then_inc(a_s, 1)
                        for c in range(2 * k, 2 * k + 2 if k < 2 else NX):
                            prep_chunk(0, c)
                    dve.wait_ge(a_p, 7)
                    dve.wait_ge(a_s, 6)
                    prep_rest(0)
                    for k in range(NCH):
                        norm(0, k)
                    with dve.Fori(0, B - 1) as i:
                        body(i, False)
                    body(B - 1, True)

                @block.tensor
                def _(pe):
                    def plain(i, k):
                        u = k if k < 3 else QL
                        pe.wait_ge(r_l, 2 + NCH * i + k + 1)
                        pe.wait_ge(qfree, Q * i + u + 1)
                        v = (slice(None), slice(8 * k, 8 * k + 8), slice(2, 2 + S1))
                        product(pe, ps_q[:, u % 2, :].rearrange("p (r c) -> p r c", c=S1), idt_h[:, 1, :],
                                idt_l[:, 1, :], rh[v], rl[v], True, True).then_inc(qful, 1)

                    def body(i, last):
                        for k in range(NCH):
                            pe.wait_ge(n_l, NCH * i + k + 1)
                            pe.wait_ge(mfree, NCH * i + k + 1)
                            for t in range(9):
                                o0 = (8 * k + (t // 3) * D1) * plen[1] + (t % 3) * D1
                                vh, vl = (a[:, o0:o0 + 8 * plen[1]].rearrange("p (r c) -> p r c", c=plen[1])
                                          [:, :, 0:S1] for a in (nh, nl))
                                mm = product(pe, ps_main[:, k % 2, :].rearrange("p (r c) -> p r c", c=S1),
                                             w3h[:, 0, t, :], w3l[:, 0, t, :], vh, vl, t == 0, t == 8)
                            mm.then_inc(main, 1)
                        for k in range(3):
                            plain(i, k)
                        pe.wait_ge(r_l, 2 + NCH * (i + 1))
                        chain_pooled(pe, i, ((1, 1),), sums, chain)
                        pe.wait_ge(qfree, Q * i + QF + 2)
                        for j, (dr, dc) in enumerate(PIX):
                            a = 112 - ATT * slot(dr, dc)
                            for hf in range(2):
                                v = (slice(hf * C, hf * C + C), slice(dr, None, 2), slice(dc, dc + 4 * NQ1 + 5, 4))
                                w = (v[0], 0, slice(a, a + P))
                                mm = product(pe, ps_q[:, 1 - hf, 0:NB1 * (NQ1 + 2)].rearrange("p (n q) -> p n q", q=NQ1 + 2),
                                             fa_h[w], fa_l[w], rh[v], rl[v], j == 0, j == 7)
                                if j == 7:
                                    mm.then_inc(qful, 1)
                        pe.wait_ge(f_z, 4 * (i + 1))
                        pe.wait_ge(l_l, i + 1)
                        between = {4: lambda: chain_hidden(pe, i, 1, 1, pooled_s, chain),
                                   10: lambda: chain_taps(pe, i, 1, hdn_s, chain),
                                   NSTAT: lambda: dyn.at(pe, i, DSTEPS)}
                        if not last:
                            between[NSTAT + 1] = lambda: group_mean_pe(pe, stats, i + 1, avg)
                            between[NSTAT + 4] = lambda: group_var_pe(pe, stats, i + 1, avg)
                        large_filter(pe, ps_lk[:, :].rearrange("p (n q) -> p n q", q=NQ1), fh, fl, 0, N1, NQ1,
                                     between).then_inc(lk_f, 1)
                        plain(i, 3)
                        pe.wait_ge(l_l, i + 2)
                        for p, (dr, dc) in enumerate(PIX):
                            pe.wait_ge(qfree, Q * i + QY + p + 1)
                            o = ps_q[:, p % 2, 0:NB1 * NQ1]
                            for hf in range(2):
                                g = slice(slot(dr, dc) * P + C * (1 - hf), slot(dr, dc) * P + C * (1 - hf) + P)
                                m = slice(hf * NB1 * NQ1, (hf + 1) * NB1 * NQ1)
                                mm = product(pe, o, ga_h[:, g], ga_l[:, g], lh[:, m], ll[:, m], hf == 0, hf == 1)
                            mm.then_inc(qful, 1)

                    pe.wait_ge(a_s, 6)
                    pe.wait_ge(a_b, 7)
                    pe.wait_ge(a_g, NA_G)
                    pe.wait_ge(a_p, 7)
                    group_mean_pe(pe, stats, 0, avg)
                    group_var_pe(pe, stats, 0, avg)
                    with pe.Fori(0, B - 1) as i:
                        body(i, False)
                    body(B - 1, True)

        G = 2
        NG = B // G
        with ExitStack() as st:
            def s1(name):
                return sem("pb_" + name, st)

            order = (3, 2)
            NB = {lv: half[lv] // 2 for lv in order}
            NQ = {lv: SIDE[lv] // 4 for lv in order}
            NBQ = {lv: 2 * NB[lv] * NQ[lv] for lv in order}
            LEN = {lv: prow[lv] * plen[lv] + 2 * DIL[lv] for lv in order}
            pl = {lv: sb(f"pl{lv}", [P, G, prow[lv], SIDE[lv]], stack=st) for lv in order}
            nh = {lv: sb(f"nh{lv}", [P, G, LEN[lv]], F32R, stack=st) for lv in order}
            nl = {lv: sb(f"nl{lv}", [P, G, LEN[lv]], F32R, stack=st) for lv in order}
            rh = {lv: sb(f"rh{lv}", [P, G, half[lv], SIDE[lv] + 8], F32R, stack=st) for lv in order}
            rl = {lv: sb(f"rl{lv}", [P, G, half[lv], SIDE[lv] + 8], F32R, stack=st) for lv in order}
            TOP = {2: 0, 3: half[2] + 3}
            NJ = TOP[3] + half[3]
            fjh = sb("fjh", [P, G, NJ + 6, NQ[2] + 4], F32R, stack=st)
            fjl = sb("fjl", [P, G, NJ + 6, NQ[2] + 4], F32R, stack=st)
            fh = {lv: fjh[:, :, TOP[lv]:TOP[lv] + half[lv] + 6, 0:NQ[lv] + 4] for lv in order}
            fl = {lv: fjl[:, :, TOP[lv]:TOP[lv] + half[lv] + 6, 0:NQ[lv] + 4] for lv in order}
            z = {lv: sb(f"z{lv}", [P, G, half[lv], SIDE[lv]], stack=st) for lv in order}
            lh = {lv: sb(f"lh{lv}", [P, G, NBQ[lv]], F32R, stack=st) for lv in order}
            ll = {lv: sb(f"ll{lv}", [P, G, NBQ[lv]], F32R, stack=st) for lv in order}
            dt_h = sb("dt_h", [P, G, ND, P], F32R, stack=st)
            dt_l = sb("dt_l", [P, G, ND, P], F32R, stack=st)
            rf = sb("rfb", [P, 2, 512], stack=st)
            flat = stat[:, :, :].rearrange("p a b -> p (a b)")
            coefs = flat[:, 0:4 * B].rearrange("p (l k b) -> p l k b", l=2, k=2)
            cg = flat[:, 4 * B:4 * B + 4 * G].rearrange("p (l k b) -> p l k b", l=2, k=2)

            items = [(lv, j) for lv in order for j in range(G)]
            NI1 = len(items)
            convs = [(3, None, ps_stat[:, 0:G * half[3] * SIDE[3]])] + [(2, j, ps_main[:, j, :]) for j in range(G)]
            relus = [(0, slice(j * 128, j * 128 + 128)) for j in range(G)] + [(1 - j, slice(0, 512)) for j in range(G)]
            rf_used = (0, 0, 0, G)
            QF, QY = NI1, NI1 + 4
            Q = QY + 16
            ps_j = ps_edge[:, 0:G * NJ * NQ[2]].rearrange("p (g n q) -> p g n q", g=G, q=NQ[2])
            ps_lk = {lv: ps_j[:, :, TOP[lv]:TOP[lv] + half[lv], 0:NQ[lv]] for lv in order}
            made = [0, 1, NI1 - 1, G]

            cf_s = s1("cf")
            p_acc = s1("p_acc")
            zero = s1("zero")
            nzero = s1("nzero")
            cg_s = s1("cg_s")
            s3 = s1("s3")
            n_i = s1("n_i")
            halo = {lv: s1(f"halo{lv}") for lv in order}
            n_h, n_l = s1("n_h"), s1("n_l")
            main = s1("main")
            mfree = s1("mfree")
            r_h = s1("r_h")
            r_l = s1("r_l")
            qful, qfree = s1("qful"), s1("qfree")
            f_h, f_z = s1("f_h"), s1("f_z")
            pooled_s, chain, hdn_s, ker_s = s1("pooled"), s1("chain"), s1("hdn"), s1("ker")
            dyn = Steps(s1("dyn"), NI1 * DSTEPS)
            z_up = s1("z_up")
            dt_f = s1("dt_f")
            lk_f = s1("lk_f")
            l_h = s1("l_h")
            l_l = s1("l_l")
            zst = s1("zst")

            def nview(a, lv):
                d, n, m = DIL[lv], prow[lv], plen[lv]
                return a[lv][:, :, d:d + n * m].rearrange("p g (r c) -> p g r c", c=m)[:, :, :, 0:SIDE[lv]]

            def tiles_of(k):
                if k == NI1 - 1:
                    return lk_mid(lk_h), lk_mid(lk_l)
                return (t[:, k % G, :, :].rearrange("p (b c) m -> p b (c m)", b=3) for t in (dt_h, dt_l))

            with nc.Block() as block:
                @block.sync
                def _(sp):
                    sp.sem_inc(mfree, 2 * G)
                    sp.sem_inc(r_l, 2 * G)
                    sp.sem_inc(qfree, 2)
                    sp.sem_inc(l_l, 2)
                    sp.sem_inc(zst, 16)
                    sp.sem_inc(z_up, 1)

                    def halos(g):
                        for k, lv in enumerate(order):
                            sp.wait_ge(n_i, NI1 * g + G * (k + 1))
                            alone(sp)
                            d, n2 = DIL[lv], half[lv]
                            m = min(d, n2)
                            for j in range(G):
                                sp.dma_start(pl[lv][0:C, j, d + n2:d + n2 + m, :],
                                             pl[lv][C:P, j, d:d + m, :]).then_inc(halo[lv], 16)
                                sp.dma_start(pl[lv][C:P, j, d - m:d, :],
                                             pl[lv][0:C, j, d + n2 - m:d + n2, :]).then_inc(halo[lv], 16)

                    def store(g):
                        sp.wait_ge(qfree, 2 + Q * (g + 1))
                        alone(sp)
                        for j in range(G):
                            for r in range(2):
                                sp.dma_start(zs2.ap()[G * g + j, :, half[2] * r:half[2] * r + half[2], :],
                                             z[2][r * C:r * C + C, j, :, :]).then_inc(zst, 16)

                    sp.wait_ge(zero, 2)
                    halos(0)
                    with sp.Fori(0, NG - 1) as g:
                        halos(g + 1)
                        store(g)
                    store(NG - 1)
                    sp.wait_ge(zst, 16 + 32 * G * NG)

                @block.gpsimd
                def _(pool):
                    def sums3(g):
                        v = p2[:, bass.ds(G * g, G), :, :].rearrange("p g (r a) (c b) -> p g r a c b", a=2, b=2)
                        quad_sum(pool, pl[3][:, :, DIL[3]:DIL[3] + half[3], :], lambda a, b: v[:, :, :, a, :, b],
                                 p_acc, 2 * g).then_inc(s3, 1)

                    def norm(g):
                        for k, lv in enumerate(order):
                            pool.wait_ge(n_h, 2 * g + k + 1)
                            for j in range(G):
                                pool.tensor_tensor(nview(nl, lv)[:, j], pl[lv][:, j, :, :],
                                                   nview(nh, lv)[:, j].bitcast(F32), ALU.subtract).then_inc(n_l, 1)

                    def body(g, last):
                        for k, (lv, j) in enumerate(items):
                            pool.wait_ge(r_h, NI1 * g + k + 1)
                            s, (b, c) = SIDE[lv], relus[k]
                            pool.tensor_tensor(rl[lv][:, j, :, 2:2 + s],
                                               rf[:, b, c].rearrange("p (r c) -> p r c", c=s),
                                               rh[lv][:, j, :, 2:2 + s].bitcast(F32), ALU.subtract).then_inc(r_l, 1)
                        if not last:
                            pool.wait_ge(n_l, NI1 * (g + 1))
                            alone(pool)
                            sums3(g + 1)
                        pool.wait_ge(qfree, 2 + Q * g + QY)
                        alone(pool)
                        for lv in order:
                            n, q = half[lv], NQ[lv]
                            for t in (fh[lv], fl[lv]):
                                for j in range(G):
                                    pool.memset(t[0:C, j, 3:3 + n, 1:2].bitcast(F32), 0.0).then_inc(f_z, 1)
                                    pool.memset(t[C:P, j, 3:3 + n, 1 + q:2 + q].bitcast(F32), 0.0).then_inc(f_z, 1)
                        pool.wait_ge(f_z, 8 * G * (g + 1))
                        alone(pool)
                        if not last:
                            norm(g + 1)

                    for lv in order:
                        pool.memset(pl[lv][:, :, :, :], 0.0).then_inc(zero, 1)
                    pool.wait_ge(zero, 2)
                    sums3(0)
                    for t in (rh[3], rl[3], rh[2], rl[2], fjh, fjl):
                        pool.memset(t[:, :, :, :].bitcast(F32), 0.0).then_inc(zero, 1)
                    pool.wait_ge(zero, 8)
                    norm(0)
                    with pool.Fori(0, NG - 1) as g:
                        body(g, False)
                    body(NG - 1, True)

                @block.scalar
                def _(act):
                    def norm(g):
                        for k, lv in enumerate(order):
                            act.wait_ge(halo[lv], 32 * G * (g + 1))
                            for j in range(G):
                                ins = act.activation(nview(nh, lv)[:, j], pl[lv][:, j, :, :], ACT.Identity)
                            ins.then_inc(n_h, 1)

                    def body(g, last):
                        for k, (lv, j) in enumerate(items):
                            act.wait_ge(main, 3 * g + (1 if lv == 3 else 2 + j))
                            act.wait_ge(r_l, 2 * G + NI1 * g + rf_used[k])
                            b, c = relus[k]
                            src = ps_stat[:, c] if lv == 3 else ps_main[:, j, :]
                            act.activation(rf[:, b, c], src, ACT.Relu, bias=b3p[:, lv:lv + 1],
                                           accum_out=rsum[:, k:k + 1]).then_inc(mfree, 1)
                        for k, lv in enumerate(order):
                            n, q = NB[lv], NQ[lv]
                            for hf in range(2):
                                act.wait_ge(qful, Q * g + QF + 2 * k + hf + 1)
                                p0 = 3 + n * hf
                                ps = ps_q[:, hf, 0:G * n * (q + 2)].rearrange("p (g n q) -> p g n q", g=G, q=q + 2)
                                act.activation(fh[lv][:, :, p0:p0 + n, 1:q + 2], ps[:, :, :, 0:q + 1], ACT.Identity,
                                               bias=b1a[:, lv:lv + 1]).then_inc(f_h, 1)
                            if k == 0:
                                chain_act(act, g, NI1, chain, hdn_s)
                        if not last:
                            norm(g + 1)
                        act.wait_ge(lk_f, g + 1)
                        for lv in order:
                            act.activation(lh[lv][:, :, :].rearrange("p g (n q) -> p g n q", q=NQ[lv]), ps_lk[lv],
                                           ACT.Identity).then_inc(l_h, 1)

                    act.wait_ge(nzero, 4)
                    norm(0)
                    with act.Fori(0, NG - 1) as g:
                        body(g, False)
                    body(NG - 1, True)

                @block.vector
                def _(dve):
                    def norm(g):
                        dve.tensor_copy(cg[:, :, :, :].rearrange("p l k b -> p (l k) b"),
                                        coefs[:, :, :, :].rearrange("p l k b -> p (l k) b")[:, :, bass.ds(G * g, G)]
                                        ).then_inc(cg_s, 1)
                        dve.wait_ge(cg_s, g + 1)
                        dve.wait_ge(s3, g + 1)
                        for k, lv in enumerate(order):
                            for j in range(G):
                                dst = pl[lv][:, j, DIL[lv]:DIL[lv] + half[lv], :]
                                src = dst if lv == 3 else p2[:, bass.ds(G * g + j, 1), :, :].rearrange(
                                    "p g r c -> p (g r) c")
                                dve.tensor_scalar(dst, src, cg[:, k, 0, j:j + 1], cg[:, k, 1, j:j + 1], ALU.subtract,
                                                  ALU.mult).then_inc(n_i, 1)

                    def body(g, last):
                        for k, (lv, j) in enumerate(items):
                            dve.wait_ge(mfree, 2 * G + NI1 * g + k + 1)
                            s, (b, c) = SIDE[lv], relus[k]
                            dve.tensor_copy(rh[lv][:, j, :, 2:2 + s],
                                            rf[:, b, c].rearrange("p (r c) -> p r c", c=s)).then_inc(r_h, 1)
                        dve.wait_ge(zst, 16 + 32 * G * g)
                        for k, (lv, j) in enumerate(items):
                            dve.wait_ge(qful, Q * g + k + 1)
                            dve.tensor_copy(z[lv][:, j, :, :].rearrange("p a b -> p (a b)"),
                                            ps_q[:, k % 2, 0:half[lv] * SIDE[lv]]).then_inc(qfree, 1)
                        chain_pooled_dve(dve, g, ((3, G), (2, G)), pooled_s, chain)
                        for k, lv in enumerate(order):
                            n, q = NB[lv], NQ[lv]
                            for hf in range(2):
                                dve.wait_ge(f_h, 4 * g + 2 * k + hf + 1)
                                p0 = 3 + n * hf
                                ps = ps_q[:, hf, 0:G * n * (q + 2)].rearrange("p (g n q) -> p g n q", g=G, q=q + 2)
                                v = fh[lv][:, :, p0:p0 + n, 1:q + 2].bitcast(F32)
                                for j in range(G):
                                    ins = dve.scalar_tensor_tensor(fl[lv][:, j, p0:p0 + n, 1:q + 2],
                                                                   ps[:, j, :, 0:q + 1], b1a[:, lv:lv + 1],
                                                                   v[:, j], ALU.add, ALU.subtract)
                                ins.then_inc(qfree, 1)
                            if k == 0 and not last:
                                dve.wait_ge(n_l, NI1 * (g + 1))
                                norm(g + 1)
                        chain_taps_dve(dve, g, NI1, chain, ker_s)
                        dve.wait_ge(ker_s, g + 1)
                        dyn.start(g)
                        for k in made:
                            if k == G:
                                dve.wait_ge(dt_f, g + 1)
                            dynamic_tiles(dve, dyn, kerr[:, k, :], *tiles_of(k))
                            dyn.wait(dve)
                        for k, lv in enumerate(order):
                            dve.wait_ge(l_h, 2 * g + 2)
                            for j in range(G):
                                o, v = (a[lv][:, j, :].rearrange("p (n q) -> p n q", q=NQ[lv]) for a in (ll, lh))
                                ins = dve.tensor_tensor(o, ps_lk[lv][:, j], v.bitcast(F32), ALU.subtract)
                            ins.then_inc(l_l, 1)
                        for k, lv in enumerate(order):
                            n, q = NB[lv], NQ[lv]
                            for p, (dr, dc) in enumerate(PIX):
                                u = QY + 8 * k + p
                                dve.wait_ge(qful, Q * g + u + 1)
                                if p == 0:
                                    dve.wait_ge(z_up, 1 + 2 * G * (g + k))
                                src = ps_q[:, p % 2, 0:G * n * q].rearrange("p (g n q) -> p g n q", g=G, q=q)
                                for j in range(G):
                                    v = z[lv][:, j, dr::2, dc::4]
                                    ins = dve.tensor_tensor(v, v, src[:, j], ALU.add)
                                ins.then_inc(qfree, 1)
                            dve.wait_ge(qfree, 2 + Q * g + QY + 8 * (k + 1))
                            if lv == 3:
                                for r in range(2):
                                    for j in range(G):
                                        v = z[2][:, j, r::2, :].rearrange("p a (b c) -> p a b c", c=2)
                                        zz = z[3][:, j, :, :].unsqueeze(3).to_broadcast([P, half[3], SIDE[3], 2])
                                        dve.tensor_tensor(v, v, zz, ALU.add).then_inc(z_up, 1)

                    for k, lv in enumerate(order):
                        k2 = float((H // SIDE[lv]) ** 2)
                        dve.tensor_scalar(coefs[:, k, 0, :], gn0[:, :, 0], k2, None, ALU.mult).then_inc(cf_s, 1)
                        dve.tensor_scalar(coefs[:, k, 1, :], gn0[:, :, 1], 1.0 / k2, None, ALU.mult).then_inc(cf_s, 1)
                    for lv in order:
                        for t in (nh[lv], nl[lv]):
                            dve.memset(t[:, :, :].bitcast(F32), 0.0).then_inc(nzero, 1)
                    dve.wait_ge(cf_s, 4)
                    norm(0)
                    with dve.Fori(0, NG - 1) as g:
                        body(g, False)
                    body(NG - 1, True)

                @block.tensor
                def _(pe):
                    def large(g):
                        pe.wait_ge(l_l, 2 * g + 2)
                        still = [(pb, cb) for pb in range(NPB) for cb in range(NCB) if (pb, cb) not in DYN]
                        for m, (pb, cb) in enumerate(still):
                            v = (slice(None), slice(None), slice(pb, pb + NJ), slice(cb, cb + NQ[2]))
                            product(pe, ps_j, lk_h[:, pb, cb, :], lk_l[:, pb, cb, :], fjh[v], fjl[v], m == 0, False)
                        for at, k in enumerate(made):
                            lv, j = items[k]
                            n, q = half[lv], NQ[lv]
                            dyn.at(pe, g, DSTEPS * (at + 1))
                            for m, (pb, cb) in enumerate(DYN):
                                v = (slice(None), j, slice(pb, pb + n), slice(cb, cb + q))
                                if k == NI1 - 1:
                                    wh, wl = lk_h[:, pb, cb, :], lk_l[:, pb, cb, :]
                                else:
                                    wh, wl = dt_h[:, k % G, m, :], dt_l[:, k % G, m, :]
                                mm = product(pe, ps_lk[lv][:, j], wh, wl, fh[lv][v], fl[lv][v], False, m == ND - 1)
                            if k == 0:
                                mm.then_inc(dt_f, 1)
                        mm.then_inc(lk_f, 1)

                    def body(g, last):
                        for k, (lv, j, o) in enumerate(convs):
                            s, d, n = SIDE[lv], DIL[lv], half[lv]
                            pe.wait_ge(n_l, NI1 * g + (G if lv == 3 else NI1))
                            pe.wait_ge(mfree, NI1 * g + (G if lv == 3 else G + 1 + j))
                            o = o.rearrange("p (g r c) -> p g r c", g=G, c=s) if lv == 3 else \
                                o.rearrange("p (r c) -> p r c", c=s)
                            sel = slice(None) if lv == 3 else j
                            for t in range(9):
                                o0 = (t // 3) * d * plen[lv] + (t % 3) * d
                                vh, vl = (a[lv][:, :, o0:o0 + n * plen[lv]].rearrange(
                                    "p g (r c) -> p g r c", c=plen[lv])[:, sel, :, 0:s] for a in (nh, nl))
                                mm = product(pe, o, w3h[:, lv - 1, t, :], w3l[:, lv - 1, t, :], vh, vl, t == 0, t == 8)
                            mm.then_inc(main, 1)
                        for k, (lv, j) in enumerate(items):
                            pe.wait_ge(r_l, 2 * G + NI1 * g + k + 1)
                            pe.wait_ge(qfree, Q * g + k + 1)
                            v = (slice(None), j, slice(None), slice(2, 2 + SIDE[lv]))
                            o = ps_q[:, k % 2, 0:half[lv] * SIDE[lv]].rearrange("p (r c) -> p r c", c=SIDE[lv])
                            product(pe, o, idt_h[:, lv, :], idt_l[:, lv, :], rh[lv][v], rl[lv][v], True,
                                    True).then_inc(qful, 1)
                        pe.wait_ge(mfree, 2 * G + NI1 * (g + 1))
                        chain_pooled(pe, g, ((3, G), (2, G)), None, chain)
                        for k, lv in enumerate(order):
                            pe.wait_ge(qfree, Q * g + QF + 2 * k + 2)
                            n, q = NB[lv], NQ[lv] + 2
                            for m, (dr, dc) in enumerate(PIX):
                                a = 112 - ATT * slot(dr, dc)
                                for hf in range(2):
                                    v = (slice(hf * C, hf * C + C), slice(None), slice(dr, None, 2),
                                         slice(dc, dc + 4 * q - 3, 4))
                                    w = (v[0], lv - 1, slice(a, a + P))
                                    mm = product(pe, ps_q[:, hf, 0:G * n * q].rearrange("p (g n q) -> p g n q", g=G, q=q),
                                                 fa_h[w], fa_l[w], rh[lv][v], rl[lv][v], m == 0, m == 7)
                                    if m == 7:
                                        mm.then_inc(qful, 1)
                                if k == 0 and m == 3:
                                    chain_hidden(pe, g, NI1, 2, pooled_s, chain)
                            if k == 0:
                                chain_taps(pe, g, NI1, hdn_s, chain)
                        pe.wait_ge(f_z, 8 * G * (g + 1))
                        large(g)
                        for k, lv in enumerate(order):
                            pe.wait_ge(l_l, 2 + 2 * g + k + 1)
                            n, q = NB[lv], NQ[lv]
                            for p, (dr, dc) in enumerate(PIX):
                                pe.wait_ge(qfree, Q * g + QY + 8 * k + p + 1)
                                o = ps_q[:, p % 2, 0:G * n * q]
                                for hf in range(2):
                                    w = slice(slot(dr, dc) * P + C * (1 - hf), slot(dr, dc) * P + C * (1 - hf) + P)
                                    m = (slice(None), slice(None), slice(hf * n * q, (hf + 1) * n * q))
                                    mm = product(pe, o.rearrange("p (g n) -> p g n", g=G), ga_h[:, w], ga_l[:, w],
                                                 lh[lv][m], ll[lv][m], hf == 0, hf == 1)
                                mm.then_inc(qful, 1)

                    with pe.Fori(0, NG - 1) as g:
                        body(g, False)
                    body(NG - 1, True)
        st1.close()

        NW = NPAIR // 4
        with ExitStack() as st:
            def s2(name):
                return sem("p2_" + name, st)

            t3_h = sb("t3_h", [P, 2, 3, P], F32R, stack=st)
            t3_l = sb("t3_l", [P, 2, 3, P], F32R, stack=st)
            fa_h = sb("fa0_h", [P, 4, P], F32R, stack=st)
            fa_l = sb("fa0_l", [P, 4, P], F32R, stack=st)
            ga_h = sb("ga0_h", [P, 4, P], F32R, stack=st)
            ga_l = sb("ga0_l", [P, 4, P], F32R, stack=st)
            zeros = sb("zeros0", [P, 2, W], stack=st)

            x1 = sb("x1", [P, NPAIR + 2, W], stack=st)
            fh = sb("fh0", [P, NPAIR + 6, 36], F32R, stack=st)
            fl = sb("fl0", [P, NPAIR + 6, 36], F32R, stack=st)
            xh = sb("xh", [P, 2, 5, W + 2], F32R, stack=st)
            xl = sb("xl", [P, 2, 5, W + 2], F32R, stack=st)
            rh = sb("rh0", [P, 8, W + 8], F32R, stack=st)
            rl = sb("rl0", [P, 8, W + 8], F32R, stack=st)
            yh = sb("yh", [P, 2, 6, W + 4], F32R, stack=st)
            yl = sb("yl", [P, 2, 6, W + 4], F32R, stack=st)
            rowf = sb("rowf", [P, W + 4], stack=st)
            colf = sb("colf", [P, 2, NPAIR + 2], stack=st)
            xp = x.rearrange("b c (p r) w -> b c p r w", r=2)
            op = out.rearrange("b c (p r) w -> b c p r w", r=2)

            with ExitStack() as se:
                b_p = sem("b_p", se)
                b_z = sem("b_z", se)
                b_ld = sem("b_ld", se)
                b_x = sem("b_x", se)
                steps = Steps(sem("b_s", se), 200)
                s3 = sb("s3", [P, 4, 3, C], stack=se)
                tile_f = sb("tile_f", [P, 2, 4, P], stack=se)
                with nc.Block() as block:
                    @block.gpsimd
                    def _(pool):
                        for t in (fh, fl):
                            pool.memset(t[:, :, :].bitcast(F32), 0.0).then_inc(b_p, 1)
                        for t in (rh, rl):
                            pool.memset(t[:, :, :].bitcast(F32), 0.0).then_inc(b_p, 1)
                        for t in (xh, xl, yh, yl):
                            pool.memset(t[:, :, :, :].bitcast(F32), 0.0).then_inc(b_p, 1)
                        pool.memset(zeros[:, :, :], 0.0).then_inc(b_p, 1)
                        pool.memset(rowf[:, :], 0.0).then_inc(b_p, 1)

                    @block.sync
                    def _(sp):
                        with nc.allow_non_contiguous_dma(reason="small weight layouts"):
                            sp.wait_ge(b_z, 1)
                            for r in range(2):
                                hp = slice(r * C, r * C + C)
                                w0 = w3t[0].rearrange("c (y x) o -> c y x o", x=3)
                                sp.dma_start(s3[hp, 1 - r:4 - r, :, :], w0).then_inc(b_ld, 16)
                            for r in range(2):
                                sp.dma_start(x1[par(r), 1:NPAIR + 1, :], xp[0, :, :, r, :]).then_inc(b_x, 16)
                            sp.wait_ge(b_x, 16 * 2)

                    @block.vector
                    def _(dve):
                        steps.start(0)

                        def step(ins):
                            steps.done(ins)
                            steps.wait(dve)

                        def split(hi, lo, src):
                            step(dve.tensor_copy(hi, src))
                            step(dve.tensor_tensor(lo, src, hi.bitcast(F32), ALU.subtract))

                        dve.memset(s3[:, :, :, :], 0.0).then_inc(b_z, 1)
                        step(dve.memset(tile_f[:, :, :, :], 0.0))
                        for dr, dc in PIX:
                            hp, q = par(dr), slot(dr, dc) * ATT
                            step(dve.tensor_copy(tile_f[hp, 0, dc, q:q + ATT], w1a[hp, 0, :]))
                        split(fa_h[:, :, :], fa_l[:, :, :], tile_f[:, 0, 0:4, :])
                        for dr, dc in PIX:
                            s = slot(dr, dc)
                            step(dve.tensor_scalar(tile_f[:, 0, dc, par(dr)], gar[:, :], slm[:, s:s + 1],
                                                   None, ALU.mult))
                        split(ga_h[:, :, :], ga_l[:, :, :], tile_f[:, 0, 0:4, :])
                        dve.wait_ge(b_ld, 16 * 2)
                        for blk in range(2):
                            for m in range(2):
                                step(dve.tensor_copy(tile_f[:, blk, 0:3, par(m)], s3[:, 2 * blk - m + 1, :, :]))
                        split(t3_h[:, :, :, :], t3_l[:, :, :, :], tile_f[:, 0:2, 0:3, :])

            zall = sb("zall", [P, NPAIR, W // 2], stack=st)
            z23 = sb("z23", [P, H // 4, W // 4], stack=st)
            xnf = sb("xnf", [P, 5, W], stack=st)
            rf = sb("rf0", [P, 512], stack=st)
            lh = sb("lh0", [P, 2, 512], F32R, stack=st)
            ll = sb("ll0", [P, 2, 512], F32R, stack=st)
            xn1 = sb("xn1", [P, 6, W], stack=st)
            ot = sb("ot", [P, 2, 4, W], stack=st)
            edge = sb("edge", [P, 256], stack=st)
            m0 = sb("m0", [P, 2], stack=st)
            m1 = sb("m1", [P, 2], stack=st)
            rs = sb("rs0", [P, NW], stack=st)

            MAIN, Q = 36, 40
            QY = 3 * NW // 2
            ps_pw = (ps_q[:, 0, :], ps_q[:, 1, :], ps_more)
            MB, MC = NW, NW + 4
            assert MAIN == MC + NW and Q == QY + 16
            m_cp, e_in = s2("m_cp"), s2("e_in")
            m_row = s2("m_row")
            x_full = s2("x_full")
            z_done = s2("z_done")
            z_full = s2("z_full")
            NLOAD = 8
            x_n, x_h, x_l = s2("x_n"), s2("x_h"), s2("x_l")
            main, mfree, qful, qfree = s2("main"), s2("mfree"), s2("qful"), s2("qfree")
            r_h, r_l, x_z, f_h, f_z = s2("r_h"), s2("r_l"), s2("x_z"), s2("f_h"), s2("f_z")
            sums = Steps(s2("sums"), 1)
            pooled_s, chain, hdn_s, ker_s = s2("pooled"), s2("chain"), s2("hdn"), s2("ker")
            dyn = Steps(s2("dyn"), DSTEPS)
            l_h, bn = s2("l_h"), s2("bn")
            stats = Steps(s2("stats"), GSTEPS + 3)
            avg, root = s2("avg"), s2("root")
            y_n, y_h, y_l = s2("y_n"), s2("y_h"), s2("y_l")
            e_mm, e_out = s2("e_mm"), s2("e_out")
            o_row, o_done = s2("o_row"), s2("o_done")
            stored = [s2("stored0"), s2("stored1")]

            def windows(eng, first, body, before={}):
                for w in range(first, 2):
                    body(w, w % 2, w // 2)
                with eng.Fori(1, NW // 2 - 1) as t:
                    for h in range(2):
                        body(2 * t + h, h, t)
                for w in range(NW - 2, NW):
                    if w in before:
                        before[w]()
                    body(w, w % 2, w // 2)

            def is_last(w, k):
                return isinstance(w, int) and w + k >= NW

            def is_first(w, k):
                return isinstance(w, int) and w < k

            with nc.Block() as block:
                @block.sync
                def _(sp):
                    sp.sem_inc(mfree, 2)
                    sp.sem_inc(qfree, 3)
                    for sm in (x_n, x_l, r_l, y_l):
                        sp.sem_inc(sm, 1)
                    for sm in (x_full, *stored):
                        sp.sem_inc(sm, 16)

                    def load_z(i):
                        for r in range(2):
                            sp.dma_start(zall[par(r), :, :], zs.ap()[i]).then_inc(z_full, 16)
                            sp.dma_start(z23[par(r), :, :], zs2.ap()[i]).then_inc(z_full, 16)

                    def load(i):
                        sp.wait_ge(x_z, NW * (i + 1))
                        alone(sp)
                        load_z(i + 1)
                        n = NPAIR // NLOAD
                        with sp.Fori(0, NLOAD) as u:
                            sp.wait_ge(o_done, NW * i + 2 * u + 2)
                            alone(sp)
                            sp.wait_ge(x_full, 16 + 32 * (NLOAD * i + u))
                            alone(sp)
                            for r in range(2):
                                sp.dma_start(x1[par(r), bass.ds(n * u + 1, n), :],
                                             xp[i + 1, :, bass.ds(n * u, n), r, :]).then_inc(x_full, 16)

                    load_z(0)
                    with sp.Fori(0, B - 1) as i:
                        load(i)

                @block.gpsimd
                def _(pool):
                    def stage_a(i, w, h, t):
                        pool.wait_ge(x_n, NW * i + w + (2 if is_last(w, 1) else 3))
                        v = x1[:, bass.ds(4 * w + 1, 4), :].rearrange("p a (b c) -> p (a b) c", c=2)
                        zz = zall[:, bass.ds(4 * w, 4), :].rearrange("p a b -> p (a b)").unsqueeze(2)
                        alone(pool)
                        pool.tensor_tensor(v, v, zz.to_broadcast([P, 256, 2]), ALU.add).then_inc(x_z, 1)
                        pool.wait_ge(r_h, NW * i + w + 1)
                        pool.tensor_tensor(rl[:, 4 * h:4 * h + 4, 2:2 + W], rf[:, :].rearrange("p (a b) -> p a b", b=W),
                                           rh[:, 4 * h:4 * h + 4, 2:2 + W].bitcast(F32),
                                           ALU.subtract).then_inc(r_l, 1)

                    def outside(i, part):
                        pool.wait_ge(r_l, NW * i + NW + part)
                        alone(pool)
                        pool.wait_ge(qfree, 3 + Q * i + (12 if part == 0 else QY))
                        alone(pool)
                        r = slice(3, 35) if part == 0 else slice(35, 3 + NPAIR)
                        for t in (fh, fl):
                            pool.memset(t[0:C, r, 1:2].bitcast(F32), 0.0).then_inc(f_z, 1)
                            pool.memset(t[C:P, r, 33:34].bitcast(F32), 0.0).then_inc(f_z, 1)
                        pool.wait_ge(f_z, 8 * i + 4 * (part + 1))
                        alone(pool)

                    def y_low(i, v, h):
                        pool.wait_ge(y_h, NW * i + v + 1)
                        pool.tensor_tensor(yl[:, h, :, 2:2 + W], xn1[:, :, :], yh[:, h, :, 2:2 + W].bitcast(F32),
                                           ALU.subtract).then_inc(y_l, 1)

                    def z_sum(i):
                        pool.wait_ge(z_full, 64 * (i + 1))
                        zz = z23[:, :, :].unsqueeze(3).to_broadcast([P, H // 4, W // 4, 2])
                        for r in range(2):
                            v = zall[:, r::2, :].rearrange("p a (b c) -> p a b c", c=2)
                            alone(pool)
                            pool.tensor_tensor(v, v, zz, ALU.add).then_inc(z_done, 1)

                    def body(i, last):
                        pool.wait_ge(z_done, 2 * (i + 1))
                        alone(pool)
                        windows(pool, 0, lambda w, h, t: stage_a(i, w, h, t), {NW - 1: lambda: outside(i, 0)})
                        outside(i, 1)
                        if not last:
                            z_sum(i + 1)
                        windows(pool, 0, lambda v, h, t: y_low(i, v, h))

                    z_sum(0)
                    with pool.Fori(0, B - 1) as i:
                        body(i, False)
                    body(B - 1, True)

                @block.scalar
                def _(act):
                    def x_high(i, w, h):
                        act.wait_ge(x_n, NW * i + w + 2)
                        if not is_first(w, 2):
                            act.wait_ge(main, MAIN * i + w - 1)
                        act.activation(xh[:, h, :, 1:1 + W], xnf[:, :, :], ACT.Identity).then_inc(x_h, 1)

                    def f_high(i, t):
                        act.wait_ge(qful, Q * i + 3 * t + 1)
                        ps = ps_pw[0][:, 0:272].rearrange("p (n q) -> p n q", q=34)
                        act.activation(fh[:, bass.ds(8 * t + 3, 8), 1:34], ps[:, :, 0:33], ACT.Identity,
                                       bias=b1a[:, 0:1]).then_inc(f_h, 1)

                    def stage_a(i, w, h, t):
                        act.wait_ge(main, MAIN * i + w + 1)
                        act.wait_ge(r_l, NW * i + w + 1)
                        act.activation(rf[:, :], ps_main[:, h, :], ACT.Relu, bias=b3p[:, 0:1],
                                       accum_out=rs[:, bass.ds(w, 1)]).then_inc(mfree, 1)
                        if not is_last(w, 2):
                            x_high(i, w + 2, h)
                        if h == 0 and not is_first(w, 1):
                            f_high(i, t - 1)

                    def y_high(i, v, h):
                        act.wait_ge(y_n, NW * i + v + 1)
                        if not is_first(v, 2):
                            act.wait_ge(main, MAIN * i + MC + v - 1)
                        act.activation(yh[:, h, :, 2:2 + W], xn1[:, :, :], ACT.Identity).then_inc(y_h, 1)

                    def store(i, v, h):
                        act.wait_ge(o_done, NW * i + v + 1)
                        for r in range(2):
                            act.dma_start(op[i, :, bass.ds(4 * v, 4), r, :],
                                          ot[par(r), h, :, :]).then_inc(stored[h], 16)

                    def stage_c(i, v, h):
                        if not is_last(v, 2):
                            y_high(i, v + 2, h)
                        store(i, v, h)

                    def body(i, last):
                        windows(act, 0, lambda w, h, t: stage_a(i, w, h, t))
                        chain_act(act, i, 1, chain, hdn_s)
                        f_high(i, NW // 2 - 1)
                        for c in range(4):
                            act.wait_ge(main, MAIN * i + MB + c + 1)
                            if c >= 2:
                                act.wait_ge(qful, Q * i + QY + 4 * (c - 1))
                            act.activation(lh[:, c % 2, :], ps_main[:, c % 2, :], ACT.Identity).then_inc(l_h, 1)
                        group_stats_act(act, stats, i, root)
                        for v in range(2):
                            y_high(i, v, v)
                        windows(act, 0, lambda v, h, t: stage_c(i, v, h), {} if last else {
                            NW - 2: lambda: x_high(i + 1, 0, 0), NW - 1: lambda: x_high(i + 1, 1, 1)})

                    x_high(0, 0, 0)
                    x_high(0, 1, 1)
                    with act.Fori(0, B - 1) as i:
                        body(i, False)
                    body(B - 1, True)
                    for h in range(2):
                        act.wait_ge(stored[h], 16 + 32 * B * NW // 2)

                @block.vector
                def _(dve):
                    def x_norm(i, w):
                        if is_first(w, 2):
                            dve.wait_ge(m_row, i + 1)
                        dve.wait_ge(x_l, NW * i + w + 1)
                        for hp, k in ((par(1), 0), (par(0), 1)):
                            ins = dve.tensor_scalar(xnf[hp, :, :], x1[hp, bass.ds(4 * w + k, 5), :], m0[hp, 0:1],
                                                    m0[hp, 1:2], ALU.subtract, ALU.mult)
                        ins.then_inc(x_n, 1)

                    def x_low(i, w, h):
                        dve.wait_ge(x_h, NW * i + w + 1)
                        dve.tensor_tensor(xl[:, h, :, 1:1 + W], xnf[:, :, :], xh[:, h, :, 1:1 + W].bitcast(F32),
                                          ALU.subtract).then_inc(x_l, 1)

                    def next_image(i):
                        dve.tensor_copy(m0[:, :], gn0[:, bass.ds(i, 1), :].rearrange("p a b -> p (a b)")).then_inc(m_cp, 1)
                        dve.wait_ge(m_cp, i + 1)
                        dve.tensor_scalar(x1[:, 0:NPAIR + 2:NPAIR + 1, :], zeros[:, :, :], m0[:, 0:1], None,
                                          ALU.add).then_inc(m_row, 1)

                    def first_norm(i):
                        next_image(i)
                        x_norm(i, 0)

                    def second_norm(i):
                        x_low(i, 0, 0)
                        x_norm(i, 1)

                    def a_out(i, t):
                        dve.wait_ge(f_h, NW // 2 * i + t + 1)
                        ps = ps_pw[0][:, 0:272].rearrange("p (n q) -> p n q", q=34)
                        dve.scalar_tensor_tensor(fl[:, bass.ds(8 * t + 3, 8), 1:34], ps[:, :, 0:33], b1a[:, 0:1],
                                                 fh[:, bass.ds(8 * t + 3, 8), 1:34].bitcast(F32), ALU.add,
                                                 ALU.subtract).then_inc(qfree, 1)
                        for h in range(2):
                            dve.wait_ge(qful, Q * i + 3 * t + h + 2)
                            dve.wait_ge(x_z, NW * i + 2 * t + h + 1)
                            v = x1[:, bass.ds(8 * t + 4 * h + 1, 4), :].rearrange("p a b -> p (a b)")
                            dve.scalar_tensor_tensor(v, ps_pw[1 + h][:, :], bz[:, 0:1], v, ALU.add,
                                                     ALU.add).then_inc(qfree, 1)

                    def stage_a(i, w, h, t):
                        if not is_last(w, 1):
                            x_low(i, w + 1, 1 - h)
                        if is_first(w, 1):
                            dve.wait_ge(x_full, 16 + 32 * NLOAD * i)
                        if not is_last(w, 2):
                            x_norm(i, w + 2)
                        dve.wait_ge(mfree, 2 + MAIN * i + w + 1)
                        if h == 0 and not is_first(w, 1):
                            dve.wait_ge(qful, Q * i + 3 * t)
                        dve.tensor_copy(rh[:, 4 * h:4 * h + 4, 2:2 + W],
                                        rf[:, :].rearrange("p (a b) -> p a b", b=W)).then_inc(r_h, 1)
                        if h == 0 and not is_first(w, 1):
                            a_out(i, t - 1)

                    def low_lk(i, c):
                        dve.wait_ge(l_h, 4 * i + c + 1)
                        dve.tensor_tensor(ll[:, c % 2, :], ps_main[:, c % 2, :], lh[:, c % 2, :].bitcast(F32),
                                          ALU.subtract).then_inc(mfree, 1)

                    def add_attention(i, c):
                        for dc in range(4):
                            dve.wait_ge(qful, Q * i + QY + 4 * c + dc + 1)
                            v = x1[:, 1 + 16 * c:17 + 16 * c, dc::4]
                            dve.tensor_tensor(v, v, ps_q[:, dc % 2, :].rearrange("p (n q) -> p n q", q=32),
                                              ALU.add).then_inc(qfree, 1)
                            dve.wait_ge(qfree, 3 + Q * i + QY + 4 * c + dc + 1)
                            dve.bn_stats(stat[:, 4 * c + dc, :], v).then_inc(bn, 1)

                    def y_norm(i, v):
                        dve.wait_ge(y_l, NW * i + v + 1)
                        dve.tensor_scalar(xn1[:, :, :], x1[:, bass.ds(4 * v, 6), :], m1[:, 0:1], m1[:, 1:2],
                                          ALU.subtract, ALU.mult).then_inc(y_n, 1)

                    def stage_c(i, v, h):
                        dve.wait_ge(main, MAIN * i + MC + v + 1)
                        dve.wait_ge(stored[h], 16 + 32 * (8 * i + v // 2))
                        o = ot[:, h, :, :]
                        dve.scalar_tensor_tensor(o.rearrange("p a b -> p (a b)"), ps_main[:, h, :], out_b[:, 0:1],
                                                 x1[:, bass.ds(4 * v + 1, 4), :].rearrange("p a b -> p (a b)"),
                                                 ALU.add, ALU.add).then_inc(mfree, 1)
                        dve.wait_ge(mfree, 2 + MAIN * i + MC + v + 1)
                        for first, r, pair in ((True, 0, 0), (False, 1, 3)):
                            if (is_first(v, 1) if first else is_last(v, 1)):
                                hp = par(r)
                                dve.tensor_tensor(o[hp, pair, :], o[hp, pair, :], edge[hp, 0:W],
                                                  ALU.subtract).then_inc(o_row, 1)
                                dve.wait_ge(o_row, 2 * i + r + 1)
                        e = edge[:, W:].rearrange("p (s n) -> p n s", s=2)[:, bass.ds(4 * v, 4), :]
                        dve.tensor_tensor(o[:, :, 0:W:W - 1], o[:, :, 0:W:W - 1], e, ALU.subtract).then_inc(o_done, 1)
                        if not is_last(v, 2):
                            y_norm(i, v + 2)

                    def body(i, last):
                        windows(dve, 0, lambda w, h, t: stage_a(i, w, h, t))
                        sums.start(i)
                        sums.done(dve.tensor_reduce(rsum[:, 0:1], rs[:, :], AX.X, ALU.add))
                        chain_pooled_dve(dve, i, ((0, 1),), pooled_s, chain)
                        a_out(i, NW // 2 - 1)
                        chain_taps_dve(dve, i, 1, chain, ker_s)
                        dve.wait_ge(ker_s, i + 1)
                        dyn.start(i)
                        dynamic_tiles(dve, dyn, kerr[:, 0, :], lk_mid(lk_h), lk_mid(lk_l))
                        dve.wait_ge(qfree, 3 + Q * i + QY)
                        for c in range(4):
                            low_lk(i, c)
                            add_attention(i, c)
                        dve.wait_ge(bn, 16 * (i + 1))
                        alone(dve)
                        stats.start(i)
                        group_stats_dve(dve, stats, lambda v: dve.wait_ge(avg, v), lambda v: dve.wait_ge(root, v),
                                        i, stat[:, :, :].rearrange("p a b -> p (a b)"), m1[:, 0:1], m1[:, 1:2])
                        stats.done(dve.tensor_scalar(x1[:, 0:NPAIR + 2:NPAIR + 1, :], zeros[:, :, :], m1[:, 0:1],
                                                     None, ALU.add))
                        stats.wait(dve)
                        y_norm(i, 0)
                        y_norm(i, 1)
                        stats.done(dve.tensor_scalar(colf[:, :, :].rearrange("p s n -> p n s"),
                                                     x1[:, :, 0:W:W - 1], m1[:, 0:1], m1[:, 1:2], ALU.subtract, ALU.mult))
                        for r, pair in ((0, 1), (1, NPAIR)):
                            hp = par(r)
                            ins = dve.tensor_scalar(rowf[hp, 2:2 + W], x1[hp, pair, :], m1[hp, 0:1], m1[hp, 1:2],
                                                    ALU.subtract, ALU.mult)
                            if r == 0:
                                ins.then_inc(e_in, 1)
                            else:
                                stats.done(ins)
                        dve.wait_ge(e_mm, i + 1)
                        dve.tensor_tensor(edge[:, :], ps_edge[:, 0:256], edge_b[:, :], ALU.add).then_inc(e_out, 1)
                        dve.wait_ge(e_out, i + 1)

                        def ahead():
                            dve.wait_ge(x_full, 16 + 32 * (NLOAD * i + 2))
                            first_norm(i + 1)

                        windows(dve, 0, lambda v, h, t: stage_c(i, v, h), {} if last else {
                            NW - 2: ahead, NW - 1: lambda: second_norm(i + 1)})

                    first_norm(0)
                    second_norm(0)
                    with dve.Fori(0, B - 1) as i:
                        body(i, False)
                    body(B - 1, True)

                @block.tensor
                def _(pe):
                    def conv3(i, w, h):
                        pe.wait_ge(x_l, NW * i + w + 2)
                        pe.wait_ge(mfree, MAIN * i + w + 1)
                        o = ps_main[:, h, :].rearrange("p (a b) -> p a b", b=W)
                        for blk in range(2):
                            for kx in range(3):
                                v = (slice(None), h, slice(blk, blk + 4), slice(kx, kx + W))
                                mm = product(pe, o, t3_h[:, blk, kx, :], t3_l[:, blk, kx, :], xh[v], xl[v],
                                             blk + kx == 0, blk + kx == 3)
                        mm.then_inc(main, 1)

                    def pointwise(i, t):
                        pe.wait_ge(r_l, NW * i + 2 * t + 3)
                        pe.wait_ge(qfree, Q * i + 3 * t + 1)
                        for dc in range(4):
                            v = (slice(None), slice(None), slice(dc, dc + 133, 4))
                            mm = product(pe, ps_pw[0][:, 0:272].rearrange("p (n q) -> p n q", q=34), fa_h[:, dc, :],
                                         fa_l[:, dc, :], rh[v], rl[v], dc == 0, dc == 3)
                        mm.then_inc(qful, 1)
                        for h in range(2):
                            pe.wait_ge(qfree, Q * i + 3 * t + 2 + h)
                            v = (slice(None), slice(4 * h, 4 * h + 4), slice(2, 2 + W))
                            product(pe, ps_pw[1 + h][:, :].rearrange("p (a b) -> p a b", b=W), idt_h[:, 0, :],
                                    idt_l[:, 0, :], rh[v], rl[v], True, True).then_inc(qful, 1)

                    def stage_a(i, w, h, t):
                        conv3(i, w, h)
                        if h == 0:
                            pointwise(i, t - 1)

                    def attention(i, c, dcs=range(4)):
                        pe.wait_ge(mfree, 2 + MAIN * i + MB + c + 1)
                        for dc in dcs:
                            pe.wait_ge(qfree, Q * i + QY + 4 * c + dc + 2)
                            product(pe, ps_q[:, dc % 2, :], ga_h[:, dc, :], ga_l[:, dc, :], lh[:, c % 2, :],
                                    ll[:, c % 2, :], True, True).then_inc(qful, 1)

                    def conv5(i, v, h):
                        pe.wait_ge(y_l, NW * i + v + 2)
                        pe.wait_ge(mfree, MAIN * i + MC + v + 1)
                        o = ps_main[:, h, :].rearrange("p (a b) -> p a b", b=W)
                        for blk in range(3):
                            for kx in range(5):
                                a = (slice(None), h, slice(blk, blk + 4), slice(kx, kx + W))
                                mm = product(pe, o, c5_h[:, blk, kx, :], c5_l[:, blk, kx, :], yh[a], yl[a],
                                             blk + kx == 0, blk + kx == 6)
                        mm.then_inc(main, 1)

                    def border(i):
                        stats.at(pe, i, stats.per)
                        pe.wait_ge(e_in, i + 1)
                        alone(pe)
                        for kx in range(5):
                            for r in range(2):
                                hp = slice(r * C, r * C + C)
                                pe.matmul(ps_edge[hp, 0:W], row_w[hp, kx, :], rowf[hp, kx:kx + W], start=(kx == 0),
                                          stop=(kx == 4), skip_group_check=True)
                        for side in range(2):
                            c0 = W + side * NPAIR
                            for blk in range(3):
                                pe.matmul(ps_edge[:, c0:c0 + NPAIR], col_w[:, side, blk, :],
                                          colf[:, side, blk:blk + NPAIR], start=False, stop=False,
                                          skip_group_check=True)
                            for r, pair in ((0, 0), (1, NPAIR - 1)):
                                hp = par(r)
                                mm = pe.matmul(ps_edge[hp, c0 + pair:c0 + pair + 1], cor_w[hp, side, :],
                                               colf[hp, side, pair + 1:pair + 2], start=False, stop=True,
                                               skip_group_check=True)
                        mm.then_inc(e_mm, 1)

                    def layer1(i, v, h):
                        conv5(i, v, h)
                        if is_first(v, 1):
                            border(i)

                    def body(i, last):
                        windows(pe, 1, lambda w, h, t: stage_a(i, w, h, t))
                        pe.wait_ge(f_z, 8 * i + 4)
                        for c in range(4):
                            if c == 0:
                                between = {3: lambda: chain_pooled(pe, i, ((0, 1),), sums, chain),
                                           6: lambda: chain_hidden(pe, i, 1, 1, pooled_s, chain),
                                           8: lambda: pointwise(i, NW // 2 - 1),
                                           12: lambda: chain_taps(pe, i, 1, hdn_s, chain),
                                           NSTAT: lambda: dyn.at(pe, i, DSTEPS)}
                            else:
                                between = {4 + 6 * dc: lambda c=c, dc=dc: attention(i, c - 1, (dc,))
                                           for dc in range(4)}
                            pe.wait_ge(mfree, MAIN * i + MB + c + 1)
                            large_filter(pe, ps_main[:, c % 2, :].rearrange("p (n q) -> p n q", q=32), fh, fl,
                                         16 * c, 16, 32, between).then_inc(main, 1)
                            if c == 0:
                                pe.wait_ge(f_z, 8 * (i + 1))
                        attention(i, 3)
                        group_mean_pe(pe, stats, i, avg)
                        group_var_pe(pe, stats, i, avg)
                        windows(pe, 0, lambda v, h, t: layer1(i, v, h))
                        if not last:
                            conv3(i + 1, 0, 0)

                    conv3(0, 0, 0)
                    with pe.Fori(0, B - 1) as i:
                        body(i, False)
                    body(B - 1, True)


def constants():
    tapmask = np.zeros((P, ND * 8, 9), np.float32)
    chmask = np.zeros((P, ATT), np.float32)
    slotmask = np.zeros((P, 8), np.float32)
    for dr, dc in PIX:
        s = slot(dr, dc)
        slotmask[s * ATT:s * ATT + ATT, s] = 1.0
        chmask[s * ATT:s * ATT + ATT] = np.eye(ATT)
        for t, (pb, cb) in enumerate(DYN):
            for er, ec in PIX:
                ky, kx = 2 * pb + dr - er - LK // 2 + 1, 4 * cb + dc - ec - LK // 2 + 1
                if 0 <= ky < 3 and 0 <= kx < 3:
                    tapmask[s * ATT:s * ATT + ATT, t * 8 + slot(er, ec), 3 * ky + kx] = 1.0
    ch = np.arange(P) % C // 2
    groupavg = (ch[:, None] == ch[None, :]).astype(np.float32) / 4
    return {"tapmask": tapmask, "chmask": chmask, "slotmask": slotmask, "groupavg": groupavg}


def kernel(x, L0_conv_ds_w3, L0_conv_ds_b3, L0_conv_ds_w1, L0_conv_ds_b1, L0_conv_kg_w1, L0_conv_kg_b1,
           L0_conv_kg_w2, L0_conv_kg_b2, L0_conv_lk_filter, L0_conv_fus_w, L0_conv_fus_b, L0_conv_fin_w,
           L0_conv_fin_b, L1_conv_w3, L1_conv_b3, L1_conv_w5, L1_conv_b5, L1_conv_wr, L1_conv_br):
    import concourse.bacc as bacc
    from concourse.bass_utils import run_bass_kernel_spmd

    a = np.asarray
    arrays = {
        "x": a(x),
        "w3t": a(L0_conv_ds_w3).transpose(0, 2, 3, 4, 1).reshape(LEVELS, C, 9, C),
        "w1t": a(L0_conv_ds_w1).transpose(0, 2, 1),
        "w1": a(L0_conv_ds_w1),
        "b3": a(L0_conv_ds_b3), "b1": a(L0_conv_ds_b1),
        "kgw1t": a(L0_conv_kg_w1).T, "kgb1": a(L0_conv_kg_b1),
        "kgw2": a(L0_conv_kg_w2).reshape(ATT, 9, ATT // 2).transpose(2, 1, 0),
        "kgb2": a(L0_conv_kg_b2).reshape(ATT, 9),
        "lkt": a(L0_conv_lk_filter).transpose(1, 2, 3, 0),
        "fus": a(L0_conv_fus_w), "fusb": a(L0_conv_fus_b),
        "fint": a(L0_conv_fin_w).T, "finb": a(L0_conv_fin_b),
        "c3t": a(L1_conv_w3).transpose(1, 2, 3, 0), "c5t": a(L1_conv_w5).transpose(1, 2, 3, 0),
        "c3b": a(L1_conv_b3), "c5b": a(L1_conv_b5),
        "wr": a(L1_conv_wr)[:, :, 0, 0], "wrt": a(L1_conv_wr)[:, :, 0, 0].T, "br": a(L1_conv_br),
        **constants(),
    }
    nc = bacc.Bacc("TRN2", target_bir_lowering=False, num_devices=1)
    feeds, aps = {}, {}
    for name, v in arrays.items():
        v = np.ascontiguousarray(v)
        feeds["in_" + name] = v
        aps[name] = nc.dram_tensor("in_" + name, v.shape, mybir.dt.from_np(v.dtype), kind="ExternalInput").ap()
    out = nc.dram_tensor("out_0", (B, C, H, W), F32, kind="ExternalOutput").ap()
    conv_kernel(nc, **aps, out=out)
    r = run_bass_kernel_spmd(nc, [feeds], core_ids=[0])
    return r.results[0]["out_0"]
```
